# Optimizing a Trainium2 kernel written in Bass

```python
import numpy as np
import jax
import jax.numpy as jnp

def _softmax(x, axis=-1):
    return jax.nn.softmax(x, axis=axis)

def _gelu(x):
    return jax.nn.gelu(x, approximate=True)

def _silu(x):
    return jax.nn.silu(x)

def _sigmoid(x):
    return jax.nn.sigmoid(x)

def _layernorm(x, axis=-1, eps=1e-05):
    m = jnp.mean(x, axis=axis, keepdims=True)
    v = jnp.var(x, axis=axis, keepdims=True)
    return (x - m) / jnp.sqrt(v + eps)

def _scatter_add(tgt, idx, src, axis=0):
    return tgt.at[idx].add(src)

def _segment_sum(src, seg, n):
    return jax.ops.segment_sum(src, seg, n)
kernel_name = 'mk_lm_tower_d2_tok_ids512_r4_9d9d85'

def setup_inputs(seed: int=0):
    np.random.seed(seed)
    _w = jnp.asarray

    def _rec_inputs():
        import jax
        import jax.numpy as jnp
        _rk = jax.random.key(seed)
        x = jax.random.randint(jax.random.fold_in(_rk, 1), (8, 256), 0, 31983, jnp.int32)
        return x
    x = _rec_inputs()

    def _L0_tok_setup():
        import math
        import jax, jax.numpy as jnp
        import numpy as np
        V, D, N, H, DFF = (8000, 128, 4, 8, 512)
        DK = D // H
        B, S = (2, 512)
        EPS = 1e-05

        def _pos_encoding(seq_len, d_model):
            pos = jnp.arange(seq_len, dtype=jnp.float32)[:, None]
            div = jnp.exp(jnp.arange(0, d_model, 2, dtype=jnp.float32) * (-math.log(10000.0) / d_model))
            ang = pos * div
            pe = jnp.zeros((seq_len, d_model), jnp.float32)
            pe = pe.at[:, 0::2].set(jnp.sin(ang)).at[:, 1::2].set(jnp.cos(ang))
            return pe

        def _layernorm(x, g, b):
            m = jnp.mean(x, axis=-1, keepdims=True)
            v = jnp.mean((x - m) ** 2, axis=-1, keepdims=True)
            return (x - m) / jnp.sqrt(v + EPS) * g + b
        key = jax.random.key(seed)
        ks = jax.random.split(key, 8)
        s = 0.02
        d = {}
        d['src'] = jax.random.randint(ks[0], (B, S), 0, V)
        d['embed'] = jax.random.normal(ks[1], (V, D), jnp.float32) * s
        d['Wq'] = jax.random.normal(ks[2], (N, D, D), jnp.float32) * s
        d['Wk'] = jax.random.normal(ks[3], (N, D, D), jnp.float32) * s
        d['Wv'] = jax.random.normal(ks[4], (N, D, D), jnp.float32) * s
        d['Wo'] = jax.random.normal(ks[5], (N, D, D), jnp.float32) * s
        d['W1'] = jax.random.normal(ks[6], (N, D, DFF), jnp.float32) * s
        d['W2'] = jax.random.normal(ks[7], (N, DFF, D), jnp.float32) * s
        for name, shape in (('bq', (N, D)), ('bk', (N, D)), ('bv', (N, D)), ('bo', (N, D)), ('b1', (N, DFF)), ('b2', (N, D)), ('be1', (N, D)), ('be2', (N, D)), ('bf', (D,))):
            d[name] = jnp.zeros(shape, jnp.float32)
        for name, shape in (('g1', (N, D)), ('g2', (N, D)), ('gf', (D,))):
            d[name] = jnp.ones(shape, jnp.float32)
        return d
    _L0_tok_all = _L0_tok_setup()
    _L0_tok_in = {k: v for k, v in _L0_tok_all.items() if k in ('embed', 'Wq', 'bq', 'Wk', 'bk', 'Wv', 'bv', 'Wo', 'bo', 'W1', 'b1', 'W2', 'b2', 'g1', 'be1', 'g2', 'be2', 'gf', 'bf')}
    del _L0_tok_all

    def _L0_attn_setup():
        import jax, jax.numpy as jnp
        import numpy as np
        DIM = 128
        HEADS = 1
        DIM_HEAD = DIM // 8
        M = DIM // 2
        ITERS = 6
        SCALE = DIM_HEAD ** (-0.5)
        KSIZE = 33
        EPS_LN = 1e-05

        def _moore_penrose_pinv(x, iters=ITERS):
            abs_x = jnp.abs(x)
            col = abs_x.sum(-1)
            row = abs_x.sum(-2)
            z = jnp.swapaxes(x, -1, -2) / (jnp.max(col) * jnp.max(row))
            I = jnp.eye(x.shape[-1], dtype=x.dtype)
            for _ in range(iters):
                xz = x @ z
                z = 0.25 * z @ (13.0 * I - xz @ (15.0 * I - xz @ (7.0 * I - xz)))
            return z

        def _reference_tuple_inner(x, norm_gamma, norm_beta, w_qkv, w_out, b_out, w_conv):
            B, N, _ = x.shape
            mu = x.mean(-1, keepdims=True)
            var = x.var(-1, keepdims=True)
            xn = (x - mu) / jnp.sqrt(var + EPS_LN) * norm_gamma + norm_beta
            qkv = xn @ w_qkv
            q, k, v = jnp.split(qkv, 3, axis=-1)
            resh = lambda t: t.reshape(B, N, HEADS, DIM_HEAD).transpose(0, 2, 1, 3)
            q, k, v = (resh(q), resh(k), resh(v))
            q = q * SCALE
            l = N // M
            q_l = q.reshape(B, HEADS, M, l, DIM_HEAD).sum(3) / l
            k_l = k.reshape(B, HEADS, M, l, DIM_HEAD).sum(3) / l
            sim1 = jnp.einsum('bhnd,bhmd->bhnm', q, k_l)
            sim2 = jnp.einsum('bhid,bhjd->bhij', q_l, k_l)
            sim3 = jnp.einsum('bhmd,bhnd->bhmn', q_l, k)
            a1 = jax.nn.softmax(sim1, axis=-1)
            a2 = jax.nn.softmax(sim2, axis=-1)
            a3 = jax.nn.softmax(sim3, axis=-1)
            a2_inv = _moore_penrose_pinv(a2)
            left = a1 @ a2_inv
            out = left @ (a3 @ v)
            res = jax.lax.conv_general_dilated(v, w_conv, window_strides=(1, 1), padding=((KSIZE // 2, KSIZE // 2), (0, 0)), dimension_numbers=('NCHW', 'OIHW', 'NCHW'), feature_group_count=HEADS)
            out = out + res
            out = out.transpose(0, 2, 1, 3).reshape(B, N, HEADS * DIM_HEAD)
            out = out @ w_out + b_out
            attn = left @ a3
            return (x + out, attn)
        key = jax.random.key(seed)
        ks = jax.random.split(key, 6)
        B, N = (4, 1024)
        return {'x': jax.random.normal(ks[0], (B, N, DIM), jnp.float32), 'norm_gamma': jnp.ones((DIM,), jnp.float32), 'norm_beta': jnp.zeros((DIM,), jnp.float32), 'w_qkv': jax.random.normal(ks[1], (DIM, 3 * HEADS * DIM_HEAD), jnp.float32) * 0.02, 'w_out': jax.random.normal(ks[2], (HEADS * DIM_HEAD, DIM), jnp.float32) * 0.02, 'b_out': jnp.zeros((DIM,), jnp.float32), 'w_conv': jax.random.normal(ks[3], (HEADS, 1, KSIZE, 1), jnp.float32) * 0.02}
    _L0_attn_all = _L0_attn_setup()
    _L0_attn_in = {k: v for k, v in _L0_attn_all.items() if k in ('norm_gamma', 'norm_beta', 'w_qkv', 'w_out', 'b_out', 'w_conv')}
    del _L0_attn_all

    def _L0_ffn_setup():
        import jax, jax.numpy as jnp
        import numpy as np
        D_MODEL = 128
        D_FF = 512
        N_EXPERTS = 8
        TOP_K = 2
        SEQ = 1024
        BATCH = 8
        FREQ_D = 2 * D_MODEL
        LN_EPS = 1e-05
        key = jax.random.key(seed)
        ks = jax.random.split(key, 12)
        s = 0.02
        return {'x': jax.random.normal(ks[0], (BATCH, SEQ, D_MODEL), dtype=jnp.float32), 'pin_w': jax.random.normal(ks[1], (FREQ_D, D_MODEL), dtype=jnp.float32) * s, 'pin_b': jax.random.normal(ks[2], (D_MODEL,), dtype=jnp.float32) * s, 'router_w': jax.random.normal(ks[3], (D_MODEL, N_EXPERTS), dtype=jnp.float32) * s, 'router_b': jax.random.normal(ks[4], (N_EXPERTS,), dtype=jnp.float32) * s, 'w1': jax.random.normal(ks[5], (N_EXPERTS, D_MODEL, D_FF), dtype=jnp.float32) * s, 'b1': jax.random.normal(ks[6], (N_EXPERTS, D_FF), dtype=jnp.float32) * s, 'w2': jax.random.normal(ks[7], (N_EXPERTS, D_FF, D_MODEL), dtype=jnp.float32) * s, 'b2': jax.random.normal(ks[8], (N_EXPERTS, D_MODEL), dtype=jnp.float32) * s, 'pout_w': jax.random.normal(ks[9], (D_MODEL, FREQ_D), dtype=jnp.float32) * s, 'pout_b': jax.random.normal(ks[10], (FREQ_D,), dtype=jnp.float32) * s, 'ln_g': jnp.ones((D_MODEL,), dtype=jnp.float32), 'ln_b': jnp.zeros((D_MODEL,), dtype=jnp.float32)}
    _L0_ffn_all = _L0_ffn_setup()
    _L0_ffn_in = {k: v for k, v in _L0_ffn_all.items() if k in ('pin_w', 'pin_b', 'router_w', 'router_b', 'w1', 'b1', 'w2', 'b2', 'pout_w', 'pout_b', 'ln_g', 'ln_b')}
    del _L0_ffn_all

    def _L1_attn_setup():
        import jax, jax.numpy as jnp
        import numpy as np
        import math
        D_MODEL = 128
        NUM_HEADS = 8
        B, S = (4, 256)
        key = jax.random.key(seed)
        ks = jax.random.split(key, 9)
        s = 1.0 / math.sqrt(D_MODEL)
        return {'x': jax.random.normal(ks[0], (B, S, D_MODEL), dtype=jnp.float32), 'Wq': jax.random.normal(ks[1], (NUM_HEADS, D_MODEL, D_MODEL), dtype=jnp.float32) * s, 'bq': jax.random.normal(ks[2], (NUM_HEADS, D_MODEL), dtype=jnp.float32) * s, 'Wk': jax.random.normal(ks[3], (NUM_HEADS, D_MODEL, D_MODEL), dtype=jnp.float32) * s, 'bk': jax.random.normal(ks[4], (NUM_HEADS, D_MODEL), dtype=jnp.float32) * s, 'Wv': jax.random.normal(ks[5], (NUM_HEADS, D_MODEL, D_MODEL), dtype=jnp.float32) * s, 'bv': jax.random.normal(ks[6], (NUM_HEADS, D_MODEL), dtype=jnp.float32) * s, 'Wo': jax.random.normal(ks[7], (NUM_HEADS * D_MODEL, D_MODEL), dtype=jnp.float32) * (1.0 / math.sqrt(NUM_HEADS * D_MODEL))}
    _L1_attn_all = _L1_attn_setup()
    _L1_attn_in = {k: v for k, v in _L1_attn_all.items() if k in ('Wq', 'bq', 'Wk', 'bk', 'Wv', 'bv', 'Wo')}
    del _L1_attn_all

    def _L1_ffn_setup():
        import jax, jax.numpy as jnp
        import numpy as np
        D_MODEL = 128
        N_HEADS = 8
        KV_OPTS = (8, 4, 1)
        D_K = D_MODEL // N_HEADS

        def gqa(x, wq, wk, wv, wo, n_kv):
            B, S, _ = x.shape
            groups = N_HEADS // n_kv
            q = (x @ wq).reshape(B, S, N_HEADS, D_K).transpose(0, 2, 1, 3)
            k = (x @ wk).reshape(B, S, n_kv, D_K).transpose(0, 2, 1, 3)
            v = (x @ wv).reshape(B, S, n_kv, D_K).transpose(0, 2, 1, 3)
            k = jnp.repeat(k, groups, axis=1)
            v = jnp.repeat(v, groups, axis=1)
            scores = jnp.einsum('bhqd,bhkd->bhqk', q, k) / jnp.sqrt(jnp.float32(D_K))
            attn = jax.nn.softmax(scores, axis=-1)
            out = jnp.einsum('bhqk,bhkd->bhqd', attn, v)
            out = out.transpose(0, 2, 1, 3).reshape(B, S, D_MODEL)
            return out @ wo
        key = jax.random.key(seed)
        ks = jax.random.split(key, 32)
        it = iter(ks)
        s = 0.02
        inp = {'x': jax.random.normal(next(it), (64, 256, D_MODEL), dtype=jnp.float32)}
        inp['r_w1'] = jax.random.normal(next(it), (D_MODEL, D_MODEL // 4), jnp.float32) * s
        inp['r_b1'] = jnp.zeros((D_MODEL // 4,), jnp.float32)
        inp['r_w2'] = jax.random.normal(next(it), (D_MODEL // 4, len(KV_OPTS)), jnp.float32) * s
        inp['r_b2'] = jnp.zeros((len(KV_OPTS),), jnp.float32)
        for i, nkv in enumerate(KV_OPTS):
            inp[f'wq{i}'] = jax.random.normal(next(it), (D_MODEL, D_MODEL), jnp.float32) * s
            inp[f'wk{i}'] = jax.random.normal(next(it), (D_MODEL, nkv * D_K), jnp.float32) * s
            inp[f'wv{i}'] = jax.random.normal(next(it), (D_MODEL, nkv * D_K), jnp.float32) * s
            inp[f'wo{i}'] = jax.random.normal(next(it), (D_MODEL, D_MODEL), jnp.float32) * s
        return inp
    _L1_ffn_all = _L1_ffn_setup()
    _L1_ffn_in = {k: v for k, v in _L1_ffn_all.items() if k in ('r_w1', 'r_b1', 'r_w2', 'r_b2', 'wq0', 'wk0', 'wv0', 'wo0', 'wq1', 'wk1', 'wv1', 'wo1', 'wq2', 'wk2', 'wv2', 'wo2')}
    del _L1_ffn_all
    return {'x': x, 'L0_tok_embed': _L0_tok_in['embed'], 'L0_tok_Wq': _L0_tok_in['Wq'], 'L0_tok_bq': _L0_tok_in['bq'], 'L0_tok_Wk': _L0_tok_in['Wk'], 'L0_tok_bk': _L0_tok_in['bk'], 'L0_tok_Wv': _L0_tok_in['Wv'], 'L0_tok_bv': _L0_tok_in['bv'], 'L0_tok_Wo': _L0_tok_in['Wo'], 'L0_tok_bo': _L0_tok_in['bo'], 'L0_tok_W1': _L0_tok_in['W1'], 'L0_tok_b1': _L0_tok_in['b1'], 'L0_tok_W2': _L0_tok_in['W2'], 'L0_tok_b2': _L0_tok_in['b2'], 'L0_tok_g1': _L0_tok_in['g1'], 'L0_tok_be1': _L0_tok_in['be1'], 'L0_tok_g2': _L0_tok_in['g2'], 'L0_tok_be2': _L0_tok_in['be2'], 'L0_tok_gf': _L0_tok_in['gf'], 'L0_tok_bf': _L0_tok_in['bf'], 'L0_attn_norm_gamma': _L0_attn_in['norm_gamma'], 'L0_attn_norm_beta': _L0_attn_in['norm_beta'], 'L0_attn_w_qkv': _L0_attn_in['w_qkv'], 'L0_attn_w_out': _L0_attn_in['w_out'], 'L0_attn_b_out': _L0_attn_in['b_out'], 'L0_attn_w_conv': _L0_attn_in['w_conv'], 'L0_ffn_pin_w': _L0_ffn_in['pin_w'], 'L0_ffn_pin_b': _L0_ffn_in['pin_b'], 'L0_ffn_router_w': _L0_ffn_in['router_w'], 'L0_ffn_router_b': _L0_ffn_in['router_b'], 'L0_ffn_w1': _L0_ffn_in['w1'], 'L0_ffn_b1': _L0_ffn_in['b1'], 'L0_ffn_w2': _L0_ffn_in['w2'], 'L0_ffn_b2': _L0_ffn_in['b2'], 'L0_ffn_pout_w': _L0_ffn_in['pout_w'], 'L0_ffn_pout_b': _L0_ffn_in['pout_b'], 'L0_ffn_ln_g': _L0_ffn_in['ln_g'], 'L0_ffn_ln_b': _L0_ffn_in['ln_b'], 'L1_attn_Wq': _L1_attn_in['Wq'], 'L1_attn_bq': _L1_attn_in['bq'], 'L1_attn_Wk': _L1_attn_in['Wk'], 'L1_attn_bk': _L1_attn_in['bk'], 'L1_attn_Wv': _L1_attn_in['Wv'], 'L1_attn_bv': _L1_attn_in['bv'], 'L1_attn_Wo': _L1_attn_in['Wo'], 'L1_ffn_r_w1': _L1_ffn_in['r_w1'], 'L1_ffn_r_b1': _L1_ffn_in['r_b1'], 'L1_ffn_r_w2': _L1_ffn_in['r_w2'], 'L1_ffn_r_b2': _L1_ffn_in['r_b2'], 'L1_ffn_wq0': _L1_ffn_in['wq0'], 'L1_ffn_wk0': _L1_ffn_in['wk0'], 'L1_ffn_wv0': _L1_ffn_in['wv0'], 'L1_ffn_wo0': _L1_ffn_in['wo0'], 'L1_ffn_wq1': _L1_ffn_in['wq1'], 'L1_ffn_wk1': _L1_ffn_in['wk1'], 'L1_ffn_wv1': _L1_ffn_in['wv1'], 'L1_ffn_wo1': _L1_ffn_in['wo1'], 'L1_ffn_wq2': _L1_ffn_in['wq2'], 'L1_ffn_wk2': _L1_ffn_in['wk2'], 'L1_ffn_wv2': _L1_ffn_in['wv2'], 'L1_ffn_wo2': _L1_ffn_in['wo2']}

def reference(x, L0_tok_embed, L0_tok_Wq, L0_tok_bq, L0_tok_Wk, L0_tok_bk, L0_tok_Wv, L0_tok_bv, L0_tok_Wo, L0_tok_bo, L0_tok_W1, L0_tok_b1, L0_tok_W2, L0_tok_b2, L0_tok_g1, L0_tok_be1, L0_tok_g2, L0_tok_be2, L0_tok_gf, L0_tok_bf, L0_attn_norm_gamma, L0_attn_norm_beta, L0_attn_w_qkv, L0_attn_w_out, L0_attn_b_out, L0_attn_w_conv, L0_ffn_pin_w, L0_ffn_pin_b, L0_ffn_router_w, L0_ffn_router_b, L0_ffn_w1, L0_ffn_b1, L0_ffn_w2, L0_ffn_b2, L0_ffn_pout_w, L0_ffn_pout_b, L0_ffn_ln_g, L0_ffn_ln_b, L1_attn_Wq, L1_attn_bq, L1_attn_Wk, L1_attn_bk, L1_attn_Wv, L1_attn_bv, L1_attn_Wo, L1_ffn_r_w1, L1_ffn_r_b1, L1_ffn_r_w2, L1_ffn_r_b2, L1_ffn_wq0, L1_ffn_wk0, L1_ffn_wv0, L1_ffn_wo0, L1_ffn_wq1, L1_ffn_wk1, L1_ffn_wv1, L1_ffn_wo1, L1_ffn_wq2, L1_ffn_wk2, L1_ffn_wv2, L1_ffn_wo2):
    import jax
    import jax.numpy as jnp

    def _L0_tok_ref(src, embed, Wq, bq, Wk, bk, Wv, bv, Wo, bo, W1, b1, W2, b2, g1, be1, g2, be2, gf, bf):
        import math
        import jax, jax.numpy as jnp
        import numpy as np
        V, D, N, H, DFF = (8000, 128, 4, 8, 512)
        DK = D // H
        B, S = (2, 512)
        EPS = 1e-05

        def _pos_encoding(seq_len, d_model):
            pos = jnp.arange(seq_len, dtype=jnp.float32)[:, None]
            div = jnp.exp(jnp.arange(0, d_model, 2, dtype=jnp.float32) * (-math.log(10000.0) / d_model))
            ang = pos * div
            pe = jnp.zeros((seq_len, d_model), jnp.float32)
            pe = pe.at[:, 0::2].set(jnp.sin(ang)).at[:, 1::2].set(jnp.cos(ang))
            return pe

        def _layernorm(x, g, b):
            m = jnp.mean(x, axis=-1, keepdims=True)
            v = jnp.mean((x - m) ** 2, axis=-1, keepdims=True)
            return (x - m) / jnp.sqrt(v + EPS) * g + b
        b, s = src.shape
        x = embed[src] + _pos_encoding(s, D)
        scale = 1.0 / math.sqrt(DK)
        for i in range(N):
            q = (x @ Wq[i] + bq[i]).reshape(b, s, H, DK).transpose(0, 2, 1, 3)
            k = (x @ Wk[i] + bk[i]).reshape(b, s, H, DK).transpose(0, 2, 1, 3)
            v = (x @ Wv[i] + bv[i]).reshape(b, s, H, DK).transpose(0, 2, 1, 3)
            scores = jnp.einsum('bhqd,bhkd->bhqk', q, k) * scale
            attn = jax.nn.softmax(scores, axis=-1)
            o = jnp.einsum('bhqk,bhkd->bhqd', attn, v)
            o = o.transpose(0, 2, 1, 3).reshape(b, s, D) @ Wo[i] + bo[i]
            x = _layernorm(x + o, g1[i], be1[i])
            f = jax.nn.relu(x @ W1[i] + b1[i]) @ W2[i] + b2[i]
            x = _layernorm(x + f, g2[i], be2[i])
        return _layernorm(x, gf, bf)

    def _L0_attn_ref(x, norm_gamma, norm_beta, w_qkv, w_out, b_out, w_conv):
        import jax, jax.numpy as jnp
        import numpy as np
        DIM = 128
        HEADS = 1
        DIM_HEAD = DIM // 8
        M = DIM // 2
        ITERS = 6
        SCALE = DIM_HEAD ** (-0.5)
        KSIZE = 33
        EPS_LN = 1e-05

        def _moore_penrose_pinv(x, iters=ITERS):
            abs_x = jnp.abs(x)
            col = abs_x.sum(-1)
            row = abs_x.sum(-2)
            z = jnp.swapaxes(x, -1, -2) / (jnp.max(col) * jnp.max(row))
            I = jnp.eye(x.shape[-1], dtype=x.dtype)
            for _ in range(iters):
                xz = x @ z
                z = 0.25 * z @ (13.0 * I - xz @ (15.0 * I - xz @ (7.0 * I - xz)))
            return z

        def _reference_tuple_inner(x, norm_gamma, norm_beta, w_qkv, w_out, b_out, w_conv):
            B, N, _ = x.shape
            mu = x.mean(-1, keepdims=True)
            var = x.var(-1, keepdims=True)
            xn = (x - mu) / jnp.sqrt(var + EPS_LN) * norm_gamma + norm_beta
            qkv = xn @ w_qkv
            q, k, v = jnp.split(qkv, 3, axis=-1)
            resh = lambda t: t.reshape(B, N, HEADS, DIM_HEAD).transpose(0, 2, 1, 3)
            q, k, v = (resh(q), resh(k), resh(v))
            q = q * SCALE
            l = N // M
            q_l = q.reshape(B, HEADS, M, l, DIM_HEAD).sum(3) / l
            k_l = k.reshape(B, HEADS, M, l, DIM_HEAD).sum(3) / l
            sim1 = jnp.einsum('bhnd,bhmd->bhnm', q, k_l)
            sim2 = jnp.einsum('bhid,bhjd->bhij', q_l, k_l)
            sim3 = jnp.einsum('bhmd,bhnd->bhmn', q_l, k)
            a1 = jax.nn.softmax(sim1, axis=-1)
            a2 = jax.nn.softmax(sim2, axis=-1)
            a3 = jax.nn.softmax(sim3, axis=-1)
            a2_inv = _moore_penrose_pinv(a2)
            left = a1 @ a2_inv
            out = left @ (a3 @ v)
            res = jax.lax.conv_general_dilated(v, w_conv, window_strides=(1, 1), padding=((KSIZE // 2, KSIZE // 2), (0, 0)), dimension_numbers=('NCHW', 'OIHW', 'NCHW'), feature_group_count=HEADS)
            out = out + res
            out = out.transpose(0, 2, 1, 3).reshape(B, N, HEADS * DIM_HEAD)
            out = out @ w_out + b_out
            attn = left @ a3
            return (x + out, attn)
        return _reference_tuple_inner(x, norm_gamma, norm_beta, w_qkv, w_out, b_out, w_conv)[0]

    def _L0_ffn_ref(x, pin_w, pin_b, router_w, router_b, w1, b1, w2, b2, pout_w, pout_b, ln_g, ln_b):
        import jax, jax.numpy as jnp
        import numpy as np
        D_MODEL = 128
        D_FF = 512
        N_EXPERTS = 8
        TOP_K = 2
        SEQ = 1024
        BATCH = 8
        FREQ_D = 2 * D_MODEL
        LN_EPS = 1e-05
        B, S, D = x.shape
        residual = x
        xf = jnp.fft.rfft(x, axis=1, norm='ortho')
        xf_ri = jnp.concatenate([xf.real, xf.imag], axis=-1)
        h = xf_ri @ pin_w + pin_b
        logits = h @ router_w + router_b
        topk_logits, topk_idx = jax.lax.top_k(logits, TOP_K)
        topk_w = jax.nn.softmax(topk_logits, axis=-1)
        hid = jax.nn.gelu(jnp.einsum('bfd,edh->befh', h, w1) + b1[None, :, None, :], approximate=False)
        all_out = jnp.einsum('befh,ehd->befd', hid, w2) + b2[None, :, None, :]
        all_out = jnp.swapaxes(all_out, 1, 2)
        sel = jnp.take_along_axis(all_out, topk_idx[..., None], axis=2)
        moe_out = jnp.sum(sel * topk_w[..., None], axis=2)
        of = moe_out @ pout_w + pout_b
        oc = jax.lax.complex(of[:, :, :D], of[:, :, D:])
        ot = jnp.fft.irfft(oc, n=S, axis=1, norm='ortho')
        mu = jnp.mean(ot, axis=-1, keepdims=True)
        var = jnp.mean(jnp.square(ot - mu), axis=-1, keepdims=True)
        ot = (ot - mu) * jax.lax.rsqrt(var + LN_EPS) * ln_g + ln_b
        return ot + residual

    def _L1_attn_ref(x, Wq, bq, Wk, bk, Wv, bv, Wo):
        import jax, jax.numpy as jnp
        import numpy as np
        import math
        D_MODEL = 128
        NUM_HEADS = 8
        B, S = (4, 256)
        q = jnp.einsum('bsd,hde->bhse', x, Wq) + bq[None, :, None, :]
        k = jnp.einsum('bsd,hde->bhse', x, Wk) + bk[None, :, None, :]
        v = jnp.einsum('bsd,hde->bhse', x, Wv) + bv[None, :, None, :]
        scores = jnp.einsum('bhqe,bhke->bhqk', q, k) / math.sqrt(D_MODEL)
        attn = jax.nn.softmax(scores, axis=-1)
        heads = jnp.einsum('bhqk,bhke->bhqe', attn, v)
        concat = heads.transpose(0, 2, 1, 3).reshape(heads.shape[0], heads.shape[2], -1)
        return concat @ Wo

    def _L1_ffn_ref(x, r_w1, r_b1, r_w2, r_b2, wq0, wk0, wv0, wo0, wq1, wk1, wv1, wo1, wq2, wk2, wv2, wo2):
        import jax, jax.numpy as jnp
        import numpy as np
        D_MODEL = 128
        N_HEADS = 8
        KV_OPTS = (8, 4, 1)
        D_K = D_MODEL // N_HEADS

        def gqa(x, wq, wk, wv, wo, n_kv):
            B, S, _ = x.shape
            groups = N_HEADS // n_kv
            q = (x @ wq).reshape(B, S, N_HEADS, D_K).transpose(0, 2, 1, 3)
            k = (x @ wk).reshape(B, S, n_kv, D_K).transpose(0, 2, 1, 3)
            v = (x @ wv).reshape(B, S, n_kv, D_K).transpose(0, 2, 1, 3)
            k = jnp.repeat(k, groups, axis=1)
            v = jnp.repeat(v, groups, axis=1)
            scores = jnp.einsum('bhqd,bhkd->bhqk', q, k) / jnp.sqrt(jnp.float32(D_K))
            attn = jax.nn.softmax(scores, axis=-1)
            out = jnp.einsum('bhqk,bhkd->bhqd', attn, v)
            out = out.transpose(0, 2, 1, 3).reshape(B, S, D_MODEL)
            return out @ wo
        routing_input = x.mean(axis=1)
        logits = jax.nn.relu(routing_input @ r_w1 + r_b1) @ r_w2 + r_b2
        sel = jnp.argmax(jax.nn.softmax(logits, axis=-1), axis=-1)
        params = [(wq0, wk0, wv0, wo0), (wq1, wk1, wv1, wo1), (wq2, wk2, wv2, wo2)]
        out = jnp.zeros_like(x)
        for i, nkv in enumerate(KV_OPTS):
            yi = gqa(x, *params[i], nkv)
            mask = (sel == i)[:, None, None]
            out = jnp.where(mask, yi, out)
        return out
    h = _L0_tok_ref(x, L0_tok_embed, L0_tok_Wq, L0_tok_bq, L0_tok_Wk, L0_tok_bk, L0_tok_Wv, L0_tok_bv, L0_tok_Wo, L0_tok_bo, L0_tok_W1, L0_tok_b1, L0_tok_W2, L0_tok_b2, L0_tok_g1, L0_tok_be1, L0_tok_g2, L0_tok_be2, L0_tok_gf, L0_tok_bf)
    h = h + _L0_attn_ref(_layernorm(h, axis=-1), L0_attn_norm_gamma, L0_attn_norm_beta, L0_attn_w_qkv, L0_attn_w_out, L0_attn_b_out, L0_attn_w_conv)
    h = h + _L0_ffn_ref(_layernorm(h, axis=-1), L0_ffn_pin_w, L0_ffn_pin_b, L0_ffn_router_w, L0_ffn_router_b, L0_ffn_w1, L0_ffn_b1, L0_ffn_w2, L0_ffn_b2, L0_ffn_pout_w, L0_ffn_pout_b, L0_ffn_ln_g, L0_ffn_ln_b)
    h = h + _L1_attn_ref(_layernorm(h, axis=-1), L1_attn_Wq, L1_attn_bq, L1_attn_Wk, L1_attn_bk, L1_attn_Wv, L1_attn_bv, L1_attn_Wo)
    h = h + _L1_ffn_ref(_layernorm(h, axis=-1), L1_ffn_r_w1, L1_ffn_r_b1, L1_ffn_r_w2, L1_ffn_r_b2, L1_ffn_wq0, L1_ffn_wk0, L1_ffn_wv0, L1_ffn_wo0, L1_ffn_wq1, L1_ffn_wk1, L1_ffn_wv1, L1_ffn_wo1, L1_ffn_wq2, L1_ffn_wk2, L1_ffn_wv2, L1_ffn_wo2)
    return h

_drawn_inputs = setup_inputs


def setup_inputs(seed=0):
    import zlib

    import numpy as np

    out = dict(_drawn_inputs(seed))
    spreads = {'L0_tok_bq': (0.0, 0.8),
     'L0_tok_bk': (0.0, 0.8),
     'L0_tok_bv': (0.0, 0.1),
     'L0_tok_bo': (0.0, 0.1),
     'L0_tok_b1': (0.0, 0.1),
     'L0_tok_b2': (0.0, 0.1),
     'L0_tok_g1': (1.0, 0.2),
     'L0_tok_be1': (0.0, 0.1),
     'L0_tok_g2': (1.0, 0.2),
     'L0_tok_be2': (0.0, 0.1),
     'L0_tok_gf': (1.0, 0.2),
     'L0_tok_bf': (0.0, 0.1),
     'L0_attn_norm_gamma': (1.0, 0.6),
     'L0_attn_norm_beta': (0.0, 0.8),
     'L0_attn_b_out': (0.0, 0.1),
     'L0_ffn_ln_g': (1.0, 0.2),
     'L0_ffn_ln_b': (0.0, 0.275),
     'L1_ffn_r_b1': (0.0, 0.1),
     'L1_ffn_r_b2': (0.0, 0.1)}
    factors = {'L0_tok_Wq': 8.0,
     'L0_tok_Wk': 8.0,
     'L0_attn_w_qkv': 8.0,
     'L0_attn_w_out': 8.0,
     'L0_attn_w_conv': 8.0,
     'L1_attn_bq': 8.0,
     'L1_attn_bk': 8.0,
     'L1_ffn_wq1': 8.0,
     'L1_ffn_wk1': 8.0,
     'L1_ffn_wv1': 5.109,
     'L1_ffn_wo1': 5.329}
    for name, (base, spread) in spreads.items():
        noise = np.random.default_rng([zlib.crc32(name.encode()), seed]).standard_normal(out[name].shape)
        drawn = base * np.exp(spread * noise) if base else spread * noise
        out[name] = jnp.asarray(drawn.astype(out[name].dtype))
    for name, factor in factors.items():
        out[name] = (out[name] * factor).astype(out[name].dtype)
    return out
```

```python
from contextlib import ExitStack

import concourse.bass as bass
from concourse import mybir



class Names:
    pass


F32 = mybir.dt.float32
BF16 = mybir.dt.bfloat16
I32 = mybir.dt.int32
ACT = mybir.ActivationFunctionType
ALU = mybir.AluOpType
AX = mybir.AxisListType

P = 128
B, S, D = 8, 256, 128
TOK = B * S
TILES = TOK // P
PAIRS = B // 2
PW = 2 * S
H, DK = 8, 16
SLOT = 32
EPS = 1e-5
LAYERS = 4
VOCAB = 8000
QPARTS = (0, 0, 0, 1, 1, 2)
KPARTS = (0, 1, 2, 0, 1, 0)
NG = len(QPARTS)
MROW = NG * DK


class Link:

    def __init__(self, eng, sem):
        self.eng, self.sem, self.n = eng, sem, 0

    def mark(self, ins):
        ins.then_inc(self.sem, 1)
        self.n += 1
        return self.n

    def wait(self, n=None):
        self.eng.wait_ge(self.sem, self.n if n is None else n)

    def step(self, ins):
        self.mark(ins)
        self.wait()


def bank_turns(order, uses):
    turns, n = {}, 0
    for item in order:
        for key in uses(item):
            turns[key] = (n % 2, n // 2)
            n += 1
    return turns


def layer_order(ffn):
    order = [("A", 0), ("A", 1)]
    order += [("M", 0, u) for u in range(8)] + [("MT", 0)]
    order += [("M", 1, u) for u in range(8)]
    for b in range(B + 3):
        extra = {u: [] for u in range(8)}
        if b % 2 == 0 and b // 2 + 2 < PAIRS:
            extra[0].append(("A", b // 2 + 2))
        if b + 1 < B:
            extra[1].append(("MT", b + 1))
        if 1 <= b <= B:
            extra[2].append(("T1", b - 1))
            extra[4].append(("T2", b - 1))
        g = b // 2 - 1
        if b % 2 == 0 and 0 <= g < PAIRS:
            extra[6].append(("C1", g))
            if g >= 1 and ffn:
                extra[3].append(("C5", g - 1))
        if ffn and b % 2 == 1 and 0 <= (b - 3) // 2 < PAIRS and b >= 3:
            g = (b - 3) // 2
            extra[3].append(("C2", g))
            extra[5].append(("C3", g))
            extra[7].append(("C4", g))
        if b < B:
            for u in range(8):
                order.append(("S", b, u))
                if b + 2 < B:
                    order.append(("M", b + 2, u))
                if u % 2 == 1 and u >= 3:
                    order.append(("AV", b, u // 2 - 1))
                order += extra[u]
            order += [("AV", b, 3), ("O", b)]
        else:
            for u in range(8):
                order += extra[u]
    if ffn:
        order.append(("C5", PAIRS - 1))
    return order


def bank_uses(item):
    kind, at = item[0], item[1]
    if kind == "A":
        return [("Aq", at), ("Ak", at), ("Av", at)]
    if kind == "C3":
        return [("C3", at, m) for m in range(4)]
    if kind in ("MT", "T1", "T2", "C1", "C2", "C4", "C5"):
        return [(kind, at)]
    return []


def emit_layer(nc, m, w, sems, ffn, out_dram=None):
    order = layer_order(ffn)
    turn = bank_turns(order, bank_uses)
    at_turn = {v: k for k, v in turn.items()}
    norms = [(kind, at) for kind, at in ((x[0], x[1]) for x in order) if kind in ("C1", "C4")]
    ln_index = {key: n for n, key in enumerate(norms)}
    turned = {"C1": "C2", "C4": "C5"}
    halves = [(0, PW, 0)] if ffn else [(0, S, 0), (S, S, 1)]
    sem = sems

    def lin(key):
        return m.lin[turn[key][0]]

    def bank_ready(eng, key):
        bank, n = turn[key]
        eng.wait_ge(sem["lin_ready"][bank], n + 1)

    def read_out(key):
        kind, at = key[0], key[1]
        if kind == "Aq":
            return sem["q_ready"], 4 * at + 2
        if kind == "Ak":
            return sem["q_ready"], 4 * at + 4
        if kind == "C3":
            return (sem["hid_dve"] if key[2] % 2 else sem["hid_act"]), 2 * at + key[2] // 2 + 1
        if kind in ("C1", "C4") and ffn:
            return sem["sum_ready"], ln_index[(kind, at)] + 1
        return {"Av": sem["v_ready"], "MT": sem["mrow_sb"], "T1": sem["otok_ready"], "T2": sem["oT_ready"], "C1": sem["out_ready"],
                "C2": sem["x1T_ready"], "C5": sem["xT_ready"]}[kind], at + 1

    def bank_free(eng, key):
        bank, n = turn[key]
        if n:
            eng.wait_ge(*read_out(at_turn[(bank, n - 1)]))

    with nc.Block() as block:

        @block.sync
        def _(sp):
            if ffn:
                w.load(sp, sem)
            stored = [0]

            def pack(g, t):
                sp.wait_ge(sem["split_done"], 2 * g + t + 1)
                sp.dma_start(m.scratch[t, :, :, g * PW:(g + 1) * PW].rearrange("a p n -> p a n"),
                             m.parts[:, t, g % 2]).then_inc(sem["parts_stored"], 16)
                stored[0] += 16
                sp.wait_ge(sem["parts_stored"], stored[0])
                if g >= 3 and t == 0:
                    sp.wait_ge(sem["av_done"], 4 * (2 * (g - 3) + 2))
                for i, part in enumerate(KPARTS if t else QPARTS):
                    sp.dma_start(m.packed[i * DK:(i + 1) * DK, t, g % 3],
                                 m.scratch[t, part, :, g * PW:(g + 1) * PW].rearrange("(h d) n -> d h n", h=H)
                                 ).then_inc(sem["packed"][g % 3], 16)

            for item in order:
                kind, at = item[0], item[1]
                if kind == "A":
                    pack(at, 0)
                    pack(at, 1)
                elif kind == "MT":
                    b = at
                    sp.wait_ge(sem["mrow_sb"], b + 1)
                    sp.dma_start(m.max_scratch[b % 2].rearrange("a h n -> (a h) n"), m.mT[0:3 * H, b % 2, :]
                                 ).then_inc(sem["mstored"], 16)
                    sp.wait_ge(sem["mstored"], 16 * (b + 1))
                    sp.dma_start(m.packed[MROW:MROW + 3, 0, (b // 2) % 3, :, (b % 2) * S:(b % 2 + 1) * S],
                                 m.max_scratch[b % 2]).then_inc(sem["mrow"][b % 2], 16)
                elif kind == "C1" and not ffn:
                    sp.wait_ge(sem["out_ready"], at + 1)
                    sp.dma_start(out_dram[at], m.rbuf[:, at % 2]).then_inc(sem["stored"][at % 2], 16)
            if not ffn:
                for i in range(2):
                    sp.wait_ge(sem["stored"][i], 16 * (PAIRS // 2))

        @block.tensor
        def _(pe):
            def use(key):
                bank_free(pe, key)
                return lin(key)

            def filled(key, ins):
                ins.then_inc(sem["lin_ready"][turn[key][0]], 1)

            for item in order:
                kind, at = item[0], item[1]
                if kind == "A":
                    g = at
                    if g == 0 and ffn:
                        pe.wait_ge(sem["w_proj"], 16)
                    for key, wt in ((("Aq", g), w.q), (("Ak", g), w.k)):
                        bank = use(key)
                        for c0, cn, hb in halves:
                            ins = pe.matmul(bank[:, c0:c0 + cn], wt(2 * g + hb),
                                            m.xT[:, g * PW + c0:g * PW + c0 + cn], start=True, stop=True)
                        filled(key, ins)
                    bank = use(("Av", g))
                    for i in range(4):
                        ins = pe.matmul(bank[:, i * P:(i + 1) * P], m.xT[:, g * PW + i * P:g * PW + (i + 1) * P],
                                        w.v(2 * g + i // 2), start=True, stop=True)
                    filled(("Av", g), ins)
                elif kind == "M":
                    b, u = at, item[2]
                    g, n, qt = b // 2, 8 * b + u, u // 4
                    c = (b % 2) * S
                    if u == 0:
                        pe.wait_ge(sem["packed"][g % 3], 16 * 2 * NG * (g // 3 + 1))
                    if n >= 2:
                        pe.wait_ge(sem["max_taken"], n - 1)
                    for i in range(2):
                        h = 2 * (u % 4) + i
                        ins = pe.matmul(m.mbank[:, n % 2, i * S:(i + 1) * S],
                                        m.packed[0:MROW, 0, g % 3, h, c + qt * P:c + (qt + 1) * P],
                                        m.packed[0:MROW, 1, g % 3, h, c:c + S], start=True, stop=True)
                    ins.then_inc(sem["max_scores"], 1)
                elif kind == "MT":
                    key = ("MT", at)
                    bank = use(key).bitcast(BF16)
                    pe.wait_ge(sem["mparts_done"], at + 1)
                    for qt in range(2):
                        ins = pe.transpose(bank[0:3 * H, qt * P:(qt + 1) * P], m.mparts[:, at % 2, qt, :],
                                           m.identb[:, :])
                    filled(key, ins)
                elif kind == "S":
                    b, u = at, item[2]
                    g, n = b // 2, 8 * b + u
                    hq, kt, hp = u // 4, (u // 2) % 2, u % 2
                    c = (b % 2) * S
                    if u == 0:
                        pe.wait_ge(sem["mrow"][b % 2], 16 * (b // 2 + 1))
                    if n >= 3:
                        pe.wait_ge(sem["probs_ready"], n - 2)
                    for i in range(2):
                        h = 4 * hq + 2 * hp + i
                        ins = pe.matmul(m.sbank[:, n % 3, i * S:(i + 1) * S],
                                        m.packed[0:MROW + 3, 1, g % 3, h, c + kt * P:c + (kt + 1) * P],
                                        m.packed[0:MROW + 3, 0, g % 3, h, c:c + S], start=True, stop=True)
                    ins.then_inc(sem["scores_ready"], 1)
                elif kind == "AV":
                    b, j = at, item[2]
                    hq, kt = j // 2, j % 2
                    n = 8 * b + 2 * j
                    pe.wait_ge(sem["probs_ready"], n + 2)
                    if j == 0:
                        pe.wait_ge(sem["v_ready"], b // 2 + 1)
                        if b:
                            pe.wait_ge(sem["o_copied"], b)
                    for i in range(4):
                        ins = pe.matmul(m.obank[SLOT * i:SLOT * (i + 1), hq * S:(hq + 1) * S],
                                        m.v[:, 2 * b + kt, 4 * hq + i, :],
                                        m.probs[:, (n + i // 2) % 6, (i % 2) * S:(i % 2 + 1) * S],
                                        start=(kt == 0), stop=(kt == 1))
                    ins.then_inc(sem["av_done"], 1)
                elif kind == "T1":
                    key = ("T1", at)
                    bank = use(key)
                    pe.wait_ge(sem["o_copied"], at + 1)
                    for qt in range(2):
                        for hq in range(2):
                            c = (2 * qt + hq) * P
                            ins = pe.transpose(bank[:, c:c + P], m.osb[:, at % 2, hq * S + qt * P:hq * S + (qt + 1) * P],
                                               m.ident[:, :])
                    filled(key, ins)
                elif kind == "T2":
                    key = ("T2", at)
                    bank = use(key)
                    pe.wait_ge(sem["otok_ready"], at + 1)
                    for qt in range(2):
                        ins = pe.transpose(bank[:, qt * P:(qt + 1) * P], m.otok[:, at % 2, qt, :], m.ident[:, :])
                    filled(key, ins)
                elif kind == "C1":
                    key = ("C1", at)
                    bank = use(key)
                    pe.wait_ge(sem["oT_ready"], 2 * at + 2)
                    if at == 0 and ffn:
                        pe.wait_ge(sem["w_rest"], 16 * 3)
                    for i in range(4):
                        ins = pe.matmul(bank[:, i * P:(i + 1) * P], m.oT[:, at % 2, i * P:(i + 1) * P],
                                        w.o(2 * at + i // 2), start=True, stop=True)
                    filled(key, ins)
                elif kind in ("C2", "C5"):
                    n = ln_index[("C1" if kind == "C2" else "C4", at)]
                    key = (kind, at)
                    bank = use(key)
                    pe.wait_ge(sem["xhat_ready"], n + 1)
                    for i in range(4):
                        ins = pe.transpose(bank[:, i * P:(i + 1) * P], m.xhat[:, n % 2, i, :], m.ident[:, :])
                    filled(key, ins)
                elif kind == "C3":
                    pe.wait_ge(sem["x1T_ready"], at + 1)
                    for c in range(4):
                        key = ("C3", at, c)
                        bank = use(key)
                        filled(key, pe.matmul(bank[:, :], w.w1[:, c * P:(c + 1) * P], m.x1T[:, at % 2, :],
                                              start=True, stop=True))
                elif kind == "C4":
                    key = ("C4", at)
                    bank = use(key)
                    pe.wait_ge(sem["hid_act"], 2 * at + 2)
                    pe.wait_ge(sem["hid_dve"], 2 * at + 2)
                    for i in range(4):
                        for c in range(4):
                            ins = pe.matmul(bank[:, i * P:(i + 1) * P], m.hidden[:, c, i * P:(i + 1) * P], w.w2[:, c, :],
                                            start=(c == 0), stop=(c == 3))
                    filled(key, ins)

        @block.scalar
        def _(act):
            chain = Link(act, sem["act_chain"])

            if ffn:
                act.wait_ge(sem["w_vec"], 16)
                chain.step(act.mul(m.bq4[:, :], w.bq, DK ** -0.5))
            for item in order:
                kind, at = item[0], item[1]
                if kind == "A":
                    g = at
                    for t, key in enumerate((("Aq", g), ("Ak", g))):
                        bank_ready(act, key)
                        if g >= 2:
                            act.wait_ge(sem["split_done"], 2 * (g - 2) + t + 1)
                            act.wait_ge(sem["parts_stored"], 16 * (2 * (g - 2) + t + 1))
                        scale = DK ** -0.5 if t == 0 else 1.0
                        bias = (m.bq4[:, 0:1] if t == 0 else w.bk) if ffn else 0.0
                        fn = ACT.Identity if ffn else ACT.Copy
                        act.activation(m.qf[:, t, g % 2], lin(key)[:, :], fn, bias=bias, scale=scale
                                       ).then_inc(sem["q_ready"], 1)
                        ins = act.activation(m.parts[:, t, g % 2, 0], lin(key)[:, :], fn, bias=bias, scale=scale)
                        ins.then_inc(sem["q_ready"], 1)
                elif kind == "MT":
                    key = ("MT", at)
                    bank_ready(act, key)
                    if at >= 2:
                        act.wait_ge(sem["mstored"], 16 * (at - 1))
                    act.activation(m.mT[0:3 * H, at % 2, :], lin(key).bitcast(BF16)[0:3 * H, 0:S], ACT.Copy
                                   ).then_inc(sem["mrow_sb"], 1)
                elif kind == "S":
                    n = 8 * at + item[2]
                    act.wait_ge(sem["scores_ready"], n + 1)
                    if n >= 6:
                        act.wait_ge(sem["av_done"], (n - 6) // 2 + 1)
                    act.activation(m.probs[:, n % 6, :], m.sbank[:, n % 3, :], ACT.Exp).then_inc(sem["probs_ready"], 1)
                elif kind == "O":
                    act.wait_ge(sem["av_done"], 4 * at + 4)
                    if at >= 2:
                        bank_ready(act, ("T1", at - 2))
                    act.activation(m.osb[:, at % 2, :], m.obank[:, :], ACT.Copy).then_inc(sem["o_copied"], 1)
                elif kind == "T2":
                    key = ("T2", at)
                    bank_ready(act, key)
                    if at >= 4 and at % 2 == 0:
                        bank_ready(act, ("C1", at // 2 - 2))
                    act.activation(m.oT[:, (at // 2) % 2, (at % 2) * S:(at % 2 + 1) * S], lin(key)[:, 0:S], ACT.Copy
                                   ).then_inc(sem["oT_ready"], 1)
                elif kind == "C2":
                    key = ("C2", at)
                    bank_ready(act, key)
                    if at >= 2:
                        bank_ready(act, ("C3", at - 2, 3))
                    act.activation(m.x1T[:, at % 2, :], lin(key)[:, :], ACT.Identity, bias=w.be1, scale=w.g1
                                   ).then_inc(sem["x1T_ready"], 1)
                elif kind == "C3":
                    for c in (0, 2):
                        key = ("C3", at, c)
                        bank_ready(act, key)
                        if at >= 1:
                            bank_ready(act, ("C4", at - 1))
                        act.activation(m.hidden[:, c, :], lin(key)[:, :], ACT.Relu, bias=w.b1[:, c:c + 1]
                                       ).then_inc(sem["hid_act"], 1)
                elif kind == "C5":
                    key = ("C5", at)
                    bank_ready(act, key)
                    bank_ready(act, ("Av", at))
                    act.activation(m.xT[:, at * PW:(at + 1) * PW], lin(key)[:, :], ACT.Identity, bias=w.be2, scale=w.g2
                                   ).then_inc(sem["xT_ready"], 1)

        @block.vector
        def _(dve):
            chain = Link(dve, sem["dve_chain"])

            def norm(key, n):
                g = key[1]
                bank_ready(dve, key)
                dve.wait_ge(sem["res"][key[0]], g + 1)
                if n >= 2:
                    kind, at = norms[n - 2]
                    bank_ready(dve, (turned[kind], at))
                    dve.wait_ge(sem["res_out"][kind], at + 1)
                r = m.rbuf[:, n % 2].rearrange("p a d -> p (a d)")
                dve.tensor_tensor(r, lin(key)[:, :], m.R[:, 4 * g:4 * g + 4, :].rearrange("p a d -> p (a d)"),
                                  ALU.add).then_inc(sem["sum_ready"], 1)
                dve.wait_ge(sem["sum_ready"], n + 1)
                for i in range(4):
                    ins = dve.bn_stats(m.stats[:, i, :], m.rbuf[:, n % 2, i, :])
                chain.step(ins)
                for i in range(4):
                    ins = dve.bn_aggr(m.mv[:, n % 2, i, :], m.stats[:, i, :])
                ins.then_inc(sem["stats_ready"], 1)
                dve.wait_ge(sem["rstd_ready"], n + 1)
                for i in range(4):
                    ins = dve.tensor_scalar(m.xhat[:, n % 2, i, :], m.rbuf[:, n % 2, i, :], m.mv[:, n % 2, i, 0:1],
                                            m.rstd[:, n % 2, i:i + 1], ALU.subtract, ALU.mult)
                ins.then_inc(sem["xhat_ready"], 1)

            if ffn:
                dve.wait_ge(sem["w_vec"], 16)
                dve.wait_ge(sem["w_bc"], 16)
            for item in order:
                kind, at = item[0], item[1]
                if kind == "A":
                    key = ("Av", at)
                    bank_ready(dve, key)
                    out = m.v[:, 4 * at:4 * at + 4, :, 0:DK]
                    src = lin(key)[:, :].rearrange("p (a h d) -> p a h d", a=4, h=H)
                    if ffn:
                        for i in range(4):
                            ins = dve.tensor_tensor(out[:, i], src[:, i], w.bv_bc.rearrange("p (h d) -> p h d", h=H), ALU.add)
                    else:
                        for i in range(4):
                            ins = dve.tensor_copy(out[:, i], src[:, i])
                    ins.then_inc(sem["v_ready"], 1)
                elif kind == "M":
                    b, u = at, item[2]
                    n = 8 * b + u
                    dve.wait_ge(sem["max_scores"], n + 1)
                    hp = u % 4
                    dve.tensor_reduce(m.nmax[:, b % 2, u // 4, 2 * hp:2 * hp + 2],
                                      m.mbank[:, n % 2, :].rearrange("p (i k) -> p i k", i=2),
                                      AX.X, ALU.max, negate=True).then_inc(sem["max_taken"], 1)
                    if u == 7:
                        nm, mp = m.nmax[:, b % 2], m.mparts[:, b % 2]
                        dve.wait_ge(sem["max_taken"], n + 1)
                        if b >= 2:
                            bank_ready(dve, ("MT", b - 2))
                        chain.step(dve.tensor_copy(mp[:, :, 0:H], nm))
                        chain.step(dve.tensor_tensor(nm, nm, mp[:, :, 0:H], ALU.subtract))
                        chain.step(dve.tensor_copy(mp[:, :, H:2 * H], nm))
                        dve.tensor_tensor(mp[:, :, 2 * H:3 * H], nm, mp[:, :, H:2 * H], ALU.subtract
                                          ).then_inc(sem["mparts_done"], 1)
                elif kind == "T1":
                    key = ("T1", at)
                    bank_ready(dve, key)
                    src = lin(key)[:, :].rearrange("p (a c) -> p a c", c=SLOT)
                    chain.step(dve.reciprocal(m.recip[:, at % 2], src[:, :, DK]))
                    if at >= 2:
                        bank_ready(dve, ("T2", at - 2))
                    dve.tensor_tensor(m.otok[:, at % 2].rearrange("p q (h d) -> p (q h) d", h=H), src[:, :, 0:DK],
                                      m.recip[:, at % 2].unsqueeze(2).broadcast_to([P, 2 * H, DK]), ALU.mult
                                      ).then_inc(sem["otok_ready"], 1)
                elif kind == "C1" and not ffn:
                    key = ("C1", at)
                    bank_ready(dve, key)
                    if at >= 2:
                        dve.wait_ge(sem["stored"][at % 2], 16 * (at // 2))
                    dve.tensor_tensor(m.rbuf[:, at % 2].rearrange("p a d -> p (a d)"), lin(key)[:, :],
                                      m.R[:, 4 * at:4 * at + 4, :].rearrange("p a d -> p (a d)"), ALU.add
                                      ).then_inc(sem["out_ready"], 1)
                elif kind in ("C1", "C4"):
                    norm((kind, at), ln_index[(kind, at)])
                elif kind == "C3":
                    for c in (1, 3):
                        key = ("C3", at, c)
                        bank_ready(dve, key)
                        if at >= 1:
                            bank_ready(dve, ("C4", at - 1))
                        dve.tensor_scalar(m.hidden[:, c, :], lin(key)[:, :], w.b1[:, c:c + 1], 0.0, ALU.add, ALU.max
                                          ).then_inc(sem["hid_dve"], 1)

        @block.gpsimd
        def _(pool):
            chain = Link(pool, sem["pool_chain"])

            if ffn:
                pool.wait_ge(sem["w_bc"], 16)
                chain.step(pool.tensor_tensor(m.be1b2[:, :], w.be1_bc, w.b2_bc, ALU.add))
            for item in order:
                kind, at = item[0], item[1]
                if kind == "A":
                    g = at
                    for t in range(2):
                        qf, parts = m.qf[:, t, g % 2], m.parts[:, t, g % 2]
                        pool.wait_ge(sem["q_ready"], 4 * g + 2 * t + 2)
                        chain.mark(pool.tensor_tensor(m.rest[:, :], qf, parts[:, 0], ALU.subtract))
                        chain.mark(pool.tensor_tensor(parts[:, 1], qf, parts[:, 0], ALU.subtract))
                        chain.wait()
                        pool.tensor_tensor(parts[:, 2], m.rest[:, :], parts[:, 1], ALU.subtract
                                           ).then_inc(sem["split_done"], 1)
                        pool.wait_ge(sem["split_done"], 2 * g + t + 1)
                    if ffn:
                        R = m.R[:, 4 * g:4 * g + 4, :]
                        pool.tensor_tensor(R, R, bc4(w.bo_bc), ALU.add).then_inc(sem["res"]["C1"], 1)
                elif ffn and kind in ("C1", "C4"):
                    n = ln_index[(kind, at)]
                    R = m.R[:, 4 * at:4 * at + 4, :]
                    pool.wait_ge(sem["stats_ready"], n + 1)
                    chain.step(pool.tensor_scalar(m.vareps[:, :], m.mv[:, n % 2, :, 1], EPS, None, ALU.add))
                    pool.tensor_tensor(m.rstd[:, n % 2, :], m.vareps[:, :], m.mhalf[:, :], ALU.pow
                                       ).then_inc(sem["rstd_ready"], 1)
                    g_bc, be_bc = (w.g1_bc, m.be1b2[:, :]) if kind == "C1" else (w.g2_bc, w.be2_bc)
                    pool.wait_ge(sem["xhat_ready"], n + 1)
                    pool.wait_ge(sem["rstd_ready"], n + 1)
                    chain.step(pool.tensor_tensor(R, m.xhat[:, n % 2], bc4(g_bc), ALU.mult))
                    pool.tensor_tensor(R, R, bc4(be_bc), ALU.add).then_inc(sem["res_out"][kind], 1)


NORM_SEMS = ("stats_ready rstd_ready xhat_ready h_ready lin_ready0 lin_ready1 xT_ready residual_done loaded dve_chain "
             "pool_chain").split()


def emit_norms(nc, m, sem, kinds, res=None, final=None, affine=None, turn=True):
    items = [(k, step - lag) for step in range(PAIRS + len(kinds)) for lag, k in enumerate(kinds)
             if 0 <= step - lag < PAIRS]
    index = {item: n for n, item in enumerate(items)}
    group = lambda buf, g: buf[:, 4 * g:4 * g + 4, :]
    source = {"F": m.R, "G": m.X, "X": m.R, "N": m.X}
    dest = {"F": m.T, "G": m.T, "X": m.X, "N": m.T}
    last = kinds[-1]
    stats, mv, vareps, rstd = m.norm_scratch
    with nc.Block() as block:
        @block.sync
        def _(sp):
            for dst, src in m.loads:
                sp.dma_start(dst, src).then_inc(sem["loaded"], 16)

        @block.vector
        def _(dve):
            chain = Link(dve, sem["dve_chain"])

            def apply(n):
                k, g = items[n]
                dve.wait_ge(sem["rstd_ready"], n + 1)
                if k == "N" and "F" in kinds:
                    dve.wait_ge(sem["h_ready"], g + 1)
                for i in range(4):
                    ins = dve.tensor_scalar(group(dest[k], g)[:, i], group(source[k], g)[:, i], mv[:, n % 3, i, 0:1],
                                            rstd[:, n % 3, i:i + 1], ALU.subtract, ALU.mult)
                ins.then_inc(sem["xhat_ready"], 1)

            for n, (k, g) in enumerate(items):
                if k == "X" and len(kinds) > 1:
                    dve.wait_ge(sem["h_ready"], g + 1)
                if k == "N":
                    dve.wait_ge(sem["xhat_ready"], index[("X", g)] + 1)
                if n >= 3:
                    dve.wait_ge(sem["xhat_ready"], n - 2)
                for i in range(4):
                    ins = dve.bn_stats(stats[:, i, :], group(source[k], g)[:, i])
                chain.step(ins)
                for i in range(4):
                    ins = dve.bn_aggr(mv[:, n % 3, i, :], stats[:, i, :])
                ins.then_inc(sem["stats_ready"], 1)
                dve.wait_ge(sem["stats_ready"], n + 1)
                if n:
                    apply(n - 1)
            apply(len(items) - 1)

        @block.gpsimd
        def _(pool):
            chain = Link(pool, sem["pool_chain"])
            pool.wait_ge(sem["loaded"], 16 * len(m.loads))
            for n, (k, g) in enumerate(items):
                pool.wait_ge(sem["stats_ready"], n + 1)
                if n >= 3:
                    pool.wait_ge(sem["xhat_ready"], n - 2)
                chain.step(pool.tensor_scalar(vareps[:, :], mv[:, n % 3, :, 1], EPS, None, ALU.add))
                ins = pool.tensor_tensor(rstd[:, n % 3, :], vareps[:, :], m.mhalf[:, :], ALU.pow)
                ins.then_inc(sem["rstd_ready"], 1)
                pool.wait_ge(sem["rstd_ready"], n + 1)
                R = group(m.R, g)
                if k == "F":
                    pool.wait_ge(sem["xhat_ready"], n + 1)
                    chain.step(pool.tensor_tensor(R, group(m.T, g), bc4(final[0]), ALU.mult))
                    pool.tensor_tensor(R, R, bc4(final[1]), ALU.add).then_inc(sem["h_ready"], 1)
                    pool.wait_ge(sem["h_ready"], g + 1)
                if k == "G":
                    pool.wait_ge(sem["xhat_ready"], n + 1)
                    T = group(m.T, g)
                    chain.step(pool.tensor_tensor(T, T, bc4(final[0]), ALU.mult))
                    chain.step(pool.tensor_tensor(T, T, bc4(final[1]), ALU.add))
                    pool.tensor_tensor(R, R, T, ALU.add).then_inc(sem["h_ready"], 1)
                    pool.wait_ge(sem["h_ready"], g + 1)
                if k == last and res is not None:
                    pool.wait_ge(sem["xhat_ready"], index[("X", g)] + 1)
                    chain.step(pool.tensor_tensor(R, R, group(m.X, g), ALU.add))
                    if res != "x":
                        chain.step(pool.tensor_tensor(R, R, bc4(res), ALU.add))

        @block.tensor
        def _(pe):
            for g in range(PAIRS if turn else 0):
                pe.wait_ge(sem["xhat_ready"], index[(last, g)] + 1)
                if g >= 2:
                    pe.wait_ge(sem["xT_ready"], g - 1)
                for i in range(4):
                    ins = pe.transpose(m.bank[g % 2][:, i * P:(i + 1) * P], group(dest[last], g)[:, i], m.ident[:, :])
                ins.then_inc(sem["lin_ready0"], 1)

        @block.scalar
        def _(act):
            act.wait_ge(sem["loaded"], 16 * len(m.loads))
            for g in range(PAIRS if turn else 0):
                act.wait_ge(sem["lin_ready0"], g + 1)
                out = m.xT[:, g * PW:(g + 1) * PW]
                if affine:
                    act.activation(out, m.bank[g % 2][:, :], ACT.Identity, scale=affine[0], bias=affine[1]
                                   ).then_inc(sem["xT_ready"], 1)
                else:
                    act.activation(out, m.bank[g % 2][:, :], ACT.Copy).then_inc(sem["xT_ready"], 1)


NYS_SEMS = ("loaded toeplitz_loaded qk_ready qk_copied v_ready v_copied landmarks_ready sims_ready shifted exps sum1 a_ready "
            "turned turned_copied a3v_ready a3v_copied row_max all_max scaled z_step z_act z_dve w_ready w_copied "
            "outT_ready outT_copied y_ready y_added consts dve_chain pool_chain act_chain").split()
LM = 64
LG = S // LM
PINV_ITERS = 6
KSIZE = 33


def nystrom(nc, m, t, sem, settle, banks, stack):
    def sb(name, shape, dt=F32):
        return stack.enter_context(nc.sbuf_tensor(name, shape, dt))

    wqkv = m.wqkv
    qT, kT = sb("ny_q", [DK, TOK]), sb("ny_k", [DK, TOK])
    v = sb("ny_v", [P, PAIRS, 2, 2, DK])
    ql, kl = sb("ny_ql", [DK, B * LM]), sb("ny_kl", [DK, B * LM])
    a1, a3, a2 = sb("a1", [P, PAIRS, 2, 2, LM]), sb("a3", [P, PAIRS, S]), sb("a2", [P, PAIRS, LM])
    a1T, a3T = sb("a1T", [P, PAIRS, S]), sb("a3T", [P, PAIRS, 2, P])
    a2D, a2T = sb("a2D", [P, PAIRS, P]), sb("a2T", [P, PAIRS, P])
    z, zT, aT = sb("z", [P, PAIRS, P]), sb("zT", [P, PAIRS, P]), sb("aT", [P, PAIRS, P])
    u = sb("u", [P, 3, PAIRS, P])
    mx, sums = sb("ny_max", [P, 24]), sb("ny_sum", [P, 24])
    rowcol, allmax = sb("rowcol", [P, 10]), sb("allmax", [P, 4])
    a3v, wv = sb("a3v", [P, PAIRS, DK]), sb("wv", [P, PAIRS, 2 * DK])
    outT = sb("outT", [2 * DK, PAIRS, S])
    wout, toep = sb("wout", [2 * DK, 2, D]), sb("toep", [P, 2, S])
    eyes = sb("eyes", [P, 3, P])
    half = [slice(0, 2), slice(2, 4)]

    with nc.Block() as block:
        @block.sync
        def _(sp):
            sp.wait_ge(sem["consts"], 1)
            for i in range(2):
                sp.dma_start(wout[i * DK:(i + 1) * DK, i, :], t.all["L0_attn_w_out"]).then_inc(sem["loaded"], 16)
            sp.dma_start(toep[:, :, :], t.taps).then_inc(sem["toeplitz_loaded"], 16)

        @block.tensor
        def _(pe):
            for g in range(PAIRS):
                for i in range(2):
                    n = 2 * g + i
                    if n >= 2:
                        pe.wait_ge(sem["qk_copied"], n - 1)
                    pe.matmul(banks[0:DK, n % 2, :], wqkv[:, i * DK:(i + 1) * DK], m.xT[:, g * PW:(g + 1) * PW],
                              start=True, stop=True).then_inc(sem["qk_ready"], 1)
            for tile in range(TILES):
                g, b2, kt = tile // 4, (tile // 2) % 2, tile % 2
                c = ((g * 2 + kt) * 2 + b2) * DK
                ins = pe.matmul(banks[:, 2, c:c + DK], m.xT[:, tile * P:(tile + 1) * P], wqkv[:, 2 * DK:3 * DK],
                                start=True, stop=True)
            ins.then_inc(sem["v_ready"], 1)
            pe.wait_ge(sem["landmarks_ready"], 2)
            for b in range(B):
                g, b2 = b // 2, b % 2
                p0 = LM * b2
                ins = pe.matmul(banks[p0:p0 + LM, 3, g * LM:(g + 1) * LM], ql[:, b * LM:(b + 1) * LM], kl[:, b * LM:(b + 1) * LM],
                                start=True, stop=True)
            ins.then_inc(sem["sims_ready"], 1)
            for b in range(B):
                g, b2 = b // 2, b % 2
                p0 = LM * b2
                ins = pe.matmul(banks[p0:p0 + LM, 4 + g // 2, (g % 2) * S:(g % 2 + 1) * S], ql[:, b * LM:(b + 1) * LM],
                                kT[:, b * S:(b + 1) * S], start=True, stop=True)
            ins.then_inc(sem["sims_ready"], 1)
            for b in range(B):
                g, b2 = b // 2, b % 2
                for kt in range(2):
                    c = (g % 2) * 256 + kt * 128 + b2 * LM
                    ins = pe.matmul(banks[:, 6 + g // 2, c:c + LM], qT[:, b * S + kt * P:b * S + (kt + 1) * P],
                                    kl[:, b * LM:(b + 1) * LM], start=True, stop=True)
            ins.then_inc(sem["sims_ready"], 1)
            pe.wait_ge(sem["a_ready"], 1)
            for g in range(PAIRS):
                ins = pe.transpose(banks[:, 3, g * P:(g + 1) * P], a2D[:, g, :], m.ident[:, :])
            ins.then_inc(sem["turned"], 1)

            def product(bank, left, right, hf, sem_inc=None):
                for g in (2 * hf, 2 * hf + 1):
                    ins = pe.matmul(banks[:, bank, (g % 2) * P:(g % 2 + 1) * P], left[:, g, :], right[:, g, :],
                                    start=True, stop=True)
                return ins

            pe.wait_ge(sem["scaled"], 2)
            for it in range(PINV_ITERS):
                for step in range(4):
                    for hf in range(2):
                        n = 2 * (4 * it + step) + hf
                        if n >= 2:
                            pe.wait_ge(sem["z_dve"], n - 1)
                        if step in (0, 1) and (it or step):
                            pe.wait_ge(sem["z_act"], 2 * (2 * it + step) + hf - 1)
                        if step == 0:
                            product(2 * hf, a2T, z, hf)
                            ins = product(2 * hf + 1, z, a2T, hf)
                        elif step < 3:
                            ins = product(2 * hf, aT, u[:, step - 1], hf)
                        else:
                            product(2 * hf, zT, u[:, 2], hf)
                            ins = product(2 * hf + 1, u[:, 2], zT, hf)
                        ins.then_inc(sem["z_step"], 1)
                if it == 0:
                    pe.wait_ge(sem["a_ready"], 3)
                    pe.wait_ge(sem["v_copied"], 1)
                    for g in range(PAIRS):
                        for kt in range(2):
                            ins = pe.transpose(banks[:, 4 + g // 2, ((g % 2) * 2 + kt) * P:((g % 2) * 2 + kt + 1) * P],
                                               a3[:, g, kt * P:(kt + 1) * P], m.ident[:, :])
                    ins.then_inc(sem["turned"], 1)
                    for g in range(PAIRS):
                        for kt in range(2):
                            ins = pe.transpose(banks[:, 6 + g // 2, ((g % 2) * 2 + kt) * P:((g % 2) * 2 + kt + 1) * P],
                                               a1[:, g, kt].rearrange("p b l -> p (b l)"), m.ident[:, :])
                    ins.then_inc(sem["turned"], 1)
                if it == 1:
                    pe.wait_ge(sem["turned_copied"], 3)
                    for b in range(B):
                        g, p0 = b // 2, LM * (b % 2)
                        for kt in range(2):
                            ins = pe.matmul(banks[p0:p0 + LM, 4, g * DK:(g + 1) * DK], a3T[:, g, kt, p0:p0 + LM],
                                            v[:, g, kt, b % 2, :], start=(kt == 0), stop=(kt == 1))
                    ins.then_inc(sem["a3v_ready"], 1)
            pe.wait_ge(sem["a3v_copied"], 1)
            pe.wait_ge(sem["z_act"], 2 * 2 * PINV_ITERS)
            pe.wait_ge(sem["z_dve"], 2 * 4 * PINV_ITERS)
            for g in range(PAIRS):
                ins = pe.matmul(banks[:, 4, g * DK:(g + 1) * DK], zT[:, g, :], a3v[:, g, :], start=True, stop=True)
            ins.then_inc(sem["w_ready"], 1)
            pe.wait_ge(sem["w_copied"], 2)
            pe.wait_ge(sem["toeplitz_loaded"], 16)
            pe.wait_ge(sem["loaded"], 32)
            for g in range(PAIRS):
                if g >= 2:
                    pe.wait_ge(sem["outT_copied"], g - 1)
                bank = banks[0:2 * DK, g % 2, 0:S]
                pe.matmul(bank, wv[:, g, :], a1T[:, g, :], start=True, stop=False)
                for kt in range(2):
                    ins = pe.matmul(bank, v[:, g, kt].rearrange("p b d -> p (b d)"), toep[:, kt, :], start=False, stop=(kt == 1))
                ins.then_inc(sem["outT_ready"], 1)
            for g in range(PAIRS):
                pe.wait_ge(sem["outT_copied"], g + 1)
                if g >= 2:
                    pe.wait_ge(sem["y_added"], g - 1)
                for kt in range(2):
                    ins = pe.matmul(banks[:, 2 + g % 2, kt * 2 * P:(kt + 1) * 2 * P], outT[:, g, kt * P:(kt + 1) * P],
                                    wout[:, :, :].rearrange("p b d -> p (b d)"), start=True, stop=True)
                ins.then_inc(sem["y_ready"], 1)

        @block.scalar
        def _(act):
            for g in range(PAIRS):
                for i, (dst, scale) in enumerate(((qT, DK ** -0.5), (kT, 1.0))):
                    act.wait_ge(sem["qk_ready"], 2 * g + i + 1)
                    act.activation(dst[:, g * PW:(g + 1) * PW], banks[0:DK, i, :], ACT.Copy, scale=scale
                                   ).then_inc(sem["qk_copied"], 1)
            act.wait_ge(sem["v_ready"], 1)
            act.activation(v[:, :, :, :, :].rearrange("p a b c d -> p (a b c d)"), banks[:, 2, 0:TILES * DK], ACT.Copy
                           ).then_inc(sem["v_copied"], 1)
            for n, a in enumerate((a2[:, :, :], a3[:, :, :], a1[:, :, :, :, :])):
                act.wait_ge(sem["shifted"], n + 1)
                act.activation(a, a, ACT.Exp).then_inc(sem["exps"], 1)
            act.wait_ge(sem["turned"], 1)
            act.activation(a2T[:, :, :].rearrange("p g n -> p (g n)"), banks[:, 3, :], ACT.Copy).then_inc(sem["turned_copied"], 1)

            def copy_half(dst, hf, n):
                act.wait_ge(sem["z_step"], n)
                act.activation(dst[:, 2 * hf:2 * hf + 2, :].rearrange("p g n -> p (g n)"), banks[:, 2 * hf + 1, 0:2 * P],
                               ACT.Copy).then_inc(sem["z_act"], 1)

            for it in range(PINV_ITERS):
                for step, dst in ((0, aT), (3, zT)):
                    for hf in range(2):
                        copy_half(dst, hf, 2 * (4 * it + step) + hf + 1)
                if it == 0:
                    act.wait_ge(sem["turned"], 2)
                    act.activation(a3T[:, :, :, :].rearrange("p g k n -> p (g k n)"),
                                   banks[:, 4:6, :].rearrange("p b n -> p (b n)"), ACT.Copy).then_inc(sem["turned_copied"], 1)
                    act.wait_ge(sem["turned"], 3)
                    act.activation(a1T[:, :, :].rearrange("p g n -> p (g n)"),
                                   banks[:, 6:8, :].rearrange("p b n -> p (b n)"), ACT.Copy).then_inc(sem["turned_copied"], 1)
                if it == 1:
                    act.wait_ge(sem["a3v_ready"], 1)
                    act.activation(a3v[:, :, :].rearrange("p g d -> p (g d)"), banks[:, 4, 0:PAIRS * DK], ACT.Copy
                                   ).then_inc(sem["a3v_copied"], 1)
            act.wait_ge(sem["w_ready"], 1)
            act.wait_ge(sem["consts"], 1)
            for i in range(2):
                p0 = LM * i
                act.activation(wv[p0:p0 + LM, :, i * DK:(i + 1) * DK],
                               banks[p0:p0 + LM, 4, 0:PAIRS * DK].rearrange("p (g d) -> p g d", g=PAIRS), ACT.Copy
                               ).then_inc(sem["w_copied"], 1)
            for g in range(PAIRS):
                act.wait_ge(sem["outT_ready"], g + 1)
                act.activation(outT[:, g, :], banks[0:2 * DK, g % 2, 0:S], ACT.Copy).then_inc(sem["outT_copied"], 1)

        @block.gpsimd
        def _(pool):
            pool.memset(a2D[:, :, :], 0.0)
            pool.memset(wv[:, :, :], 0.0)
            pool.memset(wout[:, :, :], 0.0).then_inc(sem["consts"], 1)
            pool.wait_ge(sem["row_max"], 1)
            pool.partition_all_reduce(allmax[:, 0:2], rowcol[:, 8:10], P, bass.bass_isa.ReduceOp.max).then_inc(sem["all_max"], 1)

        @block.vector
        def _(dve):
            chain = Link(dve, sem["dve_chain"])
            for i, c in enumerate((7.0, 15.0, 3.25)):
                ins = dve.tensor_scalar(eyes[:, i, :], m.ident[:, :], c, None, ALU.mult)
            chain.step(ins)
            dve.wait_ge(sem["qk_copied"], 2 * PAIRS)
            for src, dst in ((qT, ql), (kT, kl)):
                chain.step(dve.tensor_reduce(dst[:, :], src[:, :].rearrange("p (n l) -> p n l", l=LG), AX.X, ALU.add))
                dve.tensor_scalar(dst[:, :], dst[:, :], 1.0 / LG, None, ALU.mult).then_inc(sem["landmarks_ready"], 1)
            views = ((banks[:, 3, 0:PAIRS * LM].rearrange("p (g n) -> p g n", g=PAIRS), a2[:, :, :], 0, PAIRS),
                     (banks[:, 4:6, :].rearrange("p b (g n) -> p (b g) n", g=2), a3[:, :, :], 4, PAIRS),
                     (banks[:, 6:8, :].rearrange("p b (g n) -> p (b g) n", n=LM),
                      a1[:, :, :, :, :].rearrange("p g k b n -> p (g k b) n"), 8, 4 * PAIRS))

            def shift(n):
                src, dst, c, G = views[n]
                dve.wait_ge(sem["sims_ready"], n + 1)
                chain.step(dve.tensor_reduce(mx[:, c:c + G], src, AX.X, ALU.max))
                dve.tensor_tensor(dst, src, mx[:, c:c + G].unsqueeze(2).broadcast_to(list(dst.shape)), ALU.subtract
                                  ).then_inc(sem["shifted"], 1)

            def normalise(n, outs):
                src, dst, c, G = views[n]
                dve.wait_ge(sem["exps"], n + 1)
                chain.step(dve.tensor_reduce(sums[:, c:c + G], dst, AX.X, ALU.add))
                chain.step(dve.reciprocal(sums[:, c:c + G], sums[:, c:c + G]))
                for p0, p1, out in outs:
                    ins = dve.tensor_tensor(out, dst[p0:p1], sums[p0:p1, c:c + G].unsqueeze(2).broadcast_to([p1 - p0, *dst.shape[1:]]),
                                            ALU.mult)
                ins.then_inc(sem["a_ready"], 1)

            shift(0)
            shift(1)
            dve.wait_ge(sem["consts"], 1)
            normalise(0, [(0, LM, a2D[0:LM, :, 0:LM]), (LM, P, a2D[LM:P, :, LM:P])])
            shift(2)
            dve.wait_ge(sem["a_ready"], 1)
            ins = dve.tensor_reduce(rowcol[:, 0:4], a2D[:, :, :], AX.X, ALU.add, apply_absolute_value=True)
            dve.wait_ge(sem["turned_copied"], 1)
            chain.step(dve.tensor_reduce(rowcol[:, 4:8], a2T[:, :, :], AX.X, ALU.add, apply_absolute_value=True))
            ins = dve.tensor_reduce(rowcol[:, 8:10], rowcol[:, 0:8].rearrange("p (a b) -> p a b", a=2), AX.X, ALU.max)
            ins.then_inc(sem["row_max"], 1)
            normalise(1, [(0, P, a3[:, :, :])])
            normalise(2, [(0, P, a1[:, :, :, :, :].rearrange("p g k b n -> p (g k b) n"))])
            dve.wait_ge(sem["all_max"], 1)
            chain.step(dve.tensor_tensor(allmax[:, 2:3], allmax[:, 0:1], allmax[:, 1:2], ALU.mult))
            chain.step(dve.reciprocal(allmax[:, 3:4], allmax[:, 2:3]))
            for src, dst in ((a2T, z), (a2D, zT)):
                dve.tensor_scalar(dst[:, :, :], src[:, :, :], allmax[:, 3:4], None, ALU.mult).then_inc(sem["scaled"], 1)

            def z_step(it, step, hf):
                n = 2 * (4 * it + step) + hf
                dve.wait_ge(sem["z_step"], n + 1)
                src = banks[:, 2 * hf, 0:2 * P].rearrange("p (g n) -> p g n", g=2)
                if step < 2:
                    dve.tensor_tensor(u[:, step, half[hf], :], eyes[:, step, :].unsqueeze(1).broadcast_to([P, 2, P]), src,
                                      ALU.subtract).then_inc(sem["z_dve"], 1)
                elif step == 2:
                    for j in range(2):
                        ins = dve.scalar_tensor_tensor(out=u[:, 2, 2 * hf + j, :], in0=src[:, j, :], scalar=-0.25,
                                                       in1=eyes[:, 2, :], op0=ALU.mult, op1=ALU.add)
                    ins.then_inc(sem["z_dve"], 1)
                else:
                    dve.tensor_copy(z[:, half[hf], :], src).then_inc(sem["z_dve"], 1)

            for it in range(PINV_ITERS):
                for step in range(4):
                    for hf in range(2):
                        z_step(it, step, hf)
            for g in range(PAIRS):
                dve.wait_ge(sem["y_ready"], g + 1)
                for kt in range(2):
                    R = m.R[:, 4 * g:4 * g + 4, :].rearrange("p (b k) d -> p k b d", k=2)[:, kt]
                    ins = dve.tensor_tensor(R, R, banks[:, 2 + g % 2, kt * 2 * P:(kt + 1) * 2 * P].rearrange("p (b d) -> p b d", b=2),
                                            ALU.add)
                ins.then_inc(sem["y_added"], 1)
    settle()


MOE_SEMS = ("loaded rf_ready rf_copied h_psum hT_ready logits_ready chosen weights_exp gates_ready gates_turned gates_copied "
            "bias_ready bias_added w_even w_odd up_ready hid_ready down_ready down_added irf_ready irf_copied ot_ready ot_copied "
            "dve_chain pool_chain act_chain").split()
EXPERTS = 8
FREQ = S // 2 + 1
MT_ = B * P
MTOK = MT_ + B
MTILES = B + 1
CHUNKS = ((0, PW), (PW, PW), (2 * PW, B))


def frequency_experts(nc, m, t, sem, settle, banks, stack):
    def sb(name, shape, dt=F32):
        return stack.enter_context(nc.sbuf_tensor(name, shape, dt))

    fwd = sb("fwd", [P, 2, 2 * FREQ])
    xf = sb("xf", [P, 2, MTOK])
    hT = sb("hT", [P, MTILES * P])
    pin, rw, cols = sb("pin", [P, 2, P]), sb("rw", [P, EXPERTS]), sb("pin_b", [P, 1])
    rb, b2 = sb("rb", [P, 2, EXPERTS]), sb("b2", [EXPERTS, P])
    lg, oh1, oh2, key = (sb(n, [P, MTILES, EXPERTS]) for n in ("lg", "oh1", "oh2", "key"))
    gates = sb("gates", [P, EXPERTS, MTILES])
    top = sb("top", [P, 6, MTILES])
    gT = sb("gT", [EXPERTS, MTILES * P])
    acc = sb("acc", [P, MTILES, D])
    w1, w2, b1 = sb("w1", [P, 2, 4 * P]), sb("w2", [P, 2, 4, P]), sb("b1", [P, 2, 4])
    hid = sb("hid", [P, 2, 4, MTOK])
    inv, inv8 = sb("inv", [P, 2 * S]), sb("inv8", [B, B, S])
    pout, poutb, ramp = sb("pout", [P, 2, P]), sb("poutb", [2, P]), sb("ramp", [2, S])
    yT = sb("yT", [P, 2, 2 * S])

    with nc.Block() as block:
        @block.sync
        def _(sp):
            for dst, src in ((fwd[:, :, :], t.all["fwd"]), (pin[:, :, :], t.all["L0_ffn_pin_w"].rearrange("(r p) n -> p r n", p=P)),
                             (cols[:, :], t.all["L0_ffn_pin_b"].rearrange("(p a) -> p a", a=1)),
                             (rw[:, :], t.all["L0_ffn_router_w"]),
                             (rb[:, :, :], t.all["router_rows"].broadcast_to([P, 2, EXPERTS])),
                             (b2[:, :], t.all["L0_ffn_b2"]), (inv[:, :], t.all["inv"]), (inv8[:, :, :], t.all["inv8"]),
                             (pout[:, :, :], t.all["L0_ffn_pout_w"].rearrange("p (r n) -> p r n", r=2)),
                             (poutb[:, :], t.all["L0_ffn_pout_b"].rearrange("(r n) -> r n", r=2)), (ramp[:, :], t.all["ramp"])):
                sp.dma_start(dst, src).then_inc(sem["loaded"], 16)

        @block.tensor
        def _(pe):
            pe.wait_ge(sem["loaded"], 16 * 11)
            for b in range(B):
                if b >= 2:
                    pe.wait_ge(sem["rf_copied"], b - 1)
                for kt in range(2):
                    ins = pe.matmul(banks[:, b % 2, 0:2 * FREQ], m.X[:, 2 * b + kt, :], fwd[:, kt, :],
                                    start=(kt == 0), stop=(kt == 1))
                ins.then_inc(sem["rf_ready"], 1)
            pe.wait_ge(sem["rf_copied"], B)
            for c, (c0, cn) in enumerate(CHUNKS):
                for r in range(2):
                    ins = pe.matmul(banks[:, 2 + c, 0:cn], pin[:, r, :], xf[:, r, c0:c0 + cn], start=(r == 0), stop=(r == 1))
                ins.then_inc(sem["h_psum"], 1)
            pe.wait_ge(sem["hT_ready"], 4)
            for i in range(MTILES):
                ins = pe.matmul(banks[:, 5, i * EXPERTS:(i + 1) * EXPERTS], hT[:, i * P:(i + 1) * P], rw[:, :],
                                start=True, stop=True)
            ins.then_inc(sem["logits_ready"], 1)
            pe.wait_ge(sem["gates_ready"], 1)
            for i in range(MTILES):
                c = i * P
                ins = pe.transpose(banks[0:EXPERTS, c // PW, c % PW:c % PW + P], gates[:, :, i], m.ident[:, :])
            ins.then_inc(sem["gates_turned"], 1)
            pe.wait_ge(sem["gates_copied"], 1)
            for i in range(MTILES):
                c = i * P
                ins = pe.matmul(banks[:, 4 + c // PW, c % PW:c % PW + P], gT[:, i * P:(i + 1) * P], b2[:, :],
                                start=True, stop=True)
            ins.then_inc(sem["bias_ready"], 1)

        @block.scalar
        def _(act):
            for b in range(B):
                act.wait_ge(sem["rf_ready"], b + 1)
                src = banks[:, b % 2, 0:2 * FREQ].rearrange("p (r f) -> p r f", r=2)
                act.activation(xf[:, :, b * P:(b + 1) * P], src[:, :, 0:P], ACT.Copy)
                act.activation(xf[:, :, MT_ + b:MT_ + b + 1], src[:, :, P:P + 1], ACT.Copy).then_inc(sem["rf_copied"], 1)
            act.wait_ge(sem["loaded"], 16 * 11)
            for c, (c0, cn) in enumerate(CHUNKS):
                act.wait_ge(sem["h_psum"], c + 1)
                act.activation(hT[:, c0:c0 + cn], banks[:, 2 + c, 0:cn], ACT.Identity, bias=cols[:, 0:1]
                               ).then_inc(sem["hT_ready"], 1)
            act.wait_ge(sem["chosen"], 1)
            act.activation(top[:, 2, :], top[:, 2, :], ACT.Exp).then_inc(sem["weights_exp"], 1)
            act.wait_ge(sem["gates_turned"], 1)
            act.activation(gT[:, :], banks[0:EXPERTS, 0:3, :].rearrange("p b n -> p (b n)")[:, 0:MTILES * P], ACT.Copy
                           ).then_inc(sem["gates_copied"], 1)

        @block.gpsimd
        def _(pool):
            pool.memset(hT[:, MTOK:], 0.0).then_inc(sem["hT_ready"], 1)

        @block.vector
        def _(dve):
            chain = Link(dve, sem["dve_chain"])
            wide = lambda x: x.unsqueeze(2).broadcast_to([P, MTILES, EXPERTS])
            every = lambda x: x.unsqueeze(1).broadcast_to([P, MTILES, EXPERTS])
            dve.wait_ge(sem["logits_ready"], 1)
            dve.wait_ge(sem["loaded"], 16 * 11)
            chain.step(dve.tensor_tensor(lg[:, :, :], banks[:, 5, 0:MTILES * EXPERTS].rearrange("p (i e) -> p i e", e=EXPERTS),
                                         every(rb[:, 0, :]), ALU.add))
            for k, oh in enumerate((oh1, oh2)):
                chain.step(dve.tensor_reduce(top[:, k, :], lg[:, :, :], AX.X, ALU.max))
                chain.step(dve.tensor_tensor(key[:, :, :], lg[:, :, :], wide(top[:, k, :]), ALU.is_equal))
                chain.step(dve.tensor_tensor(key[:, :, :], key[:, :, :], every(rb[:, 1, :]), ALU.mult))
                chain.step(dve.tensor_reduce(top[:, 3, :], key[:, :, :], AX.X, ALU.max))
                chain.step(dve.tensor_tensor(oh[:, :, :], key[:, :, :], wide(top[:, 3, :]), ALU.is_equal))
                if k == 0:
                    chain.step(dve.scalar_tensor_tensor(out=lg[:, :, :], in0=oh[:, :, :], scalar=-3.0e38, in1=lg[:, :, :],
                                                        op0=ALU.mult, op1=ALU.add))
            dve.tensor_tensor(top[:, 2, :], top[:, 1, :], top[:, 0, :], ALU.subtract).then_inc(sem["chosen"], 1)
            dve.wait_ge(sem["weights_exp"], 1)
            chain.step(dve.tensor_scalar(top[:, 4, :], top[:, 2, :], 1.0, None, ALU.add))
            chain.step(dve.reciprocal(top[:, 4, :], top[:, 4, :]))
            chain.step(dve.tensor_tensor(top[:, 5, :], top[:, 2, :], top[:, 4, :], ALU.mult))
            chain.step(dve.tensor_tensor(oh1[:, :, :], oh1[:, :, :], wide(top[:, 4, :]), ALU.mult))
            chain.step(dve.tensor_tensor(oh2[:, :, :], oh2[:, :, :], wide(top[:, 5, :]), ALU.mult))
            dve.tensor_tensor(gates[:, :, :].rearrange("p e i -> p i e"), oh1[:, :, :], oh2[:, :, :], ALU.add
                              ).then_inc(sem["gates_ready"], 1)
            dve.wait_ge(sem["bias_ready"], 1)
            dve.tensor_copy(acc[:, :, :].rearrange("p i d -> p (i d)"),
                            banks[:, 4:7, :].rearrange("p b n -> p (b n)")[:, 0:MTILES * P]).then_inc(sem["bias_added"], 1)
    settle()

    with nc.Fori(0, EXPERTS // 2) as pair:
        with nc.Block() as block:
            @block.sync
            def _(sp):
                for j, arrived in enumerate((sem["w_even"], sem["w_odd"])):
                    at = bass.ds(2 * pair + j, 1)
                    sp.dma_start(w1[:, j, :], t.all["L0_ffn_w1"][at].rearrange("a p n -> (a p) n")).then_inc(arrived, 16)
                    sp.dma_start(b1[:, j, :], t.all["ffn_b1"][at].rearrange("a p n -> (a p) n")).then_inc(arrived, 16)
                    sp.dma_start(w2[:, j], t.all["L0_ffn_w2"][at].rearrange("a (c p) n -> p (a c) n", p=P)).then_inc(arrived, 16)

            @block.tensor
            def _(pe):
                def up(j):
                    for c in range(4):
                        for k in range(2):
                            n = 9 * j + 2 * c + k
                            if n >= 4:
                                pe.wait_ge(sem["hid_ready"], n - 3)
                            pe.matmul(banks[:, n % 4, :], w1[:, j, c * P:(c + 1) * P], hT[:, k * PW:(k + 1) * PW],
                                      start=True, stop=True).then_inc(sem["up_ready"], 1)
                    n = 9 * j + 8
                    pe.wait_ge(sem["hid_ready"], n - 3)
                    for c in range(4):
                        ins = pe.matmul(banks[:, n % 4, c * B:(c + 1) * B], w1[:, j, c * P:(c + 1) * P],
                                        hT[:, MT_:MTOK], start=True, stop=True)
                    ins.then_inc(sem["up_ready"], 1)

                def down(j):
                    pe.wait_ge(sem["hid_ready"], 9 * (j + 1))
                    for i in range(MTILES):
                        n = 3 * j + i // 4
                        if i % 4 == 0 and n >= 2:
                            pe.wait_ge(sem["down_added"], n - 1)
                        rows = P if i < B else B
                        out = banks[0:rows, 4 + n % 2, (i % 4) * P:(i % 4 + 1) * P]
                        for c in range(4):
                            ins = pe.matmul(out, hid[:, j, c, i * P:i * P + rows], w2[:, j, c, :], start=(c == 0), stop=(c == 3))
                        if i % 4 == 3 or i == B:
                            ins.then_inc(sem["down_ready"], 1)

                pe.wait_ge(sem["w_even"], 48)
                up(0)
                pe.wait_ge(sem["w_odd"], 48)
                up(1)
                down(0)
                down(1)

            @block.scalar
            def _(act):
                for j, arrived in enumerate((sem["w_even"], sem["w_odd"])):
                    act.wait_ge(arrived, 48)
                    for c in range(4):
                        for k in range(2):
                            n = 9 * j + 2 * c + k
                            act.wait_ge(sem["up_ready"], n + 1)
                            act.activation(hid[:, j, c, k * PW:(k + 1) * PW], banks[:, n % 4, :], ACT.Gelu,
                                           bias=b1[:, j, c:c + 1]).then_inc(sem["hid_ready"], 1)
                    n = 9 * j + 8
                    act.wait_ge(sem["up_ready"], n + 1)
                    for c in range(4):
                        ins = act.activation(hid[:, j, c, MT_:MTOK], banks[:, n % 4, c * B:(c + 1) * B], ACT.Gelu,
                                             bias=b1[:, j, c:c + 1])
                    ins.then_inc(sem["hid_ready"], 1)

            @block.vector
            def _(dve):
                for j in range(2):
                    for i in range(MTILES):
                        n = 3 * j + i // 4
                        if i % 4 == 0:
                            dve.wait_ge(sem["down_ready"], n + 1)
                            if j:
                                dve.wait_ge(sem["down_added"], n - 2)
                        rows = P if i < B else B
                        a = acc[0:rows, i, :]
                        ins = dve.scalar_tensor_tensor(out=a, in0=banks[0:rows, 4 + n % 2, (i % 4) * P:(i % 4 + 1) * P],
                                                       scalar=gates[0:rows, bass.ds(2 * pair + j, 1), i], in1=a,
                                                       op0=ALU.mult, op1=ALU.add)
                        if i % 4 == 3 or i == B:
                            ins.then_inc(sem["down_added"], 1)
        settle()

    with nc.Block() as block:
        @block.tensor
        def _(pe):
            def out_proj(b):
                pe.wait_ge(sem["irf_copied"], b + 1)
                if b % 2 == 0 and b >= 4:
                    pe.wait_ge(sem["ot_copied"], b // 2 - 1)
                for kt in range(2):
                    o = banks[:, 2 + (b // 2) % 2, ((b % 2) * 2 + kt) * P:((b % 2) * 2 + kt + 1) * P]
                    for r in range(2):
                        pe.matmul(o, yT[:, b % 2, r * S + kt * P:r * S + (kt + 1) * P], pout[:, r, :], start=(r == 0), stop=False)
                    ins = pe.matmul(o, ramp[:, kt * P:(kt + 1) * P], poutb[:, :], start=False, stop=True)
                if b % 2:
                    ins.then_inc(sem["ot_ready"], 1)

            for b in range(B):
                if b >= 2:
                    pe.wait_ge(sem["irf_copied"], b - 1)
                pe.matmul(banks[:, b % 2, 0:S], acc[:, b, :], inv[:, 0:S], start=True, stop=False)
                pe.matmul(banks[:, b % 2, 0:S], acc[0:B, B, :], inv8[:, b, :], start=False, stop=True)
                pe.matmul(banks[:, b % 2, S:], acc[:, b, :], inv[:, S:], start=True, stop=True).then_inc(sem["irf_ready"], 1)
                if b:
                    out_proj(b - 1)
            out_proj(B - 1)

        @block.scalar
        def _(act):
            for b in range(B):
                act.wait_ge(sem["irf_ready"], b + 1)
                if b >= 2 and b % 2 == 0:
                    act.wait_ge(sem["ot_ready"], b // 2)
                act.activation(yT[:, b % 2, :], banks[:, b % 2, :], ACT.Copy).then_inc(sem["irf_copied"], 1)

        @block.vector
        def _(dve):
            for g in range(PAIRS):
                dve.wait_ge(sem["ot_ready"], g + 1)
                dve.tensor_copy(m.X[:, 4 * g:4 * g + 4, :].rearrange("p i d -> p (i d)"), banks[:, 2 + g % 2, :]
                                ).then_inc(sem["ot_copied"], 1)
    settle()


def moe_constants():
    import numpy as np
    s, f = np.arange(S)[:, None], np.arange(FREQ)[None, :]
    turn = 2 * np.pi * ((s * f) % S) / S
    fwd = np.concatenate([np.cos(turn), -np.sin(turn)], axis=1) / np.sqrt(S)
    fwd[:, FREQ] = fwd[:, 2 * FREQ - 1] = 0.0
    twice = np.where((np.arange(FREQ) == 0) | (np.arange(FREQ) == S // 2), 1.0, 2.0)[:, None]
    cos, sin = twice * np.cos(turn.T) / np.sqrt(S), -twice * np.sin(turn.T) / np.sqrt(S)
    sin[0] = sin[-1] = 0.0
    inv8 = np.zeros((B, B, S))
    inv8[np.arange(B), np.arange(B)] = cos[-1]
    arrays = {"fwd": fwd.reshape(2, P, 2 * FREQ).transpose(1, 0, 2), "inv": np.concatenate([cos[:-1], sin[:-1]], axis=1),
              "inv8": inv8, "ramp": np.stack([cos.sum(0), sin.sum(0)])}
    return {k: np.ascontiguousarray(v.astype(np.float32)) for k, v in arrays.items()}


WIDE_SEMS = ("wqk_even wqk_odd wvo_even wvo_odd vo_ready vo_copied lin_ready0 lin_ready1 q_ready v_ready sc_ready max_ready "
             "exp_ready turned0 turned1 turned_dve turned_act av_ready added rows_ready dve_chain pool_chain act_chain").split()
WH = 8
TR = 2


def wide_attention(nc, m, t, sem, settle, banks, stack):
    def sb(name, shape, dt=F32):
        return stack.enter_context(nc.sbuf_tensor(name, shape, dt))

    wqk, wvT, wo = sb("wqk", [P, 2, 2, D]), sb("wvT", [P, 2, D]), sb("wo_h", [P, 2, D])
    cols, qb = sb("l1_cols", [P, 2, 3]), sb("l1_qb", [P, 2])
    vo, bv_wide, bvo = sb("vo", [P, 2, D]), sb("bv_wide", [P, 2, D]), sb("bvo", [P, 2, D])
    qk = sb("l1_qk", [P, 2, 2, TOK])
    vp = sb("vp", [P, 2, TILES, D])
    nmax, sums, rsum = sb("l1_nmax", [P, 2, 2]), sb("l1_sums", [P, 4, 2]), sb("l1_rsum", [P, 2, 2])
    probs, pT = sb("l1_probs", [P, 3, 2, S]), sb("l1_pT", [P, TR, 2, S])
    scale = float(D) ** -0.5

    def project_items(j):
        return [("VO", j)] + [("P", j, g, i) for g in range(PAIRS) for i in range(3)]

    units = [(j, b) for j in range(2) for b in range(B)]
    order = project_items(0)
    later = project_items(1)
    for n in range(len(units) + 2):
        if n < len(units):
            order.append(("SC", n))
        if 1 <= n <= len(units):
            order.append(("T", n - 1))
        if n >= 2:
            order.append(("AV", n - 2))
        for _ in range(2):
            if later and n >= 1:
                order.append(later.pop(0))
    assert not later
    uses = [x for x in order if x[0] in ("VO", "P")]
    turn = {key: (n % 2, n // 2) for n, key in enumerate(uses)}
    at_turn = {v: k for k, v in turn.items()}
    sc, tr, av, lin = banks[:, 0:2, :], banks[:, 2:4, :], banks[:, 4:6, :], banks[:, 6:8, :]

    with nc.Fori(0, WH // 2) as pair:
        def read_out(key):
            if key[0] == "VO":
                return sem["vo_copied"], 2 * key[1] + 2
            j, g, i = key[1:]
            return (sem["v_ready"], 4 * j + g + 1) if i == 2 else (sem["q_ready"], 8 * j + 2 * g + i + 1)

        def ready(eng, key):
            eng.wait_ge(sem["lin_ready0"] if turn[key][0] == 0 else sem["lin_ready1"], turn[key][1] + 1)

        with nc.Block() as block:
            @block.sync
            def _(sp):
                for j, (qk_in, vo_in) in enumerate(((sem["wqk_even"], sem["wvo_even"]), (sem["wqk_odd"], sem["wvo_odd"]))):
                    at = bass.ds(2 * pair + j, 1)
                    sp.dma_start(wqk[:, j], t.all["l1_qk"][at].rearrange("a p i n -> (a p) i n")).then_inc(qk_in, 16)
                    sp.dma_start(cols[:, j, :], t.all["l1_cols"][at].rearrange("a p i -> (a p) i")).then_inc(qk_in, 16)
                    sp.dma_start(wvT[:, j], t.all["l1_vT"][at].rearrange("a p n -> (a p) n")).then_inc(vo_in, 16)
                    sp.dma_start(wo[:, j], t.all["l1_o"][at].rearrange("a p n -> (a p) n")).then_inc(vo_in, 16)

            @block.tensor
            def _(pe):
                def use(key):
                    bank, n = turn[key]
                    if n:
                        pe.wait_ge(*read_out(at_turn[(bank, n - 1)]))
                    return lin[:, bank, :]

                def filled(key, ins):
                    ins.then_inc(sem["lin_ready0"] if turn[key][0] == 0 else sem["lin_ready1"], 1)

                for item in order:
                    if item[0] == "VO":
                        j = item[1]
                        bank = use(item)
                        pe.wait_ge(sem["wvo_odd"] if j else sem["wvo_even"], 32)
                        pe.matmul(bank[:, 0:D], wvT[:, j, :], wo[:, j, :], start=True, stop=True)
                        pe.wait_ge(sem["rows_ready"], j + 1)
                        filled(item, pe.matmul(bank[:, D:2 * D], bv_wide[:, j, :], wo[:, j, :], start=True, stop=True))
                    elif item[0] == "P":
                        _, j, g, i = item
                        bank = use(item)
                        if g == 0 and i == 0:
                            pe.wait_ge(sem["wqk_odd"] if j else sem["wqk_even"], 32)
                        if i < 2:
                            ins = pe.matmul(bank, wqk[:, j, i, :], m.xT[:, g * PW:(g + 1) * PW], start=True, stop=True)
                        else:
                            if g == 0:
                                pe.wait_ge(sem["vo_copied"], 2 * j + 2)
                            for a in range(4):
                                c = g * PW + a * P
                                ins = pe.matmul(bank[:, a * P:(a + 1) * P], m.xT[:, c:c + P], vo[:, j, :], start=True, stop=True)
                        filled(item, ins)
                    elif item[0] == "SC":
                        n = item[1]
                        j, b = units[n]
                        pe.wait_ge(sem["q_ready"], 8 * j + 2 * (b // 2) + 2)
                        if n >= 2:
                            pe.wait_ge(sem["exp_ready"], n - 1)
                        for qt in range(2):
                            c = b * S + qt * P
                            ins = pe.matmul(sc[:, n % 2, qt * S:(qt + 1) * S], qk[:, j, 0, c:c + P], qk[:, j, 1, b * S:(b + 1) * S],
                                            start=True, stop=True)
                        ins.then_inc(sem["sc_ready"], 1)
                    elif item[0] == "T":
                        n = item[1]
                        pe.wait_ge(sem["exp_ready"], n + 1)
                        if n >= 2:
                            pe.wait_ge(sem["turned_act"] if n % 2 else sem["turned_dve"], n // 2)
                        for kt in range(2):
                            for qt in range(2):
                                c = kt * S + qt * P
                                ins = pe.transpose(tr[:, n % 2, c:c + P], probs[:, n % 3, qt, kt * P:(kt + 1) * P], m.ident[:, :])
                        ins.then_inc(sem["turned1"] if n % 2 else sem["turned0"], 1)
                    else:
                        n = item[1]
                        j, b = units[n]
                        pe.wait_ge(sem["turned_act"] if n % 2 else sem["turned_dve"], n // 2 + 1)
                        pe.wait_ge(sem["v_ready"], 4 * j + b // 2 + 1)
                        if n >= 2:
                            pe.wait_ge(sem["added"], n - 1)
                        for qt in range(2):
                            for kt in range(2):
                                ins = pe.matmul(av[:, n % 2, qt * D:(qt + 1) * D], pT[:, n % TR, kt, qt * P:(qt + 1) * P],
                                                vp[:, j, 2 * b + kt, :], start=(kt == 0), stop=(kt == 1))
                        ins.then_inc(sem["av_ready"], 1)

            @block.scalar
            def _(act):
                chain = Link(act, sem["act_chain"])
                for item in order:
                    if item[0] == "VO":
                        j = item[1]
                        act.wait_ge(sem["wqk_odd"] if j else sem["wqk_even"], 32)
                        act.activation(bv_wide[:, j, :], cols[:, j, 2:3].broadcast_to([P, D]), ACT.Copy).then_inc(sem["rows_ready"], 1)
                        chain.step(act.mul(qb[:, j:j + 1], cols[:, j, 0:1], scale))
                        ready(act, item)
                        act.activation(vo[:, j, :], lin[:, turn[item][0], 0:D], ACT.Copy).then_inc(sem["vo_copied"], 1)
                        act.activation(bvo[:, j, :], lin[:, turn[item][0], D:2 * D], ACT.Copy).then_inc(sem["vo_copied"], 1)
                    elif item[0] == "P" and item[3] < 2:
                        _, j, g, i = item
                        ready(act, item)
                        act.activation(qk[:, j, i, g * PW:(g + 1) * PW], lin[:, turn[item][0], :], ACT.Identity,
                                       scale=1.0 if i else scale, bias=cols[:, j, 1:2] if i else qb[:, j:j + 1]
                                       ).then_inc(sem["q_ready"], 1)
                    elif item[0] == "SC":
                        n = item[1]
                        act.wait_ge(sem["max_ready"], n + 1)
                        if n >= 3:
                            act.wait_ge(sem["turned1"] if (n - 3) % 2 else sem["turned0"], (n - 3) // 2 + 1)
                        if n >= 4:
                            act.wait_ge(sem["added"], n - 3)
                        for qt in range(2):
                            ins = act.activation(probs[:, n % 3, qt, :], sc[:, n % 2, qt * S:(qt + 1) * S], ACT.Exp,
                                                 bias=nmax[:, n % 2, qt:qt + 1], accum_out=sums[:, n % 4, qt:qt + 1])
                        ins.then_inc(sem["exp_ready"], 1)
                    elif item[0] == "T" and item[1] % 2:
                        n = item[1]
                        act.wait_ge(sem["turned1"], n // 2 + 1)
                        if n >= TR:
                            act.wait_ge(sem["av_ready"], n - TR + 1)
                        act.activation(pT[:, n % TR].rearrange("p k q -> p (k q)"), tr[:, n % 2, :], ACT.Copy
                                       ).then_inc(sem["turned_act"], 1)

            @block.vector
            def _(dve):
                chain = Link(dve, sem["dve_chain"])
                for item in order:
                    if item[0] == "P" and item[3] == 2:
                        _, j, g, i = item
                        ready(dve, item)
                        dve.wait_ge(sem["vo_copied"], 2 * j + 2)
                        dve.tensor_tensor(vp[:, j, 4 * g:4 * g + 4, :], lin[:, turn[item][0], :].rearrange("p (a n) -> p a n", a=4),
                                          bc4(bvo[:, j, :]), ALU.add).then_inc(sem["v_ready"], 1)
                    elif item[0] == "SC":
                        n = item[1]
                        dve.wait_ge(sem["sc_ready"], n + 1)
                        if n >= 2:
                            dve.wait_ge(sem["exp_ready"], n - 1)
                        dve.tensor_reduce(nmax[:, n % 2, :], sc[:, n % 2, :].rearrange("p (a k) -> p a k", a=2), AX.X, ALU.max,
                                          negate=True).then_inc(sem["max_ready"], 1)
                    elif item[0] == "T" and item[1] % 2 == 0:
                        n = item[1]
                        dve.wait_ge(sem["turned0"], n // 2 + 1)
                        if n >= TR:
                            dve.wait_ge(sem["av_ready"], n - TR + 1)
                        dve.tensor_copy(pT[:, n % TR].rearrange("p k q -> p (k q)"), tr[:, n % 2, :]).then_inc(sem["turned_dve"], 1)
                    elif item[0] == "AV":
                        n = item[1]
                        j, b = units[n]
                        dve.wait_ge(sem["exp_ready"], n + 1)
                        if n >= 2:
                            dve.wait_ge(sem["added"], n - 1)
                        chain.step(dve.reciprocal(rsum[:, n % 2, :], sums[:, n % 4, :]))
                        dve.wait_ge(sem["av_ready"], n + 1)
                        if n >= B:
                            dve.wait_ge(sem["added"], n - B + 1)
                        for qt in range(2):
                            R = m.R[:, 2 * b + qt, :]
                            ins = dve.scalar_tensor_tensor(out=R, in0=av[:, n % 2, qt * D:(qt + 1) * D],
                                                           scalar=rsum[:, n % 2, qt:qt + 1], in1=R, op0=ALU.mult, op1=ALU.add)
                        ins.then_inc(sem["added"], 1)
        settle()


ROUTE_SEMS = "loaded mean_ready r1_ready r1_copied r2_ready hot_ready spread_ready spread_copied chosen dve_chain".split()
OPTIONS = 3
RH = 32


def choose_attention(nc, m, t, sem, settle, banks, stack):
    def sb(name, shape, dt=F32):
        return stack.enter_context(nc.sbuf_tensor(name, shape, dt))

    rw1, rb1, rw2 = sb("r_w1", [P, RH]), sb("r_b1", [RH, 1]), sb("r_w2", [RH, OPTIONS])
    rows = sb("r_rows", [P, 2, OPTIONS])
    wall = sb("wall", [P, OPTIONS, 4 * D])
    mean, r1 = sb("r_mean", [P, B]), sb("r1", [RH, B])
    lg, key, hot = sb("r_lg", [B, OPTIONS]), sb("r_key", [B, OPTIONS]), sb("r_hot", [B, OPTIONS])
    top, diag, ones = sb("r_top", [B, 2]), sb("r_diag", [B, B, OPTIONS]), sb("r_ones", [B, P])
    spread = sb("r_spread", [P, B, OPTIONS])
    loads = ((rw1[:, :], t.all["L1_ffn_r_w1"]), (rb1[:, :], t.all["L1_ffn_r_b1"].rearrange("(p a) -> p a", a=1)),
             (rw2[:, :], t.all["L1_ffn_r_w2"]), (rows[:, :, :], t.all["route_rows"].broadcast_to([P, 2, OPTIONS])),
             (wall[:, :, :], t.all["gqa_w"]))
    with nc.Block() as block:
        @block.sync
        def _(sp):
            for dst, src in loads:
                sp.dma_start(dst, src).then_inc(sem["loaded"], 16)

        @block.vector
        def _(dve):
            chain = Link(dve, sem["dve_chain"])
            dve.memset(ones[:, :], 1.0)
            chain.step(dve.tensor_reduce(mean[:, :], m.xT[:, :].rearrange("p (b s) -> p b s", b=B), AX.X, ALU.add))
            dve.tensor_scalar(mean[:, :], mean[:, :], 1.0 / S, None, ALU.mult).then_inc(sem["mean_ready"], 1)
            dve.wait_ge(sem["loaded"], 16 * len(loads))
            dve.wait_ge(sem["r1_ready"], 1)
            dve.tensor_scalar(r1[:, :], banks[0:RH, 0, 0:B], rb1[:, 0:1], 0.0, ALU.add, ALU.max).then_inc(sem["r1_copied"], 1)
            dve.wait_ge(sem["r2_ready"], 1)
            chain.step(dve.tensor_tensor(lg[:, :], banks[0:B, 1, 0:OPTIONS], rows[0:B, 0, :], ALU.add))
            chain.step(dve.tensor_reduce(top[:, 0:1], lg[:, :], AX.X, ALU.max))
            chain.step(dve.tensor_scalar(key[:, :], lg[:, :], top[:, 0:1], None, ALU.is_equal))
            chain.step(dve.tensor_tensor(key[:, :], key[:, :], rows[0:B, 1, :], ALU.mult))
            chain.step(dve.tensor_reduce(top[:, 1:2], key[:, :], AX.X, ALU.max))
            chain.step(dve.tensor_scalar(hot[:, :], key[:, :], top[:, 1:2], None, ALU.is_equal))
            dve.tensor_tensor(diag[:, :, :], m.ident[0:B, 0:B].unsqueeze(2).broadcast_to([B, B, OPTIONS]),
                              hot[:, :].unsqueeze(1).broadcast_to([B, B, OPTIONS]), ALU.mult).then_inc(sem["hot_ready"], 1)
            dve.wait_ge(sem["spread_ready"], 1)
            chain.step(dve.tensor_copy(spread[:, :, :].rearrange("p b o -> p (b o)"), banks[:, 2, 0:B * OPTIONS]))
            for o in range(OPTIONS):
                for b in range(B):
                    dst = m.wsel[:, b].rearrange("p i n -> p (i n)")
                    if o == 0:
                        ins = dve.tensor_scalar(dst, wall[:, o, :], spread[:, b, o:o + 1], None, ALU.mult)
                    else:
                        ins = dve.scalar_tensor_tensor(out=dst, in0=wall[:, o, :], scalar=spread[:, b, o:o + 1], in1=dst,
                                                       op0=ALU.mult, op1=ALU.add)
                chain.step(ins)

        @block.tensor
        def _(pe):
            pe.wait_ge(sem["loaded"], 16 * len(loads))
            pe.wait_ge(sem["mean_ready"], 1)
            pe.matmul(banks[0:RH, 0, 0:B], rw1[:, :], mean[:, :], start=True, stop=True).then_inc(sem["r1_ready"], 1)
            pe.wait_ge(sem["r1_copied"], 1)
            pe.matmul(banks[0:B, 1, 0:OPTIONS], r1[:, :], rw2[:, :], start=True, stop=True).then_inc(sem["r2_ready"], 1)
            pe.wait_ge(sem["hot_ready"], 1)
            pe.matmul(banks[:, 2, 0:B * OPTIONS], ones[:, :], diag[:, :, :].rearrange("p b o -> p (b o)"), start=True, stop=True
                      ).then_inc(sem["spread_ready"], 1)
    settle()


def chosen_attention(nc, m, t, sem, settle, banks, stack, out):
    attention_memory(nc, m, banks, stack, "g_")
    with nc.Block() as block:
        @block.vector
        def _(dve):
            chain = Link(dve, sem["dve_chain"])
            chain.step(dve.memset(m.v[:, :, :, DK:SLOT], 0.0))
            dve.memset(m.v[:, :, :, DK:DK + 1], 1.0)

        @block.gpsimd
        def _(pool):
            pool.memset(m.packed[MROW:MROW + 3, 1, :, :, :], 1.0)
    settle()
    w = Names()
    w.q, w.k, w.v, w.o = [(lambda b, i=i: m.wsel[:, b, i, :]) for i in range(4)]
    emit_layer(nc, m, w, sem, ffn=False, out_dram=out.rearrange("(g b) (i p) d -> g p (b i) d", b=2, p=P))
    settle()




def bc4(row):
    return row.unsqueeze(1).broadcast_to([P, 4, D])


def counters(nc, stack, names):
    made = [(n, stack.enter_context(nc.semaphore(n))) for n in names]
    first, last = made[0][1].num, made[-1][1].num
    assert last - first == len(made) - 1
    return dict(made), range(first, last + 1)


LAYER_SEMS = ("gathered0 gathered1 gathered2 gathered3 w_proj w_rest w_vec w_bc lin_ready0 lin_ready1 q_ready split_done parts_stored packed0 packed1 packed2 "
              "v_ready max_scores max_taken mparts_done mrow_sb mstored mrow0 mrow1 scores_ready probs_ready av_done o_copied "
              "otok_ready oT_ready sum_ready stats_ready rstd_ready xhat_ready x1T_ready hid_act hid_dve xT_ready "
              "out_ready stored0 stored1 res_bo res_x1 res_x act_chain dve_chain pool_chain").split()


def build(nc, t, out):
    with ExitStack() as stack:
        def sb(name, shape, dt=F32):
            return stack.enter_context(nc.sbuf_tensor(name, shape, dt))

        names = list(dict.fromkeys(LAYER_SEMS + NORM_SEMS + NYS_SEMS + MOE_SEMS + WIDE_SEMS + ROUTE_SEMS))
        s, all_sems = counters(nc, stack, names)
        sem = dict(s)
        sem["lin_ready"] = [s["lin_ready0"], s["lin_ready1"]]
        sem["packed"] = [s["packed0"], s["packed1"], s["packed2"]]
        sem["mrow"] = [s["mrow0"], s["mrow1"]]
        sem["stored"] = [s["stored0"], s["stored1"]]
        sem["res"] = {"C1": s["res_bo"], "C4": s["res_x1"]}
        sem["res_out"] = {"C1": s["res_x1"], "C4": s["res_x"]}

        def settle():
            nc.all_engine_barrier(sems_to_clear=all_sems)

        m = Names()
        m.loads = []
        m.ident, m.identb, m.mhalf = sb("ident", [P, P]), sb("identb", [P, P], BF16), sb("mhalf", [P, 4])
        m.R, m.xT = sb("R", [P, TILES, D]), sb("xT", [P, TOK])
        m.rows, m.cols, m.wqkv = sb("rows", [P, 3, D]), sb("cols", [P, 2]), sb("wqkv", [P, 3 * DK])
        banks = stack.enter_context(nc.psum_tensor("banks", [P, 8, PW], F32))
        m.norm_scratch = (sb("n_stats", [P, 4, 6]), sb("n_mv", [P, 3, 4, 2]), sb("n_vareps", [P, 4]), sb("n_rstd", [P, 3, 4]))
        m.bank = [banks[:, 0, :], banks[:, 1, :]]
        with ExitStack() as small:
            tok_transformer(nc, m, t, sem, settle, banks, small)
        m.T, m.X = sb("T", [P, TILES, D]), sb("X", [P, TILES, D])
        m.loads = [(m.rows[:, :, :], t.attn_rows.broadcast_to([P, 3, D])), (m.cols[:, :], t.attn_cols),
                   (m.wqkv[:, :], t.all["L0_attn_w_qkv"])]
        emit_norms(nc, m, sem, ("F", "X", "N"), res=m.rows[:, 2, :], final=(m.rows[:, 0, :], m.rows[:, 1, :]),
                   affine=(m.cols[:, 0:1], m.cols[:, 1:2]))
        settle()
        with ExitStack() as small:
            nystrom(nc, m, t, sem, settle, banks, small)
        m.loads = []
        emit_norms(nc, m, sem, ("X",), res="x", turn=False)
        settle()
        with ExitStack() as small:
            frequency_experts(nc, m, t, sem, settle, banks, small)
        m.loads = [(m.rows[:, 0:2, :], t.all["ffn_rows"].broadcast_to([P, 2, D]))]
        emit_norms(nc, m, sem, ("G", "X"), final=(m.rows[:, 0, :], m.rows[:, 1, :]))
        settle()
        with ExitStack() as small:
            wide_attention(nc, m, t, sem, settle, banks, small)
        m.loads = []
        emit_norms(nc, m, sem, ("X",))
        settle()
        m.wsel = sb("wsel", [P, B, 4, D])
        with ExitStack() as small:
            choose_attention(nc, m, t, sem, settle, banks, small)
        with ExitStack() as small:
            chosen_attention(nc, m, t, sem, settle, banks, small, out)


def attention_memory(nc, m, banks, stack, prefix):
    def sb(name, shape, dt=F32):
        return stack.enter_context(nc.sbuf_tensor(prefix + name, shape, dt))

    m.sbank = banks[:, 0:3, :]
    m.mbank = banks[:, 3:5, :]
    m.obank = banks[:, 5, :]
    m.lin = [banks[:, 6, :], banks[:, 7, :]]
    m.qf = sb("qf", [P, 2, 2, PW])
    m.parts = sb("parts", [P, 2, 2, 3, PW], BF16)
    m.rest = sb("rest", [P, PW])
    m.scratch = nc.dram_tensor(prefix + "qk_parts", [2, 3, P, TOK], BF16)
    m.max_scratch = nc.dram_tensor(prefix + "max_parts", [2, 3, H, S], BF16)
    m.packed = sb("packed", [P, 2, 3, H, PW], BF16)
    m.v = sb("v", [P, TILES, H, SLOT])
    m.nmax = sb("nmax", [P, 2, 2, H])
    m.mparts = sb("mparts", [P, 2, 2, 3 * H], BF16)
    m.mT = sb("mT", [P, 2, S], BF16)
    m.probs = sb("probs", [P, 6, PW])
    m.osb = sb("osb", [P, 2, PW])
    m.recip = sb("recip", [P, 2, 2 * H])
    m.otok = sb("otok", [P, 2, 2, D])
    m.oT = sb("oT", [P, 2, PW])
    m.rbuf = sb("rbuf", [P, 2, 4, D])


def tok_transformer(nc, m, t, sem, settle, banks, stack):
    def sb(name, shape, dt=F32):
        return stack.enter_context(nc.sbuf_tensor(name, shape, dt))

    attention_memory(nc, m, banks, stack, "t_")
    m.hidden = sb("hidden", [P, 4, PW])
    m.x1T = sb("x1T", [P, 2, PW])
    m.xhat = sb("xhat", [P, 2, 4, D])
    m.stats, m.mv = sb("stats", [P, 4, 6]), sb("mv", [P, 2, 4, 2])
    m.vareps, m.rstd = sb("vareps", [P, 4]), sb("rstd", [P, 2, 4])
    m.bq4, m.be1b2 = sb("bq4", [P, 1]), sb("be1b2", [P, D])
    wproj, wff1, wff2 = sb("wproj", [P, 4, D]), sb("wff1", [P, 4 * D]), sb("wff2", [P, 4, D])
    vec, bc = sb("vec", [P, 10]), sb("bc", [P, 7, D])
    ids, idf = sb("ids", [P, TILES], I32), sb("idf", [P, 2, TILES])
    pe_sb = sb("positions", [P, 2, D])

    gathered = [sem["gathered0"], sem["gathered1"], sem["gathered2"], sem["gathered3"]]
    with nc.Block() as block:
        @block.sync
        def _(sp):
            sp.dma_start(ids[:, :], t.ids).then_inc(sem["w_vec"], 16)
            sp.dma_start(m.ident[:, :], t.ident).then_inc(sem["w_proj"], 16)
            sp.dma_start(pe_sb[:, :, :], t.positions.rearrange("(i p) d -> p i d", p=P)).then_inc(sem["w_bc"], 16)

        @block.vector
        def _(dve):
            chain = Link(dve, sem["dve_chain"])
            dve.wait_ge(sem["w_vec"], 16)
            chain.step(dve.tensor_copy(idf[:, 0], ids[:, :]))
            chain.step(dve.tensor_scalar(idf[:, 1], idf[:, 0], 0.0, float(VOCAB), ALU.is_lt, ALU.mult))
            chain.step(dve.tensor_tensor(idf[:, 0], idf[:, 0], idf[:, 1], ALU.add))
            chain.step(dve.tensor_scalar(idf[:, 1], idf[:, 0], 0.0, float(VOCAB - 1), ALU.max, ALU.min))
            dve.tensor_copy(ids[:, :], idf[:, 1]).then_inc(sem["q_ready"], 1)
            dve.memset(m.v[:, :, :, DK:SLOT], 0.0).then_inc(sem["dve_chain"], 1)
            chain.n += 1
            chain.wait()
            dve.memset(m.v[:, :, :, DK:DK + 1], 1.0)
            dve.memset(m.packed[MROW:MROW + 3, 1, :, :, :], 1.0)
            dve.memset(m.mhalf[:, :], -0.5)
            dve.wait_ge(sem["w_proj"], 16)
            chain.step(dve.tensor_copy(m.identb[:, :], m.ident[:, :]))
            dve.wait_ge(sem["w_bc"], 16)
            for g in range(PAIRS):
                dve.wait_ge(gathered[g], 64)
                for b in range(2):
                    r = m.R[:, 4 * g + 2 * b:4 * g + 2 * b + 2, :]
                    ins = dve.tensor_tensor(r, r, pe_sb[:, :, :], ALU.add)
                ins.then_inc(sem["sum_ready"], 1)

        @block.gpsimd
        def _(pool):
            pool.wait_ge(sem["q_ready"], 1)
            for i in range(TILES):
                pool.indirect_dma_start(m.R[:, i, :], None, t.embed,
                                        bass.IndirectOffsetOnAxis(ap=ids[:, i:i + 1], axis=0)
                                        ).then_inc(gathered[i // 4], 16)

        @block.tensor
        def _(pe):
            pe.wait_ge(sem["w_proj"], 16)
            for g in range(PAIRS):
                pe.wait_ge(sem["sum_ready"], g + 1)
                if g >= 2:
                    pe.wait_ge(sem["xT_ready"], g - 1)
                for i in range(4):
                    ins = pe.transpose(m.lin[g % 2][:, i * P:(i + 1) * P], m.R[:, 4 * g + i, :], m.ident[:, :])
                ins.then_inc(sem["lin_ready"][0], 1)

        @block.scalar
        def _(act):
            for g in range(PAIRS):
                act.wait_ge(sem["lin_ready"][0], g + 1)
                act.activation(m.xT[:, g * PW:(g + 1) * PW], m.lin[g % 2], ACT.Copy).then_inc(sem["xT_ready"], 1)

    settle()
    w = Names()
    w.q, w.k, w.v, w.o = [(lambda b, i=i: wproj[:, i, :]) for i in range(4)]
    w.w1, w.w2 = wff1[:, :], wff2[:, :, :]
    w.bq, w.bk, w.g1, w.be1, w.g2, w.be2 = [vec[:, i:i + 1] for i in range(6)]
    w.b1 = vec[:, 6:10]
    w.bv_bc, w.bo_bc, w.b2_bc, w.g1_bc, w.be1_bc, w.g2_bc, w.be2_bc = [bc[:, i, :] for i in range(7)]
    with nc.Fori(0, LAYERS) as layer:
        at = bass.ds(layer, 1)

        def load(sp, sem):
            sp.dma_start(wproj[:, 0:3, :], t.tok_proj[at].rearrange("a p c n -> (a p) c n")[:, 0:3, :]
                         ).then_inc(sem["w_proj"], 16)
            sp.dma_start(vec[:, :], t.tok_cols[at].rearrange("a p n -> (a p) n")).then_inc(sem["w_vec"], 16)
            sp.dma_start(bc[:, :, :], t.tok_rows[at].broadcast_to([P, 7, D])).then_inc(sem["w_bc"], 16)
            sp.dma_start(wproj[:, 3, :], t.tok_proj[at].rearrange("a p c n -> (a p) c n")[:, 3, :]
                         ).then_inc(sem["w_rest"], 16)
            sp.dma_start(wff1[:, :], t.all["L0_tok_W1"][at].rearrange("a p n -> (a p) n")).then_inc(sem["w_rest"], 16)
            sp.dma_start(wff2[:, :, :], t.all["L0_tok_W2"][at].rearrange("a (c p) n -> p (a c) n", p=P)
                         ).then_inc(sem["w_rest"], 16)

        w.load = load
        emit_layer(nc, m, w, sem, ffn=True)
        settle()


_TOK_COLS = ("bq", "bk", "g1", "be1", "g2", "be2")
_TOK_ROWS = ("bv", "bo", "b2", "g1", "be1", "g2", "be2")


def shape_constants():
    import numpy as np
    import math
    pos = np.arange(S, dtype=np.float32)[:, None]
    div = np.exp(np.arange(0, D, 2, dtype=np.float32) * np.float32(-math.log(10000.0) / D)).astype(np.float32)
    ang = (pos * div).astype(np.float32)
    pe = np.zeros((S, D), np.float32)
    pe[:, 0::2], pe[:, 1::2] = np.sin(ang), np.cos(ang)
    return {"positions": pe, "ident": np.eye(P, dtype=np.float32)}


def kernel(**inputs):
    import numpy as _np
    import concourse.bacc as _bacc
    from concourse.bass_utils import run_bass_kernel_spmd as _run

    nc = _bacc.Bacc("TRN2", target_bir_lowering=False, num_devices=1)
    arrays = {k: _np.array(v) for k, v in inputs.items() if k != "x"}
    arrays["ids"] = _np.ascontiguousarray(_np.asarray(inputs["x"]).reshape(TILES, P).T)
    tok = {k[7:]: v for k, v in arrays.items() if k.startswith("L0_tok_")}
    arrays["tok_proj"] = _np.stack([tok[n] for n in ("Wq", "Wk", "Wv", "Wo")], axis=2)
    arrays["tok_cols"] = _np.concatenate([_np.stack([tok[n] for n in _TOK_COLS], axis=2),
                                          tok["b1"].reshape(LAYERS, 4, P).transpose(0, 2, 1)], axis=2)
    arrays["tok_rows"] = _np.stack([tok[n] for n in _TOK_ROWS], axis=1)
    arrays["attn_rows"] = _np.stack([tok["gf"], tok["bf"], arrays["L0_attn_b_out"]])[None]
    arrays["attn_cols"] = _np.stack([arrays["L0_attn_norm_gamma"], arrays["L0_attn_norm_beta"]], axis=1)
    taps = _np.zeros(4 * P, _np.float32)
    taps[2 * P - KSIZE // 2:2 * P + KSIZE // 2 + 1] = arrays["L0_attn_w_conv"].reshape(KSIZE)[::-1]
    arrays["taps"] = _np.stack([_np.stack([taps[(2 - kt) * P - p:(2 - kt) * P - p + S] for kt in range(2)])
                                for p in range(P)])
    arrays["router_rows"] = _np.stack([arrays["L0_ffn_router_b"], _np.arange(EXPERTS, 0, -1, dtype=_np.float32)])[None]
    arrays["ffn_b1"] = arrays["L0_ffn_b1"].reshape(EXPERTS, 4, P).transpose(0, 2, 1)
    arrays["ffn_rows"] = _np.stack([arrays["L0_ffn_ln_g"], arrays["L0_ffn_ln_b"]])[None]
    arrays.update(shape_constants())
    arrays.update(moe_constants())
    arrays["l1_qk"] = _np.stack([arrays["L1_attn_Wq"], arrays["L1_attn_Wk"]], axis=2)
    arrays["l1_cols"] = _np.stack([arrays["L1_attn_b" + n] for n in "qkv"], axis=2)
    arrays["l1_vT"] = arrays["L1_attn_Wv"].transpose(0, 2, 1)
    arrays["l1_o"] = arrays["L1_attn_Wo"].reshape(WH, D, D)
    arrays["route_rows"] = _np.stack([arrays["L1_ffn_r_b2"], _np.arange(OPTIONS, 0, -1, dtype=_np.float32)])[None]
    wide = lambda a: a.reshape(D, -1, 1, DK).repeat(D // a.shape[1], axis=2).reshape(D, D)
    arrays["gqa_w"] = _np.stack([_np.concatenate([arrays[f"L1_ffn_wq{i}"], wide(arrays[f"L1_ffn_wk{i}"]),
                                                  wide(arrays[f"L1_ffn_wv{i}"]), arrays[f"L1_ffn_wo{i}"]], axis=1)
                                 for i in range(OPTIONS)], axis=1)
    arrays = {k: _np.ascontiguousarray(v) for k, v in arrays.items()}
    aps = {k: nc.dram_tensor("in_" + k, v.shape, mybir.dt.from_np(v.dtype), kind="ExternalInput").ap()
           for k, v in arrays.items()}
    t = Names()
    t.ids, t.ident, t.positions, t.embed = aps["ids"], aps["ident"], aps["positions"], aps["L0_tok_embed"]
    t.tok_proj, t.tok_cols, t.tok_rows = aps["tok_proj"], aps["tok_cols"], aps["tok_rows"]
    t.attn_rows, t.attn_cols, t.taps, t.all = aps["attn_rows"], aps["attn_cols"], aps["taps"], aps
    out = nc.dram_tensor("out", (B, S, D), F32, kind="ExternalOutput").ap()
    build(nc, t, out)
    r = _run(nc, [{"in_" + k: v for k, v in arrays.items()}], core_ids=[0])
    return r.results[0]["out"]
```

```python
from contextlib import ExitStack

import concourse.bass as bass
from concourse import mybir



class Names:
    pass


F32 = mybir.dt.float32
BF16 = mybir.dt.bfloat16
I32 = mybir.dt.int32
ACT = mybir.ActivationFunctionType
ALU = mybir.AluOpType
AX = mybir.AxisListType

P = 128
B, S, D = 8, 256, 128
TOK = B * S
TILES = TOK // P
PAIRS = B // 2
PW = 2 * S
H, DK = 8, 16
SLOT = 32
EPS = 1e-5
LAYERS = 4
VOCAB = 8000
QPARTS = (0, 0, 0, 1, 1, 2)
KPARTS = (0, 1, 2, 0, 1, 0)
NG = len(QPARTS)
MROW = NG * DK


class Link:

    def __init__(self, eng, sem):
        self.eng, self.sem, self.n = eng, sem, 0

    def mark(self, ins):
        ins.then_inc(self.sem, 1)
        self.n += 1
        return self.n

    def wait(self, n=None):
        self.eng.wait_ge(self.sem, self.n if n is None else n)

    def step(self, ins):
        self.mark(ins)
        self.wait()


def bank_turns(order, uses):
    turns, n = {}, 0
    for item in order:
        for key in uses(item):
            turns[key] = (n % 2, n // 2)
            n += 1
    return turns


def step_items(b, ffn, first, last):
    end, pairs = (B, PAIRS) if last else (3 * B, 3 * PAIRS)
    extra = {u: [] for u in range(8)}
    if b % 2 == 0 and b // 2 + 2 < pairs:
        extra[4 if ffn else 0].append(("A", b // 2 + 2))
        extra[6 if ffn else 1].append(("V", b // 2 + 2))
    if b + 1 < end:
        extra[1].append(("MT", b + 1))
        extra[4].append(("ML", b + 1))
    if not (first and b < 1) and b - 1 < end:
        extra[2].append(("T1", b - 1))
        extra[4].append(("T2", b - 1))
    g = b // 2 - 1
    if b % 2 == 0 and not (first and g < 0) and g < pairs:
        extra[6].append(("C1", g))
    if ffn and b % 2 == 0 and not (first and g < 1) and g - 1 < pairs:
        extra[1].insert(0, ("N", "C4", g - 1))
        extra[3].append(("C5", g - 1))
    g = (b - 3) // 2
    if ffn and b % 2 == 1 and not (first and g < 0) and g < pairs:
        extra[0].append(("N", "C1", g))
        extra[3].append(("C2", g))
        for c, u in enumerate((5, 5, 6, 6)):
            extra[u].append(("C3", g, c))
        extra[7].append(("C4", g))
    items = []
    for u in range(8):
        if b < end:
            items.append(("S", b, u))
            if b + 2 < end:
                items.append(("M", b + 2, u))
            if u % 2 == 1 and u >= 3:
                items.append(("AV", b, u // 2 - 1))
        items += extra[u]
    if b < end:
        items += [("AV", b, 3), ("O", b)]
    return items


TURN_AT = 4


def layer_start(ffn, steps):
    order = [("A", 0), ("V", 0), ("A", 1), ("V", 1)]
    order += [("M", 0, u) for u in range(8)] + [("MT", 0), ("ML", 0)]
    order += [("M", 1, u) for u in range(8)]
    return order + [x for b in range(steps) for x in step_items(b, ffn, True, not ffn)]


def layer_turn():
    return [x for b in range(TURN_AT, TURN_AT + B) for x in step_items(b, True, False, False)]


def layer_end():
    return [x for b in range(TURN_AT, B + 3) for x in step_items(b, True, False, True)]


def bank_uses(item):
    kind, at = item[0], item[1]
    if kind == "A":
        return [("Aq", at), ("Ak", at)]
    if kind == "C3":
        return [item]
    if kind in ("V", "MT", "T1", "T2", "C1", "C2", "C4", "C5"):
        return [(kind, at)]
    return []


def emit_stages(nc, m, w, sem, ffn, order, out_dram=None):
    turn = bank_turns(order, bank_uses)
    at_turn = {v: k for k, v in turn.items()}
    index, made = {}, {}
    for item in order:
        kind = item[:2] if item[0] == "N" else item[0]
        index[item] = made.get(kind, 0)
        made[kind] = index[item] + 1
    norms = [x for x in order if x[0] in ("C1", "C4")]
    ln_index = {key: n for n, key in enumerate(norms)}
    applied = {(x[1], x[2]): n for n, x in enumerate(y for y in order if y[0] == "N")}
    slot = {"C1": 0, "C4": 1}
    turned = {"C1": "C2", "C4": "C5"}
    parity = {}
    for item in order:
        if item[0] == "MT":
            parity[item] = sum(1 for x in parity if x[1] % 2 == item[1] % 2)
    halves = [(0, PW, 0)] if ffn else [(0, S, 0), (S, S, 1)]

    def lin(key):
        return m.lin[turn[key][0]]

    def bank_ready(eng, key):
        if key in turn:
            bank, n = turn[key]
            eng.wait_ge(sem["lin_ready"][bank], n + 1)

    def done(eng, name, key, each=1, more=0):
        if key in index:
            eng.wait_ge(sem[name], each * (index[key] + 1) - more)

    def read_out(key):
        kind, at = key[0], key[1]
        if kind == "Aq":
            return sem["q_ready"], 4 * index[("A", at)] + 2
        if kind == "Ak":
            return sem["q_ready"], 4 * index[("A", at)] + 4
        if kind == "V":
            return sem["v_ready"], index[("V", at)] + 1
        if kind == "C3":
            return (sem["hid_dve"] if key[2] % 2 else sem["hid_act"]), index[key] // 2 + 1
        if kind in ("C1", "C4") and ffn:
            return sem["sum_ready"], ln_index[(kind, at)] + 1
        return {"MT": sem["mrow_sb"], "T1": sem["otok_ready"], "T2": sem["oT_ready"], "C1": sem["out_ready"],
                "C2": sem["x1T_ready"], "C5": sem["xT_ready"]}[kind], index[(kind, at)] + 1

    def bank_free(eng, key):
        bank, n = turn[key]
        if n:
            eng.wait_ge(*read_out(at_turn[(bank, n - 1)]))

    with nc.Block() as block:

        @block.sync
        def _(sp):
            stored = [0]

            def pack(g, t):
                sp.wait_ge(sem["split_done"], 2 * index[("A", g)] + t + 1)
                cols = slice((g % PAIRS) * PW, (g % PAIRS + 1) * PW)
                sp.dma_start(m.scratch[t, :, :, cols].rearrange("a p n -> p a n"), m.parts[:, t, g % 2]
                             ).then_inc(sem["parts_stored"], 16)
                stored[0] += 16
                sp.wait_ge(sem["parts_stored"], stored[0])
                if t == 0:
                    done(sp, "av_done", ("AV", 2 * (g - PAIRS) + 1, 3))
                for i, part in enumerate(KPARTS if t else QPARTS):
                    sp.dma_start(m.packed[i * DK:(i + 1) * DK, t, g % PAIRS],
                                 m.scratch[t, part, :, cols].rearrange("(h d) n -> d h n", h=H)
                                 ).then_inc(sem["packed"][g % PAIRS], 16)

            if ffn:
                w.load_first(sp)
            for item in order:
                kind, at = item[0], item[1]
                if kind == "A":
                    pack(at, 0)
                    pack(at, 1)
                elif kind == "C1" and not ffn:
                    sp.wait_ge(sem["out_ready"], index[item] + 1)
                    sp.dma_start(out_dram[at], m.rbuf[:, at % 2]).then_inc(sem["stored"][at % 2], 16)
                elif kind == "C4" and at == PAIRS - 1 and ("C1", PAIRS) in index:
                    bank_ready(sp, ("C4", at))
                    w.load_products(sp)
                    sp.wait_ge(sem["res_x"], index[("N", "C4", at)] + 1)
                    sp.wait_ge(sem["xT_ready"], index[("C5", at)] + 1)
                    w.load_vectors(sp)
            if not ffn:
                for i in range(2):
                    sp.wait_ge(sem["stored"][i], 16 * (PAIRS // 2))
            for item in order:
                if item[0] == "A":
                    sp.wait_ge(sem["packed"][item[1] % PAIRS], 16 * 2 * NG)
            for i in range(2):
                n = sum(1 for x in parity if x[1] % 2 == i)
                if n:
                    sp.wait_ge(sem["mrow"][i], 16 * n)
            if ffn:
                for name, n in w.loading:
                    sp.wait_ge(sem[name], 16 * n)

        @block.tensor
        def _(pe):
            def use(key):
                bank_free(pe, key)
                return lin(key)

            def filled(key, ins):
                ins.then_inc(sem["lin_ready"][turn[key][0]], 1)

            for item in order:
                kind, at = item[0], item[1]
                if kind == "A":
                    g = at % PAIRS
                    if at == w.first_pair:
                        pe.wait_ge(sem["w_proj"], 16)
                    if not ffn:
                        pe.wait_ge(sem["weights_chosen"], at + 1)
                    done(pe, "xT_ready", ("C5", at - PAIRS))
                    for key, wt in ((("Aq", at), w.q), (("Ak", at), w.k)):
                        bank = use(key)
                        for c0, cn, hb in halves:
                            ins = pe.matmul(bank[:, c0:c0 + cn], wt(2 * g + hb),
                                            m.xT[:, g * PW + c0:g * PW + c0 + cn], start=True, stop=True)
                        filled(key, ins)
                elif kind == "V":
                    g = at % PAIRS
                    bank = use(("V", at))
                    for i in range(4):
                        ins = pe.matmul(bank[:, i * P:(i + 1) * P], m.xT[:, g * PW + i * P:g * PW + (i + 1) * P],
                                        w.v(2 * g + i // 2), start=True, stop=True)
                    filled(("V", at), ins)
                elif kind == "M":
                    b, u = at, item[2]
                    g, n, qt = b // 2, index[item], u // 4
                    c = (b % 2) * S
                    if u == 0 and ("A", g) in index:
                        pe.wait_ge(sem["packed"][g % PAIRS], 16 * 2 * NG)
                    if n >= 3:
                        pe.wait_ge(sem["max_taken"], n - 2)
                    for i in range(2):
                        h = 2 * (u % 4) + i
                        ins = pe.matmul(m.mbank[:, n % 3, i * S:(i + 1) * S],
                                        m.packed[0:MROW, 0, g % PAIRS, h, c + qt * P:c + (qt + 1) * P],
                                        m.packed[0:MROW, 1, g % PAIRS, h, c:c + S], start=True, stop=True)
                    ins.then_inc(sem["max_scores"], 1)
                elif kind == "MT":
                    key = ("MT", at)
                    bank = use(key).bitcast(BF16)
                    if ("M", at, 7) in index:
                        pe.wait_ge(sem["mparts_done"], index[("M", at, 7)] // 8 + 1)
                    for qt in range(2):
                        ins = pe.transpose(bank[0:3 * H, qt * P:(qt + 1) * P], m.mparts[:, at % 2, qt, :],
                                           m.identb[:, :])
                    filled(key, ins)
                elif kind == "S":
                    b, u = at, item[2]
                    g, n = b // 2, index[item]
                    hq, kt, hp = u // 4, (u // 2) % 2, u % 2
                    c = (b % 2) * S
                    if u == 0 and ("MT", b) in parity:
                        pe.wait_ge(sem["mrow"][b % 2], 16 * (parity[("MT", b)] + 1))
                    if n >= 2:
                        pe.wait_ge(sem["probs_ready"], n - 1)
                    for i in range(2):
                        h = 4 * hq + 2 * hp + i
                        ins = pe.matmul(m.sbank[:, n % 2, i * S:(i + 1) * S],
                                        m.packed[0:MROW + 3, 1, g % PAIRS, h, c + kt * P:c + (kt + 1) * P],
                                        m.packed[0:MROW + 3, 0, g % PAIRS, h, c:c + S], start=True, stop=True)
                    ins.then_inc(sem["scores_ready"], 1)
                elif kind == "AV":
                    b, j = at, item[2]
                    hq, kt = j // 2, j % 2
                    n = index[("S", b, 2 * j)]
                    pe.wait_ge(sem["probs_ready"], n + 2)
                    if j == 0:
                        done(pe, "v_ready", ("V", b // 2))
                        done(pe, "o_copied", ("O", b - 1))
                    for i in range(4):
                        ins = pe.matmul(m.obank[SLOT * i:SLOT * (i + 1), hq * S:(hq + 1) * S],
                                        m.v[:, (2 * b + kt) % TILES, 4 * hq + i, :],
                                        m.probs[:, (n + i // 2) % 6, (i % 2) * S:(i % 2 + 1) * S],
                                        start=(kt == 0), stop=(kt == 1))
                    ins.then_inc(sem["av_done"], 1)
                elif kind == "T1":
                    key = ("T1", at)
                    bank = use(key)
                    done(pe, "o_copied", ("O", at))
                    for qt in range(2):
                        for hq in range(2):
                            c = (2 * qt + hq) * P
                            ins = pe.transpose(bank[:, c:c + P], m.osb[:, at % 2, hq * S + qt * P:hq * S + (qt + 1) * P],
                                               m.ident[:, :])
                    filled(key, ins)
                elif kind == "T2":
                    key = ("T2", at)
                    bank = use(key)
                    pe.wait_ge(sem["otok_ready"], index[("T1", at)] + 1)
                    for qt in range(2):
                        ins = pe.transpose(bank[:, qt * P:(qt + 1) * P], m.otok[:, at % 2, qt, :], m.ident[:, :])
                    filled(key, ins)
                elif kind == "C1":
                    key = ("C1", at)
                    bank = use(key)
                    done(pe, "oT_ready", ("T2", 2 * at + 1))
                    if at == w.first_sum:
                        pe.wait_ge(sem["w_rest"], 16 * 3)
                    for i in range(4):
                        ins = pe.matmul(bank[:, i * P:(i + 1) * P], m.oT[:, at % 2, i * P:(i + 1) * P],
                                        w.o(2 * at + i // 2), start=True, stop=True)
                    filled(key, ins)
                elif kind in ("C2", "C5"):
                    norm = "C1" if kind == "C2" else "C4"
                    key = (kind, at)
                    bank = use(key)
                    pe.wait_ge(sem["xhat_ready"], applied[(norm, at)] + 1)
                    for i in range(4):
                        ins = pe.transpose(bank[:, i * P:(i + 1) * P], m.xhat[:, slot[norm], i, :], m.ident[:, :])
                    filled(key, ins)
                elif kind == "C3":
                    c = item[2]
                    pe.wait_ge(sem["x1T_ready"], index[("C2", at)] + 1)
                    bank = use(item)
                    filled(item, pe.matmul(bank[:, :], w.w1[:, c * P:(c + 1) * P], m.x1T[:, at % 2, :],
                                           start=True, stop=True))
                elif kind == "C4":
                    key = ("C4", at)
                    bank = use(key)
                    pe.wait_ge(sem["hid_act"], 2 * index[item] + 2)
                    pe.wait_ge(sem["hid_dve"], 2 * index[item] + 2)
                    for i in range(4):
                        for c in range(4):
                            ins = pe.matmul(bank[:, i * P:(i + 1) * P], m.hidden[:, c, i * P:(i + 1) * P], w.w2[:, c, :],
                                            start=(c == 0), stop=(c == 3))
                    filled(key, ins)

        @block.scalar
        def _(act):
            chain = Link(act, sem["act_chain"])

            for item in order:
                kind, at = item[0], item[1]
                if kind == "A":
                    g = at
                    if g == w.first_pair:
                        act.wait_ge(sem["w_vec"], 16)
                        chain.step(act.mul(m.bq4[:, :], w.bq, DK ** -0.5))
                    for t, key in enumerate((("Aq", g), ("Ak", g))):
                        bank_ready(act, key)
                        done(act, "split_done", ("A", g - 2), 2, 1 - t)
                        done(act, "parts_stored", ("A", g - 2), 32, 16 * (1 - t))
                        scale = DK ** -0.5 if t == 0 else 1.0
                        bias = (m.bq4[:, 0:1] if t == 0 else w.bk) if ffn else 0.0
                        fn = ACT.Identity if ffn else ACT.Copy
                        act.activation(m.qf[:, t, g % 2], lin(key)[:, :], fn, bias=bias, scale=scale
                                       ).then_inc(sem["q_ready"], 1)
                        ins = act.activation(m.parts[:, t, g % 2, 0], lin(key)[:, :], fn, bias=bias, scale=scale)
                        ins.then_inc(sem["q_ready"], 1)
                elif kind == "MT":
                    key = ("MT", at)
                    bank_ready(act, key)
                    done(act, "mstored", ("MT", at - 2), 16)
                    act.activation(m.mT[0:3 * H, at % 2, :], lin(key).bitcast(BF16)[0:3 * H, 0:S], ACT.Copy
                                   ).then_inc(sem["mrow_sb"], 1)
                    act.wait_ge(sem["mrow_sb"], index[item] + 1)
                    act.dma_start(m.max_scratch[at % 2].rearrange("a h n -> (a h) n"), m.mT[0:3 * H, at % 2, :]
                                  ).then_inc(sem["mstored"], 16)
                elif kind == "ML":
                    b = at
                    act.wait_ge(sem["mstored"], 16 * (index[item] + 1))
                    act.dma_start(m.packed[MROW:MROW + 3, 0, (b // 2) % PAIRS, :, (b % 2) * S:(b % 2 + 1) * S],
                                  m.max_scratch[b % 2]).then_inc(sem["mrow"][b % 2], 16)
                elif kind == "S":
                    n = index[item]
                    act.wait_ge(sem["scores_ready"], n + 1)
                    if n >= 6:
                        act.wait_ge(sem["av_done"], (n - 6) // 2 + 1)
                    act.activation(m.probs[:, n % 6, :], m.sbank[:, n % 2, :], ACT.Exp).then_inc(sem["probs_ready"], 1)
                elif kind == "O":
                    act.wait_ge(sem["av_done"], 4 * index[item] + 4)
                    bank_ready(act, ("T1", at - 2))
                    act.activation(m.osb[:, at % 2, :], m.obank[:, :], ACT.Copy).then_inc(sem["o_copied"], 1)
                elif kind == "T2":
                    key = ("T2", at)
                    bank_ready(act, key)
                    if at % 2 == 0:
                        bank_ready(act, ("C1", at // 2 - 2))
                    act.activation(m.oT[:, (at // 2) % 2, (at % 2) * S:(at % 2 + 1) * S], lin(key)[:, 0:S], ACT.Copy
                                   ).then_inc(sem["oT_ready"], 1)
                elif kind == "C2":
                    key = ("C2", at)
                    if at == w.first_sum:
                        act.wait_ge(sem["w_rows"], 32)
                    bank_ready(act, key)
                    bank_ready(act, ("C3", at - 2, 3))
                    act.activation(m.x1T[:, at % 2, :], lin(key)[:, :], ACT.Identity, bias=w.be1, scale=w.g1
                                   ).then_inc(sem["x1T_ready"], 1)
                elif kind == "C3" and item[2] % 2 == 0:
                    c = item[2]
                    bank_ready(act, item)
                    bank_ready(act, ("C4", at - 1))
                    act.activation(m.hidden[:, c, :], lin(item)[:, :], ACT.Relu, bias=w.b1[:, c:c + 1]
                                   ).then_inc(sem["hid_act"], 1)
                elif kind == "C5":
                    key = ("C5", at)
                    bank_ready(act, key)
                    bank_ready(act, ("V", at))
                    g = at % PAIRS
                    act.activation(m.xT[:, g * PW:(g + 1) * PW], lin(key)[:, :], ACT.Identity, bias=w.be2, scale=w.g2
                                   ).then_inc(sem["xT_ready"], 1)

        @block.vector
        def _(dve):
            chain = Link(dve, sem["dve_chain"])
            if not ffn:
                w.choose(dve, chain, 0)

            def norm(key):
                g, k, n = key[1] % PAIRS, slot[key[0]], ln_index[key]
                bank_ready(dve, key)
                if key[0] == "C1":
                    done(dve, "res_bo", ("A", key[1]))
                else:
                    done(dve, "res_x1", ("N", "C1", key[1]))
                r = m.rbuf[:, k].rearrange("p a d -> p (a d)")
                if (key[0], key[1] - 1) in applied:
                    dve.wait_ge(sem["xhat_ready"], applied[(key[0], key[1] - 1)] + 1)
                dve.tensor_tensor(r, lin(key)[:, :], m.R[:, 4 * g:4 * g + 4, :].rearrange("p a d -> p (a d)"),
                                  ALU.add).then_inc(sem["sum_ready"], 1)
                dve.wait_ge(sem["sum_ready"], n + 1)
                for i in range(4):
                    ins = dve.bn_stats(m.stats[:, i, :], m.rbuf[:, k, i, :])
                chain.step(ins)
                for i in range(4):
                    ins = dve.bn_aggr(m.mv[:, k, i, :], m.stats[:, i, :])
                ins.then_inc(sem["stats_ready"], 1)
                dve.wait_ge(sem["stats_ready"], n + 1)

            def apply(kind, at):
                k = slot[kind]
                if (kind, at) in ln_index:
                    dve.wait_ge(sem["rstd_ready"], ln_index[(kind, at)] + 1)
                bank_ready(dve, (turned[kind], at - 1))
                done(dve, "res_x1" if kind == "C1" else "res_x", ("N", kind, at - 1))
                for i in range(4):
                    ins = dve.tensor_scalar(m.xhat[:, k, i, :], m.rbuf[:, k, i, :], m.mv[:, k, i, 0:1],
                                            m.rstd[:, k, i:i + 1], ALU.subtract, ALU.mult)
                ins.then_inc(sem["xhat_ready"], 1)

            for item in order:
                kind, at = item[0], item[1]
                if kind == "A":
                    for t in range(2):
                        dve.wait_ge(sem["q_ready"], 4 * index[item] + 2 * t + 2)
                        done(dve, "parts_stored", ("A", at - 2), 32, 16 * (1 - t))
                        parts = m.parts[:, t, at % 2]
                        dve.tensor_tensor(parts[:, 1], m.qf[:, t, at % 2], parts[:, 0], ALU.subtract
                                          ).then_inc(sem["second_part"], 1)
                elif kind == "V":
                    if not ffn and at + 1 < PAIRS:
                        w.choose(dve, chain, at + 1)
                    key = ("V", at)
                    bank_ready(dve, key)
                    if at == w.first_pair:
                        dve.wait_ge(sem["w_bc"], 16)
                    done(dve, "av_done", ("AV", 2 * (at - PAIRS) + 1, 3))
                    out = m.v[:, 4 * (at % PAIRS):4 * (at % PAIRS) + 4, :, 0:DK]
                    src = lin(key)[:, :].rearrange("p (a h d) -> p a h d", a=4, h=H)
                    if ffn:
                        for i in range(4):
                            ins = dve.tensor_tensor(out[:, i], src[:, i], w.bv_bc.rearrange("p (h d) -> p h d", h=H), ALU.add)
                    else:
                        for i in range(4):
                            ins = dve.tensor_copy(out[:, i], src[:, i])
                    ins.then_inc(sem["v_ready"], 1)
                elif kind == "M":
                    b, u = at, item[2]
                    n = index[item]
                    dve.wait_ge(sem["max_scores"], n + 1)
                    hp = u % 4
                    dve.tensor_reduce(m.nmax[:, b % 2, u // 4, 2 * hp:2 * hp + 2],
                                      m.mbank[:, n % 3, :].rearrange("p (i k) -> p i k", i=2),
                                      AX.X, ALU.max, negate=True).then_inc(sem["max_taken"], 1)
                    if u == 7:
                        nm, mp = m.nmax[:, b % 2], m.mparts[:, b % 2]
                        dve.wait_ge(sem["max_taken"], n + 1)
                        bank_ready(dve, ("MT", b - 2))
                        chain.step(dve.tensor_copy(mp[:, :, 0:H], nm))
                        chain.step(dve.tensor_tensor(nm, nm, mp[:, :, 0:H], ALU.subtract))
                        chain.step(dve.tensor_copy(mp[:, :, H:2 * H], nm))
                        dve.tensor_tensor(mp[:, :, 2 * H:3 * H], nm, mp[:, :, H:2 * H], ALU.subtract
                                          ).then_inc(sem["mparts_done"], 1)
                elif kind == "T1":
                    key = ("T1", at)
                    bank_ready(dve, key)
                    src = lin(key)[:, :].rearrange("p (a c) -> p a c", c=SLOT)
                    chain.step(dve.reciprocal(m.recip[:, at % 2], src[:, :, DK]))
                    bank_ready(dve, ("T2", at - 2))
                    dve.tensor_tensor(m.otok[:, at % 2].rearrange("p q (h d) -> p (q h) d", h=H), src[:, :, 0:DK],
                                      m.recip[:, at % 2].unsqueeze(2).broadcast_to([P, 2 * H, DK]), ALU.mult
                                      ).then_inc(sem["otok_ready"], 1)
                elif kind == "C1" and not ffn:
                    key = ("C1", at)
                    bank_ready(dve, key)
                    if at >= 2:
                        dve.wait_ge(sem["stored"][at % 2], 16 * (at // 2))
                    dve.tensor_tensor(m.rbuf[:, at % 2].rearrange("p a d -> p (a d)"), lin(key)[:, :],
                                      m.R[:, 4 * at:4 * at + 4, :].rearrange("p a d -> p (a d)"), ALU.add
                                      ).then_inc(sem["out_ready"], 1)
                elif kind in ("C1", "C4"):
                    norm((kind, at))
                elif kind == "N":
                    apply(item[1], item[2])
                elif kind == "C3" and item[2] % 2:
                    c = item[2]
                    if at == w.first_sum:
                        dve.wait_ge(sem["w_rows"], 32)
                    bank_ready(dve, item)
                    bank_ready(dve, ("C4", at - 1))
                    dve.tensor_scalar(m.hidden[:, c, :], lin(item)[:, :], w.b1[:, c:c + 1], 0.0, ALU.add, ALU.max
                                      ).then_inc(sem["hid_dve"], 1)

        @block.gpsimd
        def _(pool):
            chain = Link(pool, sem["pool_chain"])

            for item in order:
                kind, at = item[0], item[1]
                if kind == "A":
                    g, n = at, index[item]
                    for t in range(2):
                        qf, parts = m.qf[:, t, g % 2], m.parts[:, t, g % 2]
                        pool.wait_ge(sem["q_ready"], 4 * n + 2 * t + 2)
                        chain.step(pool.tensor_tensor(m.rest[:, :], qf, parts[:, 0], ALU.subtract))
                        pool.wait_ge(sem["second_part"], 2 * n + t + 1)
                        pool.tensor_tensor(parts[:, 2], m.rest[:, :], parts[:, 1], ALU.subtract
                                           ).then_inc(sem["split_done"], 1)
                        pool.wait_ge(sem["split_done"], 2 * n + t + 1)
                    if ffn:
                        if at == w.first_pair:
                            pool.wait_ge(sem["w_bc"], 16)
                        done(pool, "res_x", ("N", "C4", at - PAIRS))
                        R = m.R[:, 4 * (g % PAIRS):4 * (g % PAIRS) + 4, :]
                        pool.tensor_tensor(R, R, bc4(w.bo_bc), ALU.add).then_inc(sem["res_bo"], 1)
                elif ffn and kind in ("C1", "C4"):
                    n, k = ln_index[(kind, at)], slot[kind]
                    pool.wait_ge(sem["stats_ready"], n + 1)
                    if (kind, at - 1) in applied:
                        pool.wait_ge(sem["xhat_ready"], applied[(kind, at - 1)] + 1)
                    chain.step(pool.tensor_scalar(m.vareps[:, :], m.mv[:, k, :, 1], EPS, None, ALU.add))
                    pool.tensor_tensor(m.rstd[:, k, :], m.vareps[:, :], m.mhalf[:, :], ALU.pow
                                       ).then_inc(sem["rstd_ready"], 1)
                    pool.wait_ge(sem["rstd_ready"], n + 1)
                elif kind == "N":
                    kind, at = item[1:]
                    R = m.R[:, 4 * (at % PAIRS):4 * (at % PAIRS) + 4, :]
                    if kind == "C1" and at == w.first_sum:
                        pool.wait_ge(sem["w_rows"], 32)
                        chain.step(pool.tensor_tensor(m.be1b2[:, :], w.be1_bc, w.b2_bc, ALU.add))
                    g_bc, be_bc = (w.g1_bc, m.be1b2[:, :]) if kind == "C1" else (w.g2_bc, w.be2_bc)
                    pool.wait_ge(sem["xhat_ready"], applied[(kind, at)] + 1)
                    chain.step(pool.tensor_tensor(R, m.xhat[:, slot[kind]], bc4(g_bc), ALU.mult))
                    pool.tensor_tensor(R, R, bc4(be_bc), ALU.add).then_inc(sem["res_x1" if kind == "C1" else "res_x"], 1)


NORM_SEMS = ("stats_ready rstd_ready xhat_ready h_ready lin_ready0 lin_ready1 xT_ready bias_added sum_ready loaded loaded_ahead dve_chain "
             "pool_chain").split()


def emit_norms(nc, m, sem, kinds, res=None, final=None, affine=None, turn=True):
    items = [(k, step - 2 * lag) for step in range(PAIRS + 2 * len(kinds)) for lag, k in enumerate(kinds)
             if 0 <= step - 2 * lag < PAIRS]
    index = {item: n for n, item in enumerate(items)}
    group = lambda buf, g: buf[:, 4 * g:4 * g + 4, :]
    source = {"F": m.R, "G": m.X, "X": m.R, "N": m.X}
    dest = {"F": m.T, "G": m.T, "X": m.X, "N": m.T}
    last = kinds[-1]
    stats, mv, vareps, rstd, nmean = m.norm_scratch
    with nc.Block() as block:
        @block.sync
        def _(sp):
            for dst, src in m.loads:
                sp.dma_start(dst, src).then_inc(sem["loaded"], 16)
            for dst, src in m.loads_ahead:
                sp.dma_start(dst, src).then_inc(sem["loaded_ahead"], 16)
            if m.loads_ahead:
                sp.wait_ge(sem["loaded_ahead"], 16 * len(m.loads_ahead))

        @block.vector
        def _(dve):
            chain = Link(dve, sem["dve_chain"])

            def finish(n):
                k, g = items[n]
                if k == "X" and res is not None:
                    dve.wait_ge(sem["xhat_ready"], n + 1)
                    dve.tensor_tensor(group(m.R, g), group(m.R, g), group(m.X, g), ALU.add).then_inc(sem["sum_ready"], 1)
                if k not in ("F", "G"):
                    return
                T, R = group(m.T, g), group(m.R, g)
                dve.wait_ge(sem["loaded"], 16 * len(m.loads))
                dve.wait_ge(sem["xhat_ready"], n + 1)
                chain.step(dve.tensor_tensor(T, T, bc4(final[0]), ALU.mult))
                if k == "F":
                    dve.tensor_tensor(R, T, bc4(final[1]), ALU.add).then_inc(sem["h_ready"], 1)
                else:
                    dve.wait_ge(sem["bias_added"], g + 1)
                    dve.tensor_tensor(R, R, T, ALU.add).then_inc(sem["h_ready"], 1)

            for n, (k, g) in enumerate(items):
                if k == "X" and len(kinds) > 1:
                    dve.wait_ge(sem["h_ready"], g + 1)
                if k == "N":
                    dve.wait_ge(sem["xhat_ready"], index[("X", g)] + 1)
                if n >= 3:
                    dve.wait_ge(sem["xhat_ready"], n - 2)
                for i in range(4):
                    ins = dve.bn_stats(stats[:, i, :], group(source[k], g)[:, i])
                chain.step(ins)
                for i in range(4):
                    ins = dve.bn_aggr(mv[:, n % 3, i, :], stats[:, i, :])
                chain.step(ins)
                dve.tensor_scalar(vareps[:, n % 3, :], mv[:, n % 3, :, 1], EPS, None, ALU.add)
                dve.tensor_scalar(nmean[:, n % 3, :], mv[:, n % 3, :, 0], -1.0, None, ALU.mult).then_inc(sem["stats_ready"], 1)
                if n:
                    finish(n - 1)
            finish(len(items) - 1)

        @block.gpsimd
        def _(pool):
            chain = Link(pool, sem["pool_chain"])
            pool.wait_ge(sem["loaded"], 16 * len(m.loads))

            def add_bias(g):
                pool.tensor_tensor(group(m.R, g), group(m.R, g), bc4(final[1]), ALU.add).then_inc(sem["bias_added"], 1)

            for n, (k, g) in enumerate(items):
                pool.wait_ge(sem["stats_ready"], n + 1)
                if n >= 3:
                    pool.wait_ge(sem["xhat_ready"], n - 2)
                chain.step(pool.tensor_tensor(rstd[:, n % 3, :], vareps[:, n % 3, :], m.mhalf[:, :], ALU.pow))
                pool.tensor_tensor(nmean[:, n % 3, :], nmean[:, n % 3, :], rstd[:, n % 3, :], ALU.mult
                                   ).then_inc(sem["rstd_ready"], 1)
                if k == "G":
                    add_bias(g)
                if k == last and res is not None and res != "x":
                    R = group(m.R, g)
                    pool.wait_ge(sem["sum_ready"], g + 1)
                    pool.tensor_tensor(R, R, bc4(res), ALU.add)

        @block.tensor
        def _(pe):
            for g in range(PAIRS if turn else 0):
                pe.wait_ge(sem["xhat_ready"], index[(last, g)] + 1)
                if g >= 2:
                    pe.wait_ge(sem["xT_ready"], g - 1)
                for i in range(4):
                    ins = pe.transpose(m.bank[g % 2][:, i * P:(i + 1) * P], group(dest[last], g)[:, i], m.ident[:, :])
                ins.then_inc(sem["lin_ready0"], 1)

        @block.scalar
        def _(act):
            act.wait_ge(sem["loaded"], 16 * len(m.loads))

            def turn_out(g):
                act.wait_ge(sem["lin_ready0"], g + 1)
                out = m.xT[:, g * PW:(g + 1) * PW]
                if affine:
                    act.activation(out, m.bank[g % 2][:, :], ACT.Identity, scale=affine[0], bias=affine[1]
                                   ).then_inc(sem["xT_ready"], 1)
                else:
                    act.activation(out, m.bank[g % 2][:, :], ACT.Copy).then_inc(sem["xT_ready"], 1)

            for n, (k, g) in enumerate(items):
                act.wait_ge(sem["rstd_ready"], n + 1)
                if k == "N" and "F" in kinds:
                    act.wait_ge(sem["h_ready"], g + 1)
                for i in range(4):
                    ins = act.activation(group(dest[k], g)[:, i], group(source[k], g)[:, i], ACT.Identity,
                                         scale=rstd[:, n % 3, i:i + 1], bias=nmean[:, n % 3, i:i + 1])
                ins.then_inc(sem["xhat_ready"], 1)
                if turn and k == last and g:
                    turn_out(g - 1)
            if turn:
                turn_out(PAIRS - 1)


NYS_SEMS = ("loaded sums_ready toeplitz_loaded qk_ready qk_copied v_ready v_copied landmarks_ready sims_ready shifted exps a_ready "
            "turned turned_copied a3v_ready a3v_copied row_max all_max scaled z_step z_act z_dve w_ready w_copied "
            "outT_ready outT_copied y_ready y_added consts dve_chain pool_chain act_chain").split()
LM = 64
LG = S // LM
PINV_ITERS = 6
KSIZE = 33


def nystrom(nc, m, t, sem, settle, banks, stack):
    def sb(name, shape, dt=F32):
        return stack.enter_context(nc.sbuf_tensor(name, shape, dt))

    wqkv = m.wqkv
    qT, kT = sb("ny_q", [DK, TOK]), sb("ny_k", [DK, TOK])
    v = sb("ny_v", [P, PAIRS, 2, 2, DK])
    ql, kl = sb("ny_ql", [DK, B * LM]), sb("ny_kl", [DK, B * LM])
    a1, a3, a2 = sb("a1", [P, PAIRS, 2, 2, LM]), sb("a3", [P, PAIRS, S]), sb("a2", [P, PAIRS, LM])
    a1T, a3T = sb("a1T", [P, PAIRS, S]), sb("a3T", [P, PAIRS, 2, P])
    a2D, a2T = sb("a2D", [P, PAIRS, P]), sb("a2T", [P, PAIRS, P])
    z, zT, aT = sb("z", [P, PAIRS, P]), sb("zT", [P, PAIRS, P]), sb("aT", [P, PAIRS, P])
    u = sb("u", [P, 3, PAIRS, P])
    mx, sums = sb("ny_max", [P, 24]), sb("ny_sum", [P, 24])
    rowcol, allmax = sb("rowcol", [P, 10]), sb("allmax", [P, 4])
    a3v, wv = sb("a3v", [P, PAIRS, DK]), sb("wv", [P, PAIRS, 2 * DK])
    outT = sb("outT", [2 * DK, PAIRS, S])
    wout, toep = sb("wout", [2 * DK, 2, D]), sb("toep", [P, 2, S])
    eyes = sb("eyes", [P, 3, P])
    views = ((banks[:, 3, 0:PAIRS * LM].rearrange("p (g n) -> p g n", g=PAIRS), a2[:, :, :], 0, PAIRS),
             (banks[:, 4:6, :].rearrange("p b (g n) -> p (b g) n", g=2), a3[:, :, :], 4, PAIRS),
             (banks[:, 6:8, :].rearrange("p b (g n) -> p (b g) n", n=LM),
              a1[:, :, :, :, :].rearrange("p g k b n -> p (g k b) n"), 8, 4 * PAIRS))
    half = [slice(0, 2), slice(2, 4)]

    with nc.Block() as block:
        @block.sync
        def _(sp):
            sp.wait_ge(sem["consts"], 1)
            for i in range(2):
                sp.dma_start(wout[i * DK:(i + 1) * DK, i, :], t.all["L0_attn_w_out"]).then_inc(sem["loaded"], 16)
            sp.dma_start(toep[:, :, :], t.taps).then_inc(sem["toeplitz_loaded"], 16)

        @block.tensor
        def _(pe):
            for g in range(PAIRS):
                for i in range(2):
                    n = 2 * g + i
                    if n >= 2:
                        pe.wait_ge(sem["qk_copied"], n - 1)
                    pe.matmul(banks[0:DK, n % 2, :], wqkv[:, i * DK:(i + 1) * DK], m.xT[:, g * PW:(g + 1) * PW],
                              start=True, stop=True).then_inc(sem["qk_ready"], 1)
            for tile in range(TILES):
                g, b2, kt = tile // 4, (tile // 2) % 2, tile % 2
                c = ((g * 2 + kt) * 2 + b2) * DK
                ins = pe.matmul(banks[:, 2, c:c + DK], m.xT[:, tile * P:(tile + 1) * P], wqkv[:, 2 * DK:3 * DK],
                                start=True, stop=True)
            ins.then_inc(sem["v_ready"], 1)
            pe.wait_ge(sem["landmarks_ready"], 2)
            for b in range(B):
                g, b2 = b // 2, b % 2
                p0 = LM * b2
                ins = pe.matmul(banks[p0:p0 + LM, 3, g * LM:(g + 1) * LM], ql[:, b * LM:(b + 1) * LM], kl[:, b * LM:(b + 1) * LM],
                                start=True, stop=True)
            ins.then_inc(sem["sims_ready"], 1)
            for b in range(B):
                g, b2 = b // 2, b % 2
                p0 = LM * b2
                ins = pe.matmul(banks[p0:p0 + LM, 4 + g // 2, (g % 2) * S:(g % 2 + 1) * S], ql[:, b * LM:(b + 1) * LM],
                                kT[:, b * S:(b + 1) * S], start=True, stop=True)
            ins.then_inc(sem["sims_ready"], 1)
            for b in range(B):
                g, b2 = b // 2, b % 2
                for kt in range(2):
                    c = (g % 2) * 256 + kt * 128 + b2 * LM
                    ins = pe.matmul(banks[:, 6 + g // 2, c:c + LM], qT[:, b * S + kt * P:b * S + (kt + 1) * P],
                                    kl[:, b * LM:(b + 1) * LM], start=True, stop=True)
            ins.then_inc(sem["sims_ready"], 1)
            pe.wait_ge(sem["a_ready"], 1)
            for g in range(PAIRS):
                ins = pe.transpose(banks[:, 3, g * P:(g + 1) * P], a2D[:, g, :], m.ident[:, :])
            ins.then_inc(sem["turned"], 1)

            def product(bank, left, right, hf, sem_inc=None):
                for g in (2 * hf, 2 * hf + 1):
                    ins = pe.matmul(banks[:, bank, (g % 2) * P:(g % 2 + 1) * P], left[:, g, :], right[:, g, :],
                                    start=True, stop=True)
                return ins

            pe.wait_ge(sem["scaled"], 2)
            for it in range(PINV_ITERS):
                for step in range(4):
                    for hf in range(2):
                        n = 2 * (4 * it + step) + hf
                        if n >= 2:
                            pe.wait_ge(sem["z_dve"], n - 1)
                        if step in (0, 1) and (it or step):
                            pe.wait_ge(sem["z_act"], 2 * (2 * it + step) + hf - 1)
                        if step == 0:
                            product(2 * hf, a2T, z, hf)
                            ins = product(2 * hf + 1, z, a2T, hf)
                        elif step < 3:
                            ins = product(2 * hf, aT, u[:, step - 1], hf)
                        else:
                            product(2 * hf, zT, u[:, 2], hf)
                            ins = product(2 * hf + 1, u[:, 2], zT, hf)
                        ins.then_inc(sem["z_step"], 1)
                if it == 0:
                    pe.wait_ge(sem["a_ready"], 3)
                    pe.wait_ge(sem["v_copied"], 1)
                    for g in range(PAIRS):
                        for kt in range(2):
                            ins = pe.transpose(banks[:, 4 + g // 2, ((g % 2) * 2 + kt) * P:((g % 2) * 2 + kt + 1) * P],
                                               a3[:, g, kt * P:(kt + 1) * P], m.ident[:, :])
                    ins.then_inc(sem["turned"], 1)
                    for g in range(PAIRS):
                        for kt in range(2):
                            ins = pe.transpose(banks[:, 6 + g // 2, ((g % 2) * 2 + kt) * P:((g % 2) * 2 + kt + 1) * P],
                                               a1[:, g, kt].rearrange("p b l -> p (b l)"), m.ident[:, :])
                    ins.then_inc(sem["turned"], 1)
                if it == 1:
                    pe.wait_ge(sem["turned_copied"], 3)
                    for b in range(B):
                        g, p0 = b // 2, LM * (b % 2)
                        for kt in range(2):
                            ins = pe.matmul(banks[p0:p0 + LM, 4, g * DK:(g + 1) * DK], a3T[:, g, kt, p0:p0 + LM],
                                            v[:, g, kt, b % 2, :], start=(kt == 0), stop=(kt == 1))
                    ins.then_inc(sem["a3v_ready"], 1)
            pe.wait_ge(sem["a3v_copied"], 1)
            pe.wait_ge(sem["z_act"], 2 * 2 * PINV_ITERS)
            pe.wait_ge(sem["z_dve"], 2 * 4 * PINV_ITERS)
            for g in range(PAIRS):
                ins = pe.matmul(banks[:, 4, g * DK:(g + 1) * DK], zT[:, g, :], a3v[:, g, :], start=True, stop=True)
            ins.then_inc(sem["w_ready"], 1)
            pe.wait_ge(sem["w_copied"], 2)
            pe.wait_ge(sem["toeplitz_loaded"], 16)
            pe.wait_ge(sem["loaded"], 32)
            for g in range(PAIRS):
                if g >= 2:
                    pe.wait_ge(sem["outT_copied"], g - 1)
                bank = banks[0:2 * DK, g % 2, 0:S]
                pe.matmul(bank, wv[:, g, :], a1T[:, g, :], start=True, stop=False)
                for kt in range(2):
                    ins = pe.matmul(bank, v[:, g, kt].rearrange("p b d -> p (b d)"), toep[:, kt, :], start=False, stop=(kt == 1))
                ins.then_inc(sem["outT_ready"], 1)
            for g in range(PAIRS):
                pe.wait_ge(sem["outT_copied"], g + 1)
                if g >= 2:
                    pe.wait_ge(sem["y_added"], g - 1)
                for kt in range(2):
                    ins = pe.matmul(banks[:, 2 + g % 2, kt * 2 * P:(kt + 1) * 2 * P], outT[:, g, kt * P:(kt + 1) * P],
                                    wout[:, :, :].rearrange("p b d -> p (b d)"), start=True, stop=True)
                ins.then_inc(sem["y_ready"], 1)

        @block.scalar
        def _(act):
            for g in range(PAIRS):
                for i, (dst, scale) in enumerate(((qT, DK ** -0.5), (kT, 1.0))):
                    act.wait_ge(sem["qk_ready"], 2 * g + i + 1)
                    act.activation(dst[:, g * PW:(g + 1) * PW], banks[0:DK, i, :], ACT.Copy, scale=scale
                                   ).then_inc(sem["qk_copied"], 1)
            act.wait_ge(sem["v_ready"], 1)
            act.activation(v[:, :, :, :, :].rearrange("p a b c d -> p (a b c d)"), banks[:, 2, 0:TILES * DK], ACT.Copy
                           ).then_inc(sem["v_copied"], 1)
            for n, a in enumerate((a2[:, :, :], a3[:, :, :], a1[:, :, :, :, :])):
                act.wait_ge(sem["shifted"], n + 1)
                act.activation(a, a, ACT.Exp).then_inc(sem["exps"], 1)
            act.wait_ge(sem["turned"], 1)
            act.activation(a2T[:, :, :].rearrange("p g n -> p (g n)"), banks[:, 3, :], ACT.Copy).then_inc(sem["turned_copied"], 1)

            def copy_half(dst, hf, n):
                act.wait_ge(sem["z_step"], n)
                act.activation(dst[:, 2 * hf:2 * hf + 2, :].rearrange("p g n -> p (g n)"), banks[:, 2 * hf + 1, 0:2 * P],
                               ACT.Copy).then_inc(sem["z_act"], 1)

            for it in range(PINV_ITERS):
                for step, dst in ((0, aT), (3, zT)):
                    for hf in range(2):
                        copy_half(dst, hf, 2 * (4 * it + step) + hf + 1)
                if it == 0:
                    act.wait_ge(sem["turned"], 2)
                    act.activation(a3T[:, :, :, :].rearrange("p g k n -> p (g k n)"),
                                   banks[:, 4:6, :].rearrange("p b n -> p (b n)"), ACT.Copy).then_inc(sem["turned_copied"], 1)
                    act.wait_ge(sem["turned"], 3)
                    act.activation(a1T[:, :, :].rearrange("p g n -> p (g n)"),
                                   banks[:, 6:8, :].rearrange("p b n -> p (b n)"), ACT.Copy).then_inc(sem["turned_copied"], 1)
                if it == 1:
                    act.wait_ge(sem["a3v_ready"], 1)
                    act.activation(a3v[:, :, :].rearrange("p g d -> p (g d)"), banks[:, 4, 0:PAIRS * DK], ACT.Copy
                                   ).then_inc(sem["a3v_copied"], 1)
            act.wait_ge(sem["w_ready"], 1)
            act.wait_ge(sem["consts"], 1)
            for i in range(2):
                p0 = LM * i
                act.activation(wv[p0:p0 + LM, :, i * DK:(i + 1) * DK],
                               banks[p0:p0 + LM, 4, 0:PAIRS * DK].rearrange("p (g d) -> p g d", g=PAIRS), ACT.Copy
                               ).then_inc(sem["w_copied"], 1)
            for g in range(PAIRS):
                act.wait_ge(sem["outT_ready"], g + 1)
                act.activation(outT[:, g, :], banks[0:2 * DK, g % 2, 0:S], ACT.Copy).then_inc(sem["outT_copied"], 1)

        @block.gpsimd
        def _(pool):
            pool.memset(a2D[:, :, :], 0.0)
            pool.memset(wv[:, :, :], 0.0)
            pool.memset(wout[:, :, :], 0.0).then_inc(sem["consts"], 1)
            pool.wait_ge(sem["row_max"], 1)
            pool.partition_all_reduce(allmax[:, 0:2], rowcol[:, 8:10], P, bass.bass_isa.ReduceOp.max).then_inc(sem["all_max"], 1)
            for n in (1, 2):
                src, dst, c, G = views[n]
                pool.wait_ge(sem["exps"], n + 1)
                pool.wait_ge(sem["sums_ready"], n)
                pool.tensor_tensor(dst, dst, sums[:, c:c + G].unsqueeze(2).broadcast_to(list(dst.shape)), ALU.mult
                                   ).then_inc(sem["a_ready"], 1)

        @block.vector
        def _(dve):
            chain = Link(dve, sem["dve_chain"])
            for i, c in enumerate((7.0, 15.0, 3.25)):
                ins = dve.tensor_scalar(eyes[:, i, :], m.ident[:, :], c, None, ALU.mult)
            chain.step(ins)
            dve.wait_ge(sem["qk_copied"], 2 * PAIRS)
            for src, dst in ((qT, ql), (kT, kl)):
                chain.step(dve.tensor_reduce(dst[:, :], src[:, :].rearrange("p (n l) -> p n l", l=LG), AX.X, ALU.add))
                dve.tensor_scalar(dst[:, :], dst[:, :], 1.0 / LG, None, ALU.mult).then_inc(sem["landmarks_ready"], 1)
            def shift(n):
                src, dst, c, G = views[n]
                dve.wait_ge(sem["sims_ready"], n + 1)
                chain.step(dve.tensor_reduce(mx[:, c:c + G], src, AX.X, ALU.max))
                dve.tensor_tensor(dst, src, mx[:, c:c + G].unsqueeze(2).broadcast_to(list(dst.shape)), ALU.subtract
                                  ).then_inc(sem["shifted"], 1)

            def sum_up(n):
                src, dst, c, G = views[n]
                dve.wait_ge(sem["exps"], n + 1)
                chain.step(dve.tensor_reduce(sums[:, c:c + G], dst, AX.X, ALU.add))
                return dve.reciprocal(sums[:, c:c + G], sums[:, c:c + G])

            shift(0)
            shift(1)
            dve.wait_ge(sem["consts"], 1)
            chain.step(sum_up(0))
            for p0 in (0, LM):
                ins = dve.tensor_tensor(a2D[p0:p0 + LM, :, p0:p0 + LM], a2[p0:p0 + LM, :, :],
                                        sums[p0:p0 + LM, 0:PAIRS].unsqueeze(2).broadcast_to([LM, PAIRS, LM]), ALU.mult)
            ins.then_inc(sem["a_ready"], 1)
            shift(2)
            dve.wait_ge(sem["a_ready"], 1)
            ins = dve.tensor_reduce(rowcol[:, 0:4], a2D[:, :, :], AX.X, ALU.add, apply_absolute_value=True)
            dve.wait_ge(sem["turned_copied"], 1)
            chain.step(dve.tensor_reduce(rowcol[:, 4:8], a2T[:, :, :], AX.X, ALU.add, apply_absolute_value=True))
            ins = dve.tensor_reduce(rowcol[:, 8:10], rowcol[:, 0:8].rearrange("p (a b) -> p a b", a=2), AX.X, ALU.max)
            ins.then_inc(sem["row_max"], 1)
            for n in (1, 2):
                sum_up(n).then_inc(sem["sums_ready"], 1)
            dve.wait_ge(sem["all_max"], 1)
            chain.step(dve.tensor_tensor(allmax[:, 2:3], allmax[:, 0:1], allmax[:, 1:2], ALU.mult))
            chain.step(dve.reciprocal(allmax[:, 3:4], allmax[:, 2:3]))
            for src, dst in ((a2T, z), (a2D, zT)):
                dve.tensor_scalar(dst[:, :, :], src[:, :, :], allmax[:, 3:4], None, ALU.mult).then_inc(sem["scaled"], 1)

            def z_step(it, step, hf):
                n = 2 * (4 * it + step) + hf
                dve.wait_ge(sem["z_step"], n + 1)
                src = banks[:, 2 * hf, 0:2 * P].rearrange("p (g n) -> p g n", g=2)
                if step < 2:
                    dve.tensor_tensor(u[:, step, half[hf], :], eyes[:, step, :].unsqueeze(1).broadcast_to([P, 2, P]), src,
                                      ALU.subtract).then_inc(sem["z_dve"], 1)
                elif step == 2:
                    for j in range(2):
                        ins = dve.scalar_tensor_tensor(out=u[:, 2, 2 * hf + j, :], in0=src[:, j, :], scalar=-0.25,
                                                       in1=eyes[:, 2, :], op0=ALU.mult, op1=ALU.add)
                    ins.then_inc(sem["z_dve"], 1)
                else:
                    dve.tensor_copy(z[:, half[hf], :], src).then_inc(sem["z_dve"], 1)

            for it in range(PINV_ITERS):
                for step in range(4):
                    for hf in range(2):
                        z_step(it, step, hf)
            for g in range(PAIRS):
                dve.wait_ge(sem["y_ready"], g + 1)
                for kt in range(2):
                    R = m.R[:, 4 * g:4 * g + 4, :].rearrange("p (b k) d -> p k b d", k=2)[:, kt]
                    ins = dve.tensor_tensor(R, R, banks[:, 2 + g % 2, kt * 2 * P:(kt + 1) * 2 * P].rearrange("p (b d) -> p b d", b=2),
                                            ALU.add)
                ins.then_inc(sem["y_added"], 1)
    settle()


MOE_SEMS = ("loaded fwd_loaded rf_ready rf_copied h_psum hT_ready logits_ready chosen weights_exp gates_ready gates_turned gates_copied "
            "bias_ready bias_added experts_loaded w2_odd up_ready hid_ready down_ready down_added irf_ready irf_copied ot_ready ot_copied "
            "dve_chain pool_chain act_chain").split()
EXPERTS = 8
FREQ = S // 2 + 1
MT_ = B * P
MTOK = MT_ + B
MTILES = B + 1
CHUNKS = ((0, PW), (PW, PW), (2 * PW, B))


def frequency_experts(nc, m, t, sem, settle, banks, stack):
    def sb(name, shape, dt=F32):
        return stack.enter_context(nc.sbuf_tensor(name, shape, dt))

    fwd = sb("fwd", [P, 2, 2 * FREQ])
    xf = sb("xf", [P, 2, MTOK])
    hT = sb("hT", [P, MTILES * P])
    pin, rw, cols = sb("pin", [P, 2, P]), sb("rw", [P, EXPERTS]), sb("pin_b", [P, 1])
    rb, b2 = sb("rb", [P, 2, EXPERTS]), sb("b2", [EXPERTS, P])
    lg, oh1, oh2, key = (sb(n, [P, MTILES, EXPERTS]) for n in ("lg", "oh1", "oh2", "key"))
    gates = sb("gates", [P, EXPERTS, MTILES])
    top = sb("top", [P, 6, MTILES])
    gT = sb("gT", [EXPERTS, MTILES * P])
    acc = sb("acc", [P, MTILES, D])
    w1, w2, b1 = sb("w1", [P, 2, 4 * P]), sb("w2", [P, 2, 4, P]), sb("b1", [P, 2, 4])
    hid = sb("hid", [P, 2, 4, MTOK])
    inv, inv8 = sb("inv", [P, 2 * S]), sb("inv8", [B, B, S])
    pout, poutb, ramp = sb("pout", [P, 2, P]), sb("poutb", [2, P]), sb("ramp", [2, S])
    yT = sb("yT", [P, 2, 2 * S])

    def up_weights(j, expert):
        return ((w1[:, j, :], t.all["L0_ffn_w1"][expert].rearrange("a p n -> (a p) n")),
                (b1[:, j, :], t.all["ffn_b1"][expert].rearrange("a p n -> (a p) n")))

    def w2_weights(j, expert):
        return w2[:, j], t.all["L0_ffn_w2"][expert].rearrange("a (c p) n -> p (a c) n", p=P)

    with nc.Block() as block:
        @block.sync
        def _(sp):
            for dst, src in ((fwd[:, :, :], t.all["fwd"]), (pin[:, :, :], t.all["L0_ffn_pin_w"].rearrange("(r p) n -> p r n", p=P)),
                             (cols[:, :], t.all["L0_ffn_pin_b"].rearrange("(p a) -> p a", a=1)),
                             (rw[:, :], t.all["L0_ffn_router_w"]),
                             (rb[:, :, :], t.all["router_rows"].broadcast_to([P, 2, EXPERTS])),
                             (b2[:, :], t.all["L0_ffn_b2"]), (inv[:, :], t.all["inv"]), (inv8[:, :, :], t.all["inv8"]),
                             (pout[:, :, :], t.all["L0_ffn_pout_w"].rearrange("p (r n) -> p r n", r=2)),
                             (poutb[:, :], t.all["L0_ffn_pout_b"].rearrange("(r n) -> r n", r=2)), (ramp[:, :], t.all["ramp"])):
                sp.dma_start(dst, src).then_inc(sem["fwd_loaded" if src is t.all["fwd"] else "loaded"], 16)
            for j in range(2):
                for dst, src in up_weights(j, slice(j, j + 1)) + ((w2_weights(j, slice(j, j + 1)),) if j == 0 else ()):
                    sp.dma_start(dst, src).then_inc(sem["experts_loaded"], 16)
            sp.wait_ge(sem["experts_loaded"], 16 * 5)

        @block.tensor
        def _(pe):
            pe.wait_ge(sem["fwd_loaded"], 16)
            for b in range(B):
                if b >= 2:
                    pe.wait_ge(sem["rf_copied"], b - 1)
                for kt in range(2):
                    ins = pe.matmul(banks[:, b % 2, 0:2 * FREQ], m.X[:, 2 * b + kt, :], fwd[:, kt, :],
                                    start=(kt == 0), stop=(kt == 1))
                ins.then_inc(sem["rf_ready"], 1)
            pe.wait_ge(sem["rf_copied"], B)
            pe.wait_ge(sem["loaded"], 16 * 10)
            for c, (c0, cn) in enumerate(CHUNKS):
                for r in range(2):
                    ins = pe.matmul(banks[:, 2 + c, 0:cn], pin[:, r, :], xf[:, r, c0:c0 + cn], start=(r == 0), stop=(r == 1))
                ins.then_inc(sem["h_psum"], 1)
            pe.wait_ge(sem["hT_ready"], 4)
            for i in range(MTILES):
                ins = pe.matmul(banks[:, 5, i * EXPERTS:(i + 1) * EXPERTS], hT[:, i * P:(i + 1) * P], rw[:, :],
                                start=True, stop=True)
            ins.then_inc(sem["logits_ready"], 1)
            pe.wait_ge(sem["gates_ready"], 1)
            for i in range(MTILES):
                c = i * P
                ins = pe.transpose(banks[0:EXPERTS, c // PW, c % PW:c % PW + P], gates[:, :, i], m.ident[:, :])
            ins.then_inc(sem["gates_turned"], 1)
            pe.wait_ge(sem["gates_copied"], 1)
            for i in range(MTILES):
                c = i * P
                ins = pe.matmul(banks[:, 4 + c // PW, c % PW:c % PW + P], gT[:, i * P:(i + 1) * P], b2[:, :],
                                start=True, stop=True)
            ins.then_inc(sem["bias_ready"], 1)

        @block.scalar
        def _(act):
            for b in range(B):
                act.wait_ge(sem["rf_ready"], b + 1)
                src = banks[:, b % 2, 0:2 * FREQ].rearrange("p (r f) -> p r f", r=2)
                act.activation(xf[:, :, b * P:(b + 1) * P], src[:, :, 0:P], ACT.Copy)
                act.activation(xf[:, :, MT_ + b:MT_ + b + 1], src[:, :, P:P + 1], ACT.Copy).then_inc(sem["rf_copied"], 1)
            act.wait_ge(sem["loaded"], 16 * 10)
            for c, (c0, cn) in enumerate(CHUNKS):
                act.wait_ge(sem["h_psum"], c + 1)
                act.activation(hT[:, c0:c0 + cn], banks[:, 2 + c, 0:cn], ACT.Identity, bias=cols[:, 0:1]
                               ).then_inc(sem["hT_ready"], 1)
            act.wait_ge(sem["chosen"], 1)
            act.activation(top[:, 2, :], top[:, 2, :], ACT.Exp).then_inc(sem["weights_exp"], 1)
            act.wait_ge(sem["gates_turned"], 1)
            act.activation(gT[:, :], banks[0:EXPERTS, 0:3, :].rearrange("p b n -> p (b n)")[:, 0:MTILES * P], ACT.Copy
                           ).then_inc(sem["gates_copied"], 1)

        @block.gpsimd
        def _(pool):
            pool.memset(hT[:, MTOK:], 0.0).then_inc(sem["hT_ready"], 1)

        @block.vector
        def _(dve):
            chain = Link(dve, sem["dve_chain"])
            wide = lambda x: x.unsqueeze(2).broadcast_to([P, MTILES, EXPERTS])
            every = lambda x: x.unsqueeze(1).broadcast_to([P, MTILES, EXPERTS])
            dve.wait_ge(sem["logits_ready"], 1)
            dve.wait_ge(sem["loaded"], 16 * 10)
            chain.step(dve.tensor_tensor(lg[:, :, :], banks[:, 5, 0:MTILES * EXPERTS].rearrange("p (i e) -> p i e", e=EXPERTS),
                                         every(rb[:, 0, :]), ALU.add))
            for k, oh in enumerate((oh1, oh2)):
                chain.step(dve.tensor_reduce(top[:, k, :], lg[:, :, :], AX.X, ALU.max))
                chain.step(dve.tensor_tensor(key[:, :, :], lg[:, :, :], wide(top[:, k, :]), ALU.is_equal))
                chain.step(dve.tensor_tensor(key[:, :, :], key[:, :, :], every(rb[:, 1, :]), ALU.mult))
                chain.step(dve.tensor_reduce(top[:, 3, :], key[:, :, :], AX.X, ALU.max))
                chain.step(dve.tensor_tensor(oh[:, :, :], key[:, :, :], wide(top[:, 3, :]), ALU.is_equal))
                if k == 0:
                    chain.step(dve.scalar_tensor_tensor(out=lg[:, :, :], in0=oh[:, :, :], scalar=-3.0e38, in1=lg[:, :, :],
                                                        op0=ALU.mult, op1=ALU.add))
            dve.tensor_tensor(top[:, 2, :], top[:, 1, :], top[:, 0, :], ALU.subtract).then_inc(sem["chosen"], 1)
            dve.wait_ge(sem["weights_exp"], 1)
            chain.step(dve.tensor_scalar(top[:, 4, :], top[:, 2, :], 1.0, None, ALU.add))
            chain.step(dve.reciprocal(top[:, 4, :], top[:, 4, :]))
            chain.step(dve.tensor_tensor(top[:, 5, :], top[:, 2, :], top[:, 4, :], ALU.mult))
            chain.step(dve.tensor_tensor(oh1[:, :, :], oh1[:, :, :], wide(top[:, 4, :]), ALU.mult))
            chain.step(dve.tensor_tensor(oh2[:, :, :], oh2[:, :, :], wide(top[:, 5, :]), ALU.mult))
            dve.tensor_tensor(gates[:, :, :].rearrange("p e i -> p i e"), oh1[:, :, :], oh2[:, :, :], ALU.add
                              ).then_inc(sem["gates_ready"], 1)
            dve.wait_ge(sem["bias_ready"], 1)
            dve.tensor_copy(acc[:, :, :].rearrange("p i d -> p (i d)"),
                            banks[:, 4:7, :].rearrange("p b n -> p (b n)")[:, 0:MTILES * P]).then_inc(sem["bias_added"], 1)
    settle()

    def one(expert):
        return bass.ds(expert, 1)

    def turn_of_experts(even, odd, ahead):
        with nc.Block() as block:
            @block.sync
            def _(sp):
                sp.dma_start(*w2_weights(1, one(odd))).then_inc(sem["w2_odd"], 16)
                if ahead is not None:
                    for j in range(2):
                        sp.wait_ge(sem["hid_ready"], 9 * (j + 1))
                        for dst, src in up_weights(j, one(ahead[j])):
                            sp.dma_start(dst, src).then_inc(sem["experts_loaded"], 16)
                    sp.wait_ge(sem["down_ready"], 3)
                    sp.dma_start(*w2_weights(0, one(ahead[0]))).then_inc(sem["experts_loaded"], 16)
                    sp.wait_ge(sem["experts_loaded"], 16 * 5)
                sp.wait_ge(sem["w2_odd"], 16)

            @block.tensor
            def _(pe):
                def up(j):
                    for c in range(4):
                        for k in range(2):
                            n = 9 * j + 2 * c + k
                            if n >= 4:
                                pe.wait_ge(sem["hid_ready"], n - 3)
                            pe.matmul(banks[:, n % 4, :], w1[:, j, c * P:(c + 1) * P], hT[:, k * PW:(k + 1) * PW],
                                      start=True, stop=True).then_inc(sem["up_ready"], 1)
                    n = 9 * j + 8
                    pe.wait_ge(sem["hid_ready"], n - 3)
                    for c in range(4):
                        ins = pe.matmul(banks[:, n % 4, c * B:(c + 1) * B], w1[:, j, c * P:(c + 1) * P],
                                        hT[:, MT_:MTOK], start=True, stop=True)
                    ins.then_inc(sem["up_ready"], 1)

                def down(j):
                    pe.wait_ge(sem["hid_ready"], 9 * (j + 1))
                    for i in range(MTILES):
                        n = 3 * j + i // 4
                        if i % 4 == 0 and n >= 2:
                            pe.wait_ge(sem["down_added"], n - 1)
                        rows = P if i < B else B
                        out = banks[0:rows, 4 + n % 2, (i % 4) * P:(i % 4 + 1) * P]
                        for c in range(4):
                            ins = pe.matmul(out, hid[:, j, c, i * P:i * P + rows], w2[:, j, c, :], start=(c == 0), stop=(c == 3))
                        if i % 4 == 3 or i == B:
                            ins.then_inc(sem["down_ready"], 1)

                up(0)
                up(1)
                down(0)
                pe.wait_ge(sem["w2_odd"], 16)
                down(1)

            @block.scalar
            def _(act):
                for j in range(2):
                    for c in range(4):
                        for k in range(2):
                            n = 9 * j + 2 * c + k
                            act.wait_ge(sem["up_ready"], n + 1)
                            act.activation(hid[:, j, c, k * PW:(k + 1) * PW], banks[:, n % 4, :], ACT.Gelu,
                                           bias=b1[:, j, c:c + 1]).then_inc(sem["hid_ready"], 1)
                    n = 9 * j + 8
                    act.wait_ge(sem["up_ready"], n + 1)
                    for c in range(4):
                        ins = act.activation(hid[:, j, c, MT_:MTOK], banks[:, n % 4, c * B:(c + 1) * B], ACT.Gelu,
                                             bias=b1[:, j, c:c + 1])
                    ins.then_inc(sem["hid_ready"], 1)

            @block.vector
            def _(dve):
                for j in range(2):
                    for i in range(MTILES):
                        n = 3 * j + i // 4
                        if i % 4 == 0:
                            dve.wait_ge(sem["down_ready"], n + 1)
                            if j:
                                dve.wait_ge(sem["down_added"], n - 2)
                        rows = P if i < B else B
                        a = acc[0:rows, i, :]
                        ins = dve.scalar_tensor_tensor(out=a, in0=banks[0:rows, 4 + n % 2, (i % 4) * P:(i % 4 + 1) * P],
                                                       scalar=gates[0:rows, one((even, odd)[j]), i], in1=a,
                                                       op0=ALU.mult, op1=ALU.add)
                        if i % 4 == 3 or i == B:
                            ins.then_inc(sem["down_added"], 1)
        settle()

    with nc.Fori(0, EXPERTS // 2 - 1) as pair:
        turn_of_experts(2 * pair, 2 * pair + 1, (2 * pair + 2, 2 * pair + 3))
    turn_of_experts(EXPERTS - 2, EXPERTS - 1, None)

    with nc.Block() as block:
        @block.tensor
        def _(pe):
            def out_proj(b):
                pe.wait_ge(sem["irf_copied"], b + 1)
                if b % 2 == 0 and b >= 4:
                    pe.wait_ge(sem["ot_copied"], b // 2 - 1)
                for kt in range(2):
                    o = banks[:, 2 + (b // 2) % 2, ((b % 2) * 2 + kt) * P:((b % 2) * 2 + kt + 1) * P]
                    for r in range(2):
                        pe.matmul(o, yT[:, b % 2, r * S + kt * P:r * S + (kt + 1) * P], pout[:, r, :], start=(r == 0), stop=False)
                    ins = pe.matmul(o, ramp[:, kt * P:(kt + 1) * P], poutb[:, :], start=False, stop=True)
                if b % 2:
                    ins.then_inc(sem["ot_ready"], 1)

            for b in range(B):
                if b >= 2:
                    pe.wait_ge(sem["irf_copied"], b - 1)
                pe.matmul(banks[:, b % 2, 0:S], acc[:, b, :], inv[:, 0:S], start=True, stop=False)
                pe.matmul(banks[:, b % 2, 0:S], acc[0:B, B, :], inv8[:, b, :], start=False, stop=True)
                pe.matmul(banks[:, b % 2, S:], acc[:, b, :], inv[:, S:], start=True, stop=True).then_inc(sem["irf_ready"], 1)
                if b:
                    out_proj(b - 1)
            out_proj(B - 1)

        @block.scalar
        def _(act):
            for b in range(B):
                act.wait_ge(sem["irf_ready"], b + 1)
                if b >= 2 and b % 2 == 0:
                    act.wait_ge(sem["ot_ready"], b // 2)
                act.activation(yT[:, b % 2, :], banks[:, b % 2, :], ACT.Copy).then_inc(sem["irf_copied"], 1)

        @block.vector
        def _(dve):
            for g in range(PAIRS):
                dve.wait_ge(sem["ot_ready"], g + 1)
                dve.tensor_copy(m.X[:, 4 * g:4 * g + 4, :].rearrange("p i d -> p (i d)"), banks[:, 2 + g % 2, :]
                                ).then_inc(sem["ot_copied"], 1)
    settle()


def moe_constants():
    import numpy as np
    s, f = np.arange(S)[:, None], np.arange(FREQ)[None, :]
    turn = 2 * np.pi * ((s * f) % S) / S
    fwd = np.concatenate([np.cos(turn), -np.sin(turn)], axis=1) / np.sqrt(S)
    fwd[:, FREQ] = fwd[:, 2 * FREQ - 1] = 0.0
    twice = np.where((np.arange(FREQ) == 0) | (np.arange(FREQ) == S // 2), 1.0, 2.0)[:, None]
    cos, sin = twice * np.cos(turn.T) / np.sqrt(S), -twice * np.sin(turn.T) / np.sqrt(S)
    sin[0] = sin[-1] = 0.0
    inv8 = np.zeros((B, B, S))
    inv8[np.arange(B), np.arange(B)] = cos[-1]
    arrays = {"fwd": fwd.reshape(2, P, 2 * FREQ).transpose(1, 0, 2), "inv": np.concatenate([cos[:-1], sin[:-1]], axis=1),
              "inv8": inv8, "ramp": np.stack([cos.sum(0), sin.sum(0)])}
    return {k: np.ascontiguousarray(v.astype(np.float32)) for k, v in arrays.items()}


WIDE_SEMS = ("heads_loaded vo_copied lin_ready0 lin_ready1 q_ready v_ready sc_ready max_ready "
             "exp_ready turned0 turned1 turned_dve turned_act av_ready added rows_ready dve_chain pool_chain act_chain").split()
WH = 8
TR = 2


HEAD_LOADS = 4


def head_loads(t, m, j, head):
    return ((m.l1_wqk[:, j], t.all["l1_qk"][head].rearrange("a p i n -> (a p) i n")),
            (m.l1_cols[:, j, :], t.all["l1_cols"][head].rearrange("a p i -> (a p) i")),
            (m.l1_wvT[:, j], t.all["l1_vT"][head].rearrange("a p n -> (a p) n")),
            (m.l1_wo[:, j], t.all["l1_o"][head].rearrange("a p n -> (a p) n")))


def wide_attention(nc, m, t, sem, settle, banks, stack, last_loads):
    def sb(name, shape, dt=F32):
        return stack.enter_context(nc.sbuf_tensor(name, shape, dt))

    wqk, wvT, wo, cols = m.l1_wqk, m.l1_wvT, m.l1_wo, m.l1_cols
    qb = sb("l1_qb", [P, 2])
    vo, bv_wide, bvo = sb("vo", [P, 2, D]), sb("bv_wide", [P, 2, D]), sb("bvo", [P, 2, D])
    qk = sb("l1_qk", [P, 2, 2, TOK])
    vp = sb("vp", [P, 2, TILES, D])
    nmax, sums, rsum = sb("l1_nmax", [P, 2, 2]), sb("l1_sums", [P, 4, 2]), sb("l1_rsum", [P, 2, 2])
    probs, pT = sb("l1_probs", [P, 3, 2, S]), sb("l1_pT", [P, TR, 2, S])
    scale = float(D) ** -0.5

    def project_items(j):
        return [("VO", j)] + [("P", j, g, i) for g in range(PAIRS) for i in range(3)]

    units = [(j, b) for j in range(2) for b in range(B)]
    order = project_items(0)
    later = project_items(1)
    for n in range(len(units) + 2):
        if n < len(units):
            order.append(("SC", n))
        if 1 <= n <= len(units):
            order.append(("T", n - 1))
        if n >= 2:
            order.append(("AV", n - 2))
        for _ in range(2):
            if later and n >= 1:
                order.append(later.pop(0))
    assert not later
    uses = [x for x in order if x[0] in ("VO", "P")]
    turn = {key: (n % 2, n // 2) for n, key in enumerate(uses)}
    at_turn = {v: k for k, v in turn.items()}
    sc, tr, av, lin = banks[:, 0:2, :], banks[:, 2:4, :], banks[:, 4:6, :], banks[:, 6:8, :]

    def turn_of_heads(next_heads):
        def read_out(key):
            if key[0] == "VO":
                return sem["vo_copied"], 2 * key[1] + 2
            j, g, i = key[1:]
            return (sem["v_ready"], 4 * j + g + 1) if i == 2 else (sem["q_ready"], 8 * j + 2 * g + i + 1)

        def ready(eng, key):
            eng.wait_ge(sem["lin_ready0"] if turn[key][0] == 0 else sem["lin_ready1"], turn[key][1] + 1)

        with nc.Block() as block:
            @block.sync
            def _(sp):
                if next_heads is not None:
                    for j in range(2):
                        sp.wait_ge(sem["q_ready"], 8 * (j + 1))
                        sp.wait_ge(sem["vo_copied"], 2 * j + 2)
                        for dst, src in head_loads(t, m, j, next_heads[j]):
                            sp.dma_start(dst, src).then_inc(sem["heads_loaded"], 16)
                    sp.wait_ge(sem["heads_loaded"], 16 * 2 * HEAD_LOADS)
                else:
                    for dst, src in last_loads:
                        sp.dma_start(dst, src).then_inc(sem["heads_loaded"], 16)
                    sp.wait_ge(sem["heads_loaded"], 16 * len(last_loads))

            @block.gpsimd
            def _(pool):
                if next_heads is None:
                    pool.memset(m.packed[MROW:MROW + 3, 1, :, :, :], 1.0)

            @block.tensor
            def _(pe):
                def use(key):
                    bank, n = turn[key]
                    if n:
                        pe.wait_ge(*read_out(at_turn[(bank, n - 1)]))
                    return lin[:, bank, :]

                def filled(key, ins):
                    ins.then_inc(sem["lin_ready0"] if turn[key][0] == 0 else sem["lin_ready1"], 1)

                for item in order:
                    if item[0] == "VO":
                        j = item[1]
                        bank = use(item)
                        pe.matmul(bank[:, 0:D], wvT[:, j, :], wo[:, j, :], start=True, stop=True)
                        pe.wait_ge(sem["rows_ready"], j + 1)
                        filled(item, pe.matmul(bank[:, D:2 * D], bv_wide[:, j, :], wo[:, j, :], start=True, stop=True))
                    elif item[0] == "P":
                        _, j, g, i = item
                        bank = use(item)
                        if i < 2:
                            ins = pe.matmul(bank, wqk[:, j, i, :], m.xT[:, g * PW:(g + 1) * PW], start=True, stop=True)
                        else:
                            if g == 0:
                                pe.wait_ge(sem["vo_copied"], 2 * j + 2)
                            for a in range(4):
                                c = g * PW + a * P
                                ins = pe.matmul(bank[:, a * P:(a + 1) * P], m.xT[:, c:c + P], vo[:, j, :], start=True, stop=True)
                        filled(item, ins)
                    elif item[0] == "SC":
                        n = item[1]
                        j, b = units[n]
                        pe.wait_ge(sem["q_ready"], 8 * j + 2 * (b // 2) + 2)
                        if n >= 2:
                            pe.wait_ge(sem["exp_ready"], n - 1)
                        for qt in range(2):
                            c = b * S + qt * P
                            ins = pe.matmul(sc[:, n % 2, qt * S:(qt + 1) * S], qk[:, j, 0, c:c + P], qk[:, j, 1, b * S:(b + 1) * S],
                                            start=True, stop=True)
                        ins.then_inc(sem["sc_ready"], 1)
                    elif item[0] == "T":
                        n = item[1]
                        pe.wait_ge(sem["exp_ready"], n + 1)
                        if n >= 2:
                            pe.wait_ge(sem["turned_act"] if n % 2 else sem["turned_dve"], n // 2)
                        for kt in range(2):
                            for qt in range(2):
                                c = kt * S + qt * P
                                ins = pe.transpose(tr[:, n % 2, c:c + P], probs[:, n % 3, qt, kt * P:(kt + 1) * P], m.ident[:, :])
                        ins.then_inc(sem["turned1"] if n % 2 else sem["turned0"], 1)
                    else:
                        n = item[1]
                        j, b = units[n]
                        pe.wait_ge(sem["turned_act"] if n % 2 else sem["turned_dve"], n // 2 + 1)
                        pe.wait_ge(sem["v_ready"], 4 * j + b // 2 + 1)
                        if n >= 2:
                            pe.wait_ge(sem["added"], n - 1)
                        for qt in range(2):
                            for kt in range(2):
                                ins = pe.matmul(av[:, n % 2, qt * D:(qt + 1) * D], pT[:, n % TR, kt, qt * P:(qt + 1) * P],
                                                vp[:, j, 2 * b + kt, :], start=(kt == 0), stop=(kt == 1))
                        ins.then_inc(sem["av_ready"], 1)

            @block.scalar
            def _(act):
                chain = Link(act, sem["act_chain"])
                for item in order:
                    if item[0] == "VO":
                        j = item[1]
                        act.activation(bv_wide[:, j, :], cols[:, j, 2:3].broadcast_to([P, D]), ACT.Copy).then_inc(sem["rows_ready"], 1)
                        chain.step(act.mul(qb[:, j:j + 1], cols[:, j, 0:1], scale))
                        ready(act, item)
                        act.activation(vo[:, j, :], lin[:, turn[item][0], 0:D], ACT.Copy).then_inc(sem["vo_copied"], 1)
                        act.activation(bvo[:, j, :], lin[:, turn[item][0], D:2 * D], ACT.Copy).then_inc(sem["vo_copied"], 1)
                    elif item[0] == "P" and item[3] < 2:
                        _, j, g, i = item
                        ready(act, item)
                        act.activation(qk[:, j, i, g * PW:(g + 1) * PW], lin[:, turn[item][0], :], ACT.Identity,
                                       scale=1.0 if i else scale, bias=cols[:, j, 1:2] if i else qb[:, j:j + 1]
                                       ).then_inc(sem["q_ready"], 1)
                    elif item[0] == "SC":
                        n = item[1]
                        act.wait_ge(sem["max_ready"], n + 1)
                        if n >= 3:
                            act.wait_ge(sem["turned1"] if (n - 3) % 2 else sem["turned0"], (n - 3) // 2 + 1)
                        if n >= 4:
                            act.wait_ge(sem["added"], n - 3)
                        for qt in range(2):
                            ins = act.activation(probs[:, n % 3, qt, :], sc[:, n % 2, qt * S:(qt + 1) * S], ACT.Exp,
                                                 bias=nmax[:, n % 2, qt:qt + 1], accum_out=sums[:, n % 4, qt:qt + 1])
                        ins.then_inc(sem["exp_ready"], 1)
                    elif item[0] == "T" and item[1] % 2:
                        n = item[1]
                        act.wait_ge(sem["turned1"], n // 2 + 1)
                        if n >= TR:
                            act.wait_ge(sem["av_ready"], n - TR + 1)
                        act.activation(pT[:, n % TR].rearrange("p k q -> p (k q)"), tr[:, n % 2, :], ACT.Copy
                                       ).then_inc(sem["turned_act"], 1)

            @block.vector
            def _(dve):
                chain = Link(dve, sem["dve_chain"])
                for item in order:
                    if item[0] == "P" and item[3] == 2:
                        _, j, g, i = item
                        ready(dve, item)
                        dve.wait_ge(sem["vo_copied"], 2 * j + 2)
                        dve.tensor_tensor(vp[:, j, 4 * g:4 * g + 4, :], lin[:, turn[item][0], :].rearrange("p (a n) -> p a n", a=4),
                                          bc4(bvo[:, j, :]), ALU.add).then_inc(sem["v_ready"], 1)
                    elif item[0] == "SC":
                        n = item[1]
                        dve.wait_ge(sem["sc_ready"], n + 1)
                        if n >= 2:
                            dve.wait_ge(sem["exp_ready"], n - 1)
                        dve.tensor_reduce(nmax[:, n % 2, :], sc[:, n % 2, :].rearrange("p (a k) -> p a k", a=2), AX.X, ALU.max,
                                          negate=True).then_inc(sem["max_ready"], 1)
                    elif item[0] == "T" and item[1] % 2 == 0:
                        n = item[1]
                        dve.wait_ge(sem["turned0"], n // 2 + 1)
                        if n >= TR:
                            dve.wait_ge(sem["av_ready"], n - TR + 1)
                        dve.tensor_copy(pT[:, n % TR].rearrange("p k q -> p (k q)"), tr[:, n % 2, :]).then_inc(sem["turned_dve"], 1)
                    elif item[0] == "AV":
                        n = item[1]
                        j, b = units[n]
                        dve.wait_ge(sem["exp_ready"], n + 1)
                        if n >= 2:
                            dve.wait_ge(sem["added"], n - 1)
                        chain.step(dve.reciprocal(rsum[:, n % 2, :], sums[:, n % 4, :]))
                        dve.wait_ge(sem["av_ready"], n + 1)
                        if n >= B:
                            dve.wait_ge(sem["added"], n - B + 1)
                        for qt in range(2):
                            R = m.R[:, 2 * b + qt, :]
                            ins = dve.scalar_tensor_tensor(out=R, in0=av[:, n % 2, qt * D:(qt + 1) * D],
                                                           scalar=rsum[:, n % 2, qt:qt + 1], in1=R, op0=ALU.mult, op1=ALU.add)
                        ins.then_inc(sem["added"], 1)
        settle()

    with nc.Fori(0, WH // 2 - 1) as pair:
        turn_of_heads([bass.ds(2 * pair + 2 + j, 1) for j in range(2)])
    turn_of_heads(None)


ROUTE_SEMS = "mean_ready r1_ready r1_copied r2_ready hot_ready spread_ready weights_chosen route_chain".split()
OPTIONS = 3
RH = 32


def route_memory(nc, t, stack):
    r = Names()

    def sb(name, shape):
        return stack.enter_context(nc.sbuf_tensor(name, shape, F32))

    r.w1, r.b1, r.w2 = sb("r_w1", [P, RH]), sb("r_b1", [RH, 1]), sb("r_w2", [RH, OPTIONS])
    r.rows, r.wall = sb("r_rows", [P, 2, OPTIONS]), sb("wall", [P, OPTIONS, 4 * D])
    r.mean, r.r1 = sb("r_mean", [P, B]), sb("r1", [RH, B])
    r.lg, r.key, r.hot = sb("r_lg", [B, OPTIONS]), sb("r_key", [B, OPTIONS]), sb("r_hot", [B, OPTIONS])
    r.top, r.diag, r.ones = sb("r_top", [B, 2]), sb("r_diag", [B, B, OPTIONS]), sb("r_ones", [B, P])
    r.spread = sb("r_spread", [P, B, OPTIONS])
    r.loads = ((r.w1[:, :], t.all["L1_ffn_r_w1"]), (r.b1[:, :], t.all["L1_ffn_r_b1"].rearrange("(p a) -> p a", a=1)),
               (r.w2[:, :], t.all["L1_ffn_r_w2"]), (r.rows[:, :, :], t.all["route_rows"].broadcast_to([P, 2, OPTIONS])),
               (r.wall[:, :, :], t.all["gqa_w"]))
    return r


def choose_attention(nc, m, r, sem, banks):
    rb1, rw1, rw2, rows, mean, r1 = r.b1, r.w1, r.w2, r.rows, r.mean, r.r1
    lg, key, hot, top, diag, ones, spread = r.lg, r.key, r.hot, r.top, r.diag, r.ones, r.spread
    with nc.Block() as block:
        @block.vector
        def _(dve):
            chain = Link(dve, sem["route_chain"])
            dve.memset(ones[:, :], 1.0)
            chain.step(dve.tensor_reduce(mean[:, :], m.xT[:, :].rearrange("p (b s) -> p b s", b=B), AX.X, ALU.add))
            dve.tensor_scalar(mean[:, :], mean[:, :], 1.0 / S, None, ALU.mult).then_inc(sem["mean_ready"], 1)
            dve.wait_ge(sem["r1_ready"], 1)
            dve.tensor_scalar(r1[:, :], banks[0:RH, 0, 0:B], rb1[:, 0:1], 0.0, ALU.add, ALU.max).then_inc(sem["r1_copied"], 1)
            dve.wait_ge(sem["r2_ready"], 1)
            chain.step(dve.tensor_tensor(lg[:, :], banks[0:B, 1, 0:OPTIONS], rows[0:B, 0, :], ALU.add))
            chain.step(dve.tensor_reduce(top[:, 0:1], lg[:, :], AX.X, ALU.max))
            chain.step(dve.tensor_scalar(key[:, :], lg[:, :], top[:, 0:1], None, ALU.is_equal))
            chain.step(dve.tensor_tensor(key[:, :], key[:, :], rows[0:B, 1, :], ALU.mult))
            chain.step(dve.tensor_reduce(top[:, 1:2], key[:, :], AX.X, ALU.max))
            chain.step(dve.tensor_scalar(hot[:, :], key[:, :], top[:, 1:2], None, ALU.is_equal))
            dve.tensor_tensor(diag[:, :, :], m.ident[0:B, 0:B].unsqueeze(2).broadcast_to([B, B, OPTIONS]),
                              hot[:, :].unsqueeze(1).broadcast_to([B, B, OPTIONS]), ALU.mult).then_inc(sem["hot_ready"], 1)
            dve.wait_ge(sem["spread_ready"], 1)
            chain.step(dve.tensor_copy(spread[:, :, :].rearrange("p b o -> p (b o)"), banks[:, 2, 0:B * OPTIONS]))

        @block.scalar
        def _(act):
            act.activation(m.v[:, :, :, DK + 1:SLOT], m.ident[:, 0:1].unsqueeze(2).unsqueeze(3).broadcast_to([P, TILES, H, SLOT - DK - 1]),
                           ACT.Copy, scale=0.0)
            act.activation(m.v[:, :, :, DK:DK + 1], m.ident[:, 0:1].unsqueeze(2).unsqueeze(3).broadcast_to([P, TILES, H, 1]),
                           ACT.Copy, scale=0.0, bias=1.0)

        @block.tensor
        def _(pe):
            pe.wait_ge(sem["mean_ready"], 1)
            pe.matmul(banks[0:RH, 0, 0:B], rw1[:, :], mean[:, :], start=True, stop=True).then_inc(sem["r1_ready"], 1)
            pe.wait_ge(sem["r1_copied"], 1)
            pe.matmul(banks[0:B, 1, 0:OPTIONS], r1[:, :], rw2[:, :], start=True, stop=True).then_inc(sem["r2_ready"], 1)
            pe.wait_ge(sem["hot_ready"], 1)
            pe.matmul(banks[:, 2, 0:B * OPTIONS], ones[:, :], diag[:, :, :].rearrange("p b o -> p (b o)"), start=True, stop=True
                      ).then_inc(sem["spread_ready"], 1)


def chosen_attention(nc, m, r, sem, out):
    w = Names()
    w.q, w.k, w.v, w.o = [(lambda b, i=i: m.wsel[:, b, i, :]) for i in range(4)]
    w.first_pair, w.first_sum = None, None

    def choose(dve, chain, g):
        for o in range(OPTIONS):
            for b in (2 * g, 2 * g + 1):
                dst, scale = m.wsel[:, b].rearrange("p i n -> p (i n)"), r.spread[:, b, o:o + 1]
                if o == 0:
                    ins = dve.tensor_scalar(dst, r.wall[:, o, :], scale, None, ALU.mult)
                else:
                    ins = dve.scalar_tensor_tensor(out=dst, in0=r.wall[:, o, :], scalar=scale, in1=dst,
                                                   op0=ALU.mult, op1=ALU.add)
            if o < OPTIONS - 1:
                chain.step(ins)
            else:
                ins.then_inc(sem["weights_chosen"], 1)

    w.choose = choose
    emit_stages(nc, m, w, sem, False, layer_start(False, B + 1), out_dram=out.rearrange("(g b) (i p) d -> g p (b i) d", b=2, p=P))




def bc4(row):
    return row.unsqueeze(1).broadcast_to([P, 4, D])


def counters(nc, stack, names):
    made = [(n, stack.enter_context(nc.semaphore(n))) for n in names]
    first, last = made[0][1].num, made[-1][1].num
    assert last - first == len(made) - 1
    return dict(made), range(first, last + 1)


LAYER_SEMS = ("gathered0 gathered1 gathered2 gathered3 w_proj w_rest w_vec w_bc w_rows lin_ready0 lin_ready1 q_ready second_part split_done parts_stored packed0 packed1 packed2 packed3 "
              "v_ready max_scores max_taken mparts_done mrow_sb mstored mrow0 mrow1 scores_ready probs_ready av_done o_copied "
              "otok_ready oT_ready sum_ready stats_ready rstd_ready xhat_ready x1T_ready hid_act hid_dve xT_ready "
              "out_ready stored0 stored1 res_bo res_x1 res_x act_chain dve_chain pool_chain").split()


def build(nc, t, out):
    with ExitStack() as stack:
        def sb(name, shape, dt=F32):
            return stack.enter_context(nc.sbuf_tensor(name, shape, dt))

        names = list(dict.fromkeys(LAYER_SEMS + NORM_SEMS + NYS_SEMS + MOE_SEMS + WIDE_SEMS + ROUTE_SEMS))
        s, all_sems = counters(nc, stack, names)
        sem = dict(s)
        sem["lin_ready"] = [s["lin_ready0"], s["lin_ready1"]]
        sem["packed"] = [s["packed0"], s["packed1"], s["packed2"], s["packed3"]]
        sem["mrow"] = [s["mrow0"], s["mrow1"]]
        sem["stored"] = [s["stored0"], s["stored1"]]
        sem["res"] = {"C1": s["res_bo"], "C4": s["res_x1"]}
        sem["res_out"] = {"C1": s["res_x1"], "C4": s["res_x"]}

        def settle():
            nc.all_engine_barrier(sems_to_clear=all_sems)

        m = Names()
        m.loads, m.loads_ahead = [], []
        m.ident, m.identb, m.mhalf = sb("ident", [P, P]), sb("identb", [P, P], BF16), sb("mhalf", [P, 4])
        m.R, m.xT = sb("R", [P, TILES, D]), sb("xT", [P, TOK])
        m.rows, m.cols, m.wqkv = sb("rows", [P, 3, D]), sb("cols", [P, 2]), sb("wqkv", [P, 3 * DK])
        banks = stack.enter_context(nc.psum_tensor("banks", [P, 8, PW], F32))
        m.norm_scratch = (sb("n_stats", [P, 4, 6]), sb("n_mv", [P, 3, 4, 2]), sb("n_vareps", [P, 3, 4]), sb("n_rstd", [P, 3, 4]),
                          sb("n_nmean", [P, 3, 4]))
        m.bank = [banks[:, 0, :], banks[:, 1, :]]
        with ExitStack() as small:
            tok_transformer(nc, m, t, sem, settle, banks, small)
        m.T, m.X = sb("T", [P, TILES, D]), sb("X", [P, TILES, D])
        m.loads = [(m.rows[:, :, :], t.attn_rows.broadcast_to([P, 3, D])), (m.cols[:, :], t.attn_cols),
                   (m.wqkv[:, :], t.all["L0_attn_w_qkv"])]
        emit_norms(nc, m, sem, ("F", "X", "N"), res=m.rows[:, 2, :], final=(m.rows[:, 0, :], m.rows[:, 1, :]),
                   affine=(m.cols[:, 0:1], m.cols[:, 1:2]))
        settle()
        with ExitStack() as small:
            nystrom(nc, m, t, sem, settle, banks, small)
        m.loads = []
        emit_norms(nc, m, sem, ("X",), res="x", turn=False)
        settle()
        with ExitStack() as small:
            frequency_experts(nc, m, t, sem, settle, banks, small)
        m.loads = [(m.rows[:, 0:2, :], t.all["ffn_rows"].broadcast_to([P, 2, D]))]
        m.l1_wqk, m.l1_cols = sb("l1_wqk", [P, 2, 2, D]), sb("l1_cols", [P, 2, 3])
        m.l1_wvT, m.l1_wo = sb("l1_wvT", [P, 2, D]), sb("l1_wo", [P, 2, D])
        for j in range(2):
            m.loads_ahead += head_loads(t, m, j, slice(j, j + 1))
        emit_norms(nc, m, sem, ("G", "X"), final=(m.rows[:, 0, :], m.rows[:, 1, :]))
        settle()
        route = route_memory(nc, t, stack)
        m.packed = packed_memory(nc, stack, "g_")
        with ExitStack() as small:
            wide_attention(nc, m, t, sem, settle, banks, small, route.loads)
        m.loads, m.loads_ahead = [], []
        emit_norms(nc, m, sem, ("X",))
        settle()
        m.wsel = sb("wsel", [P, B, 4, D])
        attention_memory(nc, m, banks, stack, "g_")
        choose_attention(nc, m, route, sem, banks)
        chosen_attention(nc, m, route, sem, out)
        settle()


def packed_memory(nc, stack, prefix):
    return stack.enter_context(nc.sbuf_tensor(prefix + "packed", [P, 2, PAIRS, H, PW], BF16))


def attention_memory(nc, m, banks, stack, prefix):
    def sb(name, shape, dt=F32):
        return stack.enter_context(nc.sbuf_tensor(prefix + name, shape, dt))

    m.sbank = banks[:, 0:2, :]
    m.mbank = banks[:, 2:5, :]
    m.obank = banks[:, 5, :]
    m.lin = [banks[:, 6, :], banks[:, 7, :]]
    m.qf = sb("qf", [P, 2, 2, PW])
    m.parts = sb("parts", [P, 2, 2, 3, PW], BF16)
    m.rest = sb("rest", [P, PW])
    m.scratch = nc.dram_tensor(prefix + "qk_parts", [2, 3, P, TOK], BF16)
    m.max_scratch = nc.dram_tensor(prefix + "max_parts", [2, 3, H, S], BF16)
    m.v = sb("v", [P, TILES, H, SLOT])
    m.nmax = sb("nmax", [P, 2, 2, H])
    m.mparts = sb("mparts", [P, 2, 2, 3 * H], BF16)
    m.mT = sb("mT", [P, 2, S], BF16)
    m.probs = sb("probs", [P, 6, PW])
    m.osb = sb("osb", [P, 2, PW])
    m.recip = sb("recip", [P, 2, 2 * H])
    m.otok = sb("otok", [P, 2, 2, D])
    m.oT = sb("oT", [P, 2, PW])
    m.rbuf = sb("rbuf", [P, 2, 4, D])


def tok_transformer(nc, m, t, sem, settle, banks, stack):
    def sb(name, shape, dt=F32):
        return stack.enter_context(nc.sbuf_tensor(name, shape, dt))

    m.packed = packed_memory(nc, stack, "t_")
    attention_memory(nc, m, banks, stack, "t_")
    m.hidden = sb("hidden", [P, 4, PW])
    m.x1T = sb("x1T", [P, 2, PW])
    m.xhat = sb("xhat", [P, 2, 4, D])
    m.stats, m.mv = sb("stats", [P, 4, 6]), sb("mv", [P, 2, 4, 2])
    m.vareps, m.rstd = sb("vareps", [P, 4]), sb("rstd", [P, 2, 4])
    m.bq4, m.be1b2 = sb("bq4", [P, 1]), sb("be1b2", [P, D])
    wproj, wff1, wff2 = sb("wproj", [P, 4, D]), sb("wff1", [P, 4 * D]), sb("wff2", [P, 4, D])
    vec, bc = sb("vec", [P, 10]), sb("bc", [P, 7, D])
    ids, idf = sb("ids", [P, TILES], I32), sb("idf", [P, 2, TILES])
    pe_sb = sb("positions", [P, 2, D])

    gathered = [sem["gathered0"], sem["gathered1"], sem["gathered2"], sem["gathered3"]]
    with nc.Block() as block:
        @block.sync
        def _(sp):
            sp.dma_start(ids[:, :], t.ids).then_inc(sem["w_vec"], 16)
            sp.dma_start(m.ident[:, :], t.ident).then_inc(sem["w_proj"], 16)
            sp.dma_start(pe_sb[:, :, :], t.positions.rearrange("(i p) d -> p i d", p=P)).then_inc(sem["w_bc"], 16)

        @block.vector
        def _(dve):
            chain = Link(dve, sem["dve_chain"])
            dve.wait_ge(sem["w_vec"], 16)
            chain.step(dve.tensor_copy(idf[:, 0], ids[:, :]))
            chain.step(dve.tensor_scalar(idf[:, 1], idf[:, 0], 0.0, float(VOCAB), ALU.is_lt, ALU.mult))
            chain.step(dve.tensor_tensor(idf[:, 0], idf[:, 0], idf[:, 1], ALU.add))
            chain.step(dve.tensor_scalar(idf[:, 1], idf[:, 0], 0.0, float(VOCAB - 1), ALU.max, ALU.min))
            dve.tensor_copy(ids[:, :], idf[:, 1]).then_inc(sem["q_ready"], 1)
            dve.memset(m.v[:, :, :, DK:SLOT], 0.0).then_inc(sem["dve_chain"], 1)
            chain.n += 1
            chain.wait()
            dve.memset(m.v[:, :, :, DK:DK + 1], 1.0)
            dve.memset(m.packed[MROW:MROW + 3, 1, 2:, :, :], 1.0)
            dve.memset(m.mhalf[:, :], -0.5)
            dve.wait_ge(sem["w_proj"], 16)
            chain.step(dve.tensor_copy(m.identb[:, :], m.ident[:, :]))
            dve.wait_ge(sem["w_bc"], 16)
            for g in range(PAIRS):
                dve.wait_ge(gathered[g], 64)
                for b in range(2):
                    r = m.R[:, 4 * g + 2 * b:4 * g + 2 * b + 2, :]
                    ins = dve.tensor_tensor(r, r, pe_sb[:, :, :], ALU.add)
                ins.then_inc(sem["sum_ready"], 1)

        @block.gpsimd
        def _(pool):
            pool.wait_ge(sem["q_ready"], 1)
            for i in range(TILES):
                pool.indirect_dma_start(m.R[:, i, :], None, t.embed,
                                        bass.IndirectOffsetOnAxis(ap=ids[:, i:i + 1], axis=0)
                                        ).then_inc(gathered[i // 4], 16)

        @block.tensor
        def _(pe):
            pe.wait_ge(sem["w_proj"], 16)
            for g in range(PAIRS):
                pe.wait_ge(sem["sum_ready"], g + 1)
                if g >= 2:
                    pe.wait_ge(sem["xT_ready"], g - 1)
                for i in range(4):
                    ins = pe.transpose(m.lin[g % 2][:, i * P:(i + 1) * P], m.R[:, 4 * g + i, :], m.ident[:, :])
                ins.then_inc(sem["lin_ready"][0], 1)

        @block.scalar
        def _(act):
            act.wait_ge(sem["w_proj"], 16)
            act.activation(m.packed[MROW:MROW + 3, 1, 0:2, :, :].rearrange("p a h n -> p (a h n)"),
                           m.ident[MROW:MROW + 3, 0:1].broadcast_to([3, 2 * H * PW]), ACT.Copy, scale=0.0, bias=1.0)
            for g in range(PAIRS):
                act.wait_ge(sem["lin_ready"][0], g + 1)
                act.activation(m.xT[:, g * PW:(g + 1) * PW], m.lin[g % 2], ACT.Copy).then_inc(sem["xT_ready"], 1)

    settle()
    w = Names()
    w.q, w.k, w.v, w.o = [(lambda b, i=i: wproj[:, i, :]) for i in range(4)]
    w.w1, w.w2 = wff1[:, :], wff2[:, :, :]
    w.bq, w.bk, w.g1, w.be1, w.g2, w.be2 = [vec[:, i:i + 1] for i in range(6)]
    w.b1 = vec[:, 6:10]
    w.bv_bc, w.bo_bc, w.b2_bc, w.g1_bc, w.be1_bc, w.g2_bc, w.be2_bc = [bc[:, i, :] for i in range(7)]

    def loads_of(layer):
        def load_projections(sp):
            sp.dma_start(wproj[:, 0:3, :], t.tok_proj[layer].rearrange("a p c n -> (a p) c n")[:, 0:3, :]
                         ).then_inc(sem["w_proj"], 16)
            sp.dma_start(vec[:, 0:2], t.tok_cols[layer].rearrange("a p n -> (a p) n")[:, 0:2]).then_inc(sem["w_vec"], 16)
            sp.dma_start(bc[:, 0:2, :], t.tok_rows[layer][:, 0:2, :].broadcast_to([P, 2, D])).then_inc(sem["w_bc"], 16)

        def load_products(sp):
            sp.dma_start(wproj[:, 3, :], t.tok_proj[layer].rearrange("a p c n -> (a p) c n")[:, 3, :]
                         ).then_inc(sem["w_rest"], 16)
            sp.dma_start(wff1[:, :], t.all["L0_tok_W1"][layer].rearrange("a p n -> (a p) n")).then_inc(sem["w_rest"], 16)
            sp.dma_start(wff2[:, :, :], t.all["L0_tok_W2"][layer].rearrange("a (c p) n -> p (a c) n", p=P)
                         ).then_inc(sem["w_rest"], 16)

        def load_vectors(sp):
            sp.dma_start(vec[:, 2:10], t.tok_cols[layer].rearrange("a p n -> (a p) n")[:, 2:10]).then_inc(sem["w_rows"], 16)
            sp.dma_start(bc[:, 2:7, :], t.tok_rows[layer][:, 2:7, :].broadcast_to([P, 5, D])).then_inc(sem["w_rows"], 16)

        return load_projections, load_products, load_vectors

    first_loads = loads_of(slice(0, 1))

    def load_all(sp):
        for load in first_loads:
            load(sp)

    every_load = (("w_proj", 1), ("w_vec", 1), ("w_bc", 1), ("w_rest", 3), ("w_rows", 2))
    w.load_first, w.loading, w.first_pair, w.first_sum = load_all, every_load, 0, 0
    emit_stages(nc, m, w, sem, True, layer_start(True, TURN_AT))
    settle()
    with nc.Fori(0, LAYERS - 1) as layer:
        w.load_first, w.load_products, w.load_vectors = loads_of(bass.ds(layer + 1, 1))
        w.first_pair, w.first_sum = PAIRS, PAIRS
        emit_stages(nc, m, w, sem, True, layer_turn())
        settle()
    w.load_first, w.loading, w.first_pair, w.first_sum = lambda sp: None, (), None, None
    emit_stages(nc, m, w, sem, True, layer_end())
    settle()


_TOK_COLS = ("bq", "bk", "g1", "be1", "g2", "be2")
_TOK_ROWS = ("bv", "bo", "b2", "g1", "be1", "g2", "be2")


def shape_constants():
    import numpy as np
    import math
    pos = np.arange(S, dtype=np.float32)[:, None]
    div = np.exp(np.arange(0, D, 2, dtype=np.float32) * np.float32(-math.log(10000.0) / D)).astype(np.float32)
    ang = (pos * div).astype(np.float32)
    pe = np.zeros((S, D), np.float32)
    pe[:, 0::2], pe[:, 1::2] = np.sin(ang), np.cos(ang)
    return {"positions": pe, "ident": np.eye(P, dtype=np.float32)}


def kernel(**inputs):
    import numpy as _np
    import concourse.bacc as _bacc
    from concourse.bass_utils import run_bass_kernel_spmd as _run

    nc = _bacc.Bacc("TRN2", target_bir_lowering=False, num_devices=1)
    arrays = {k: _np.array(v) for k, v in inputs.items() if k != "x"}
    arrays["ids"] = _np.ascontiguousarray(_np.asarray(inputs["x"]).reshape(TILES, P).T)
    tok = {k[7:]: v for k, v in arrays.items() if k.startswith("L0_tok_")}
    arrays["tok_proj"] = _np.stack([tok[n] for n in ("Wq", "Wk", "Wv", "Wo")], axis=2)
    arrays["tok_cols"] = _np.concatenate([_np.stack([tok[n] for n in _TOK_COLS], axis=2),
                                          tok["b1"].reshape(LAYERS, 4, P).transpose(0, 2, 1)], axis=2)
    arrays["tok_rows"] = _np.stack([tok[n] for n in _TOK_ROWS], axis=1)
    arrays["attn_rows"] = _np.stack([tok["gf"], tok["bf"], arrays["L0_attn_b_out"]])[None]
    arrays["attn_cols"] = _np.stack([arrays["L0_attn_norm_gamma"], arrays["L0_attn_norm_beta"]], axis=1)
    taps = _np.zeros(4 * P, _np.float32)
    taps[2 * P - KSIZE // 2:2 * P + KSIZE // 2 + 1] = arrays["L0_attn_w_conv"].reshape(KSIZE)[::-1]
    arrays["taps"] = _np.stack([_np.stack([taps[(2 - kt) * P - p:(2 - kt) * P - p + S] for kt in range(2)])
                                for p in range(P)])
    arrays["router_rows"] = _np.stack([arrays["L0_ffn_router_b"], _np.arange(EXPERTS, 0, -1, dtype=_np.float32)])[None]
    arrays["ffn_b1"] = arrays["L0_ffn_b1"].reshape(EXPERTS, 4, P).transpose(0, 2, 1)
    arrays["ffn_rows"] = _np.stack([arrays["L0_ffn_ln_g"], arrays["L0_ffn_ln_b"]])[None]
    arrays.update(shape_constants())
    arrays.update(moe_constants())
    arrays["l1_qk"] = _np.stack([arrays["L1_attn_Wq"], arrays["L1_attn_Wk"]], axis=2)
    arrays["l1_cols"] = _np.stack([arrays["L1_attn_b" + n] for n in "qkv"], axis=2)
    arrays["l1_vT"] = arrays["L1_attn_Wv"].transpose(0, 2, 1)
    arrays["l1_o"] = arrays["L1_attn_Wo"].reshape(WH, D, D)
    arrays["route_rows"] = _np.stack([arrays["L1_ffn_r_b2"], _np.arange(OPTIONS, 0, -1, dtype=_np.float32)])[None]
    wide = lambda a: a.reshape(D, -1, 1, DK).repeat(D // a.shape[1], axis=2).reshape(D, D)
    arrays["gqa_w"] = _np.stack([_np.concatenate([arrays[f"L1_ffn_wq{i}"], wide(arrays[f"L1_ffn_wk{i}"]),
                                                  wide(arrays[f"L1_ffn_wv{i}"]), arrays[f"L1_ffn_wo{i}"]], axis=1)
                                 for i in range(OPTIONS)], axis=1)
    arrays = {k: _np.ascontiguousarray(v) for k, v in arrays.items()}
    aps = {k: nc.dram_tensor("in_" + k, v.shape, mybir.dt.from_np(v.dtype), kind="ExternalInput").ap()
           for k, v in arrays.items()}
    t = Names()
    t.ids, t.ident, t.positions, t.embed = aps["ids"], aps["ident"], aps["positions"], aps["L0_tok_embed"]
    t.tok_proj, t.tok_cols, t.tok_rows = aps["tok_proj"], aps["tok_cols"], aps["tok_rows"]
    t.attn_rows, t.attn_cols, t.taps, t.all = aps["attn_rows"], aps["attn_cols"], aps["taps"], aps
    out = nc.dram_tensor("out", (B, S, D), F32, kind="ExternalOutput").ap()
    build(nc, t, out)
    r = _run(nc, [{"in_" + k: v for k, v in arrays.items()}], core_ids=[0])
    return r.results[0]["out"]
```
